# Optimizing a Trainium2 kernel written in Bass

```python
import numpy as np
import jax
import jax.numpy as jnp

def _softmax(x, axis=-1):
    return jax.nn.softmax(x, axis=axis)

def _gelu(x):
    return jax.nn.gelu(x, approximate=True)

def _silu(x):
    return jax.nn.silu(x)

def _sigmoid(x):
    return jax.nn.sigmoid(x)

def _layernorm(x, axis=-1, eps=1e-05):
    m = jnp.mean(x, axis=axis, keepdims=True)
    v = jnp.var(x, axis=axis, keepdims=True)
    return (x - m) / jnp.sqrt(v + eps)

def _scatter_add(tgt, idx, src, axis=0):
    return tgt.at[idx].add(src)

def _segment_sum(src, seg, n):
    return jax.ops.segment_sum(src, seg, n)
kernel_name = 'mk_decoder_preln_d1_seqx_r4_12dfd0'

def setup_inputs(seed: int=0):
    np.random.seed(seed)
    _w = jnp.asarray

    def _rec_inputs():
        import jax
        import jax.numpy as jnp
        _rk = jax.random.key(seed)
        x = 7.22e-05 + 1 * jax.random.normal(jax.random.fold_in(_rk, 1), (8, 256, 256), jnp.float32)
        _lenS = 256 - jax.random.randint(jax.random.fold_in(_rk, 7), (8,), 0, max(1, 256 // 4) + 1, jnp.int32)
        _lenS2 = 256 - jax.random.randint(jax.random.fold_in(_rk, 8), (8,), 0, max(1, 256 // 4) + 1, jnp.int32)
        _ctx_1024P = jax.random.normal(jax.random.fold_in(_rk, 11), (8, 16, 256), jnp.float32)
        _ctx_1024c = jax.random.dirichlet(jax.random.fold_in(_rk, 511), 0.3 * jnp.ones((16,), jnp.float32), (8, 256))
        _ctx_1024t = jnp.einsum('bsk,bkd->bsd', _ctx_1024c, _ctx_1024P)
        _ctx_1024t = _ctx_1024t * jax.lax.rsqrt(jnp.mean(jnp.square(_ctx_1024t)) + 1e-12) * 0.953939
        ctx_1024 = 4.13588e-05 + 0.999923 * (_ctx_1024t + 0.3 * jax.random.normal(jax.random.fold_in(_rk, 611), (8, 256, 256), jnp.float32))
        _validS = jnp.arange(256)[None, :] < _lenS[:, None]
        _validS2 = jnp.arange(256)[None, :] < _lenS2[:, None]
        _causal = jnp.tril(jnp.ones((256, 256), dtype=bool))
        mask_BxSxS2_bk1 = jnp.broadcast_to(_validS2[:, None, :], (8, 256, 256))
        return (x, ctx_1024, mask_BxSxS2_bk1)
    x, ctx_1024, mask_BxSxS2_bk1 = _rec_inputs()

    def _L0_attn_setup():
        import jax, jax.numpy as jnp
        import numpy as np
        D_MODEL = 256
        NUM_HEADS = 16
        D_HEAD = 64
        N_CTX = 512
        BATCH = 4
        NEG_INF = -10000000000.0
        key = jax.random.key(seed)
        k1, k2, k3, k4, k5 = jax.random.split(key, 5)
        s = 1.0 / np.sqrt(D_MODEL).astype(np.float32)
        x = jax.random.normal(k1, (BATCH, N_CTX, D_MODEL), dtype=jnp.float32)
        W_K = jax.random.normal(k2, (NUM_HEADS, D_HEAD, D_MODEL), dtype=jnp.float32) * s
        W_Q = jax.random.normal(k3, (NUM_HEADS, D_HEAD, D_MODEL), dtype=jnp.float32) * s
        W_V = jax.random.normal(k4, (NUM_HEADS, D_HEAD, D_MODEL), dtype=jnp.float32) * s
        W_O = jax.random.normal(k5, (D_MODEL, NUM_HEADS * D_HEAD), dtype=jnp.float32) * s
        return {'x': x, 'W_K': W_K, 'W_Q': W_Q, 'W_V': W_V, 'W_O': W_O}
    _L0_attn_all = _L0_attn_setup()
    _L0_attn_in = {k: v for k, v in _L0_attn_all.items() if k in ('W_K', 'W_Q', 'W_V', 'W_O')}
    del _L0_attn_all

    def _L0_xattn_setup():
        import jax, jax.numpy as jnp
        import numpy as np
        HEADS = 16
        D_MODEL = 256
        D_HEAD = D_MODEL // HEADS

        def _split_head(x):
            B, S, _ = x.shape
            return x.reshape(B, S, HEADS, D_HEAD).transpose(0, 2, 1, 3)
        key = jax.random.key(seed)
        ks = jax.random.split(key, 12)
        B, S = (4, 512)
        scale = D_MODEL ** (-0.5)
        inp = {'q': jax.random.normal(ks[0], (B, S, D_MODEL), jnp.float32), 'k': jax.random.normal(ks[1], (B, S, D_MODEL), jnp.float32), 'v': jax.random.normal(ks[2], (B, S, D_MODEL), jnp.float32), 'mask': jnp.triu(jnp.ones((S, S), bool), k=1)[None].repeat(B, axis=0), 'wq': jax.random.normal(ks[3], (D_MODEL, D_MODEL), jnp.float32) * scale, 'bq': jnp.zeros((D_MODEL,), jnp.float32), 'wk': jax.random.normal(ks[4], (D_MODEL, D_MODEL), jnp.float32) * scale, 'bk': jnp.zeros((D_MODEL,), jnp.float32), 'wv': jax.random.normal(ks[5], (D_MODEL, D_MODEL), jnp.float32) * scale, 'bv': jnp.zeros((D_MODEL,), jnp.float32), 'wo': jax.random.normal(ks[6], (D_MODEL, D_MODEL), jnp.float32) * scale, 'bo': jnp.zeros((D_MODEL,), jnp.float32)}
        return inp
    _L0_xattn_all = _L0_xattn_setup()
    _L0_xattn_in = {k: v for k, v in _L0_xattn_all.items() if k in ('wq', 'bq', 'wk', 'bk', 'wv', 'bv', 'wo', 'bo')}
    del _L0_xattn_all

    def _L0_ffn_setup():
        import jax, jax.numpy as jnp
        import numpy as np
        DIM = 256
        HIDDEN = 1024
        N_EXPERTS = 8
        K = 2
        TEMP = 1.0

        def _expert_ffn(xf, wa, ba, wb, bb):
            h = xf @ wa.T + ba
            h1, h2 = jnp.split(h, 2, axis=-1)
            h = jax.nn.silu(h1) * h2
            return h @ wb.T + bb
        key = jax.random.key(seed)
        ks = jax.random.split(key, 7)
        s = 0.02
        x = jax.random.normal(ks[0], (4, 512, DIM), dtype=jnp.float32)
        router_w = jax.random.normal(ks[1], (N_EXPERTS, DIM), dtype=jnp.float32) * s
        router_b = jnp.zeros((N_EXPERTS,), dtype=jnp.float32)
        w1 = jax.random.normal(ks[2], (N_EXPERTS, 2 * HIDDEN, DIM), dtype=jnp.float32) * s
        b1 = jnp.zeros((N_EXPERTS, 2 * HIDDEN), dtype=jnp.float32)
        w2 = jax.random.normal(ks[3], (N_EXPERTS, DIM, HIDDEN), dtype=jnp.float32) * s
        b2 = jnp.zeros((N_EXPERTS, DIM), dtype=jnp.float32)
        return {'x': x, 'router_w': router_w, 'router_b': router_b, 'w1': w1, 'b1': b1, 'w2': w2, 'b2': b2}
    _L0_ffn_all = _L0_ffn_setup()
    _L0_ffn_in = {k: v for k, v in _L0_ffn_all.items() if k in ('router_w', 'router_b', 'w1', 'b1', 'w2', 'b2')}
    del _L0_ffn_all
    return {'x': x, 'ctx_1024': ctx_1024, 'mask_BxSxS2_bk1': mask_BxSxS2_bk1, 'L0_attn_W_K': _L0_attn_in['W_K'], 'L0_attn_W_Q': _L0_attn_in['W_Q'], 'L0_attn_W_V': _L0_attn_in['W_V'], 'L0_attn_W_O': _L0_attn_in['W_O'], 'L0_xattn_wq': _L0_xattn_in['wq'], 'L0_xattn_bq': _L0_xattn_in['bq'], 'L0_xattn_wk': _L0_xattn_in['wk'], 'L0_xattn_bk': _L0_xattn_in['bk'], 'L0_xattn_wv': _L0_xattn_in['wv'], 'L0_xattn_bv': _L0_xattn_in['bv'], 'L0_xattn_wo': _L0_xattn_in['wo'], 'L0_xattn_bo': _L0_xattn_in['bo'], 'L0_ffn_router_w': _L0_ffn_in['router_w'], 'L0_ffn_router_b': _L0_ffn_in['router_b'], 'L0_ffn_w1': _L0_ffn_in['w1'], 'L0_ffn_b1': _L0_ffn_in['b1'], 'L0_ffn_w2': _L0_ffn_in['w2'], 'L0_ffn_b2': _L0_ffn_in['b2']}

def reference(x, ctx_1024, mask_BxSxS2_bk1, L0_attn_W_K, L0_attn_W_Q, L0_attn_W_V, L0_attn_W_O, L0_xattn_wq, L0_xattn_bq, L0_xattn_wk, L0_xattn_bk, L0_xattn_wv, L0_xattn_bv, L0_xattn_wo, L0_xattn_bo, L0_ffn_router_w, L0_ffn_router_b, L0_ffn_w1, L0_ffn_b1, L0_ffn_w2, L0_ffn_b2):
    import jax
    import jax.numpy as jnp

    def _L0_attn_ref(x, W_K, W_Q, W_V, W_O):
        import jax, jax.numpy as jnp
        import numpy as np
        D_MODEL = 256
        NUM_HEADS = 16
        D_HEAD = 64
        N_CTX = 512
        BATCH = 4
        NEG_INF = -10000000000.0
        b, q_len, d_model = x.shape
        d_head = W_K.shape[1]
        K = jnp.einsum('bpd,ihd->biph', x, W_K)
        Q = jnp.einsum('bpd,ihd->biph', x, W_Q)
        V = jnp.einsum('bpd,ihd->biph', x, W_V)
        scores = jnp.einsum('biph,biqh->biqp', K, Q)
        mask = jnp.tril(jnp.ones((q_len, q_len), dtype=bool))
        scores = jnp.where(mask[None, None, :, :], scores, NEG_INF)
        attn = jax.nn.softmax(scores / np.sqrt(d_head).astype(np.float32), axis=-1)
        z = jnp.einsum('biph,biqp->biqh', V, attn)
        z_flat = jnp.transpose(z, (0, 2, 1, 3)).reshape(b, q_len, -1)
        out = jnp.einsum('bqf,df->bqd', z_flat, W_O)
        return out

    def _L0_xattn_ref(q, k, v, mask, wq, bq, wk, bk, wv, bv, wo, bo):
        import jax, jax.numpy as jnp
        import numpy as np
        HEADS = 16
        D_MODEL = 256
        D_HEAD = D_MODEL // HEADS

        def _split_head(x):
            B, S, _ = x.shape
            return x.reshape(B, S, HEADS, D_HEAD).transpose(0, 2, 1, 3)
        qh = _split_head(q @ wq.T + bq) * D_HEAD ** (-0.5)
        kh = _split_head(k @ wk.T + bk)
        vh = _split_head(v @ wv.T + bv)
        scores = jnp.einsum('bhqd,bhkd->bhqk', qh, kh)
        scores = jnp.where(mask[:, None, :, :], -1e+20, scores)
        weights = jax.nn.softmax(scores, axis=-1)
        ctx = jnp.einsum('bhqk,bhkd->bhqd', weights, vh)
        B, H, S, D = ctx.shape
        ctx = ctx.transpose(0, 2, 1, 3).reshape(B, S, H * D)
        return ctx @ wo.T + bo

    def _L0_ffn_ref(x, router_w, router_b, w1, b1, w2, b2):
        import jax, jax.numpy as jnp
        import numpy as np
        DIM = 256
        HIDDEN = 1024
        N_EXPERTS = 8
        K = 2
        TEMP = 1.0

        def _expert_ffn(xf, wa, ba, wb, bb):
            h = xf @ wa.T + ba
            h1, h2 = jnp.split(h, 2, axis=-1)
            h = jax.nn.silu(h1) * h2
            return h @ wb.T + bb
        b, t, d = x.shape
        logits = (x @ router_w.T + router_b) / TEMP
        topk_val, topk_idx = jax.lax.top_k(logits, K)
        weights = jax.nn.softmax(topk_val, axis=-1)
        xf = x.reshape(-1, d)
        outs = jax.vmap(_expert_ffn, in_axes=(None, 0, 0, 0, 0))(xf, w1, b1, w2, b2)
        outs = jnp.transpose(outs, (1, 0, 2))
        idx = topk_idx.reshape(-1, K)
        gathered = jnp.take_along_axis(outs, idx[:, :, None], axis=1)
        combined = (gathered * weights.reshape(-1, K, 1)).sum(axis=1)
        return combined.reshape(b, t, d)
    x = x + _L0_attn_ref(_layernorm(x, axis=-1), L0_attn_W_K, L0_attn_W_Q, L0_attn_W_V, L0_attn_W_O)
    x = x + _L0_xattn_ref(_layernorm(x, axis=-1), ctx_1024, ctx_1024, mask_BxSxS2_bk1, L0_xattn_wq, L0_xattn_bq, L0_xattn_wk, L0_xattn_bk, L0_xattn_wv, L0_xattn_bv, L0_xattn_wo, L0_xattn_bo)
    x = x + _L0_ffn_ref(_layernorm(x, axis=-1), L0_ffn_router_w, L0_ffn_router_b, L0_ffn_w1, L0_ffn_b1, L0_ffn_w2, L0_ffn_b2)
    return x

_drawn_inputs = setup_inputs


def setup_inputs(seed=0):
    import zlib

    import numpy as np

    out = dict(_drawn_inputs(seed))
    spreads = {'L0_xattn_bq': (0.0, 0.322),
     'L0_xattn_bk': (0.0, 0.8),
     'L0_xattn_bv': (0.0, 0.1),
     'L0_xattn_bo': (0.0, 0.1),
     'L0_ffn_router_b': (0.0, 0.323),
     'L0_ffn_b1': (0.0, 0.8),
     'L0_ffn_b2': (0.0, 0.1)}
    factors = {'L0_ffn_w1': 2.723, 'L0_ffn_w2': 2.711}
    for name, (base, spread) in spreads.items():
        noise = np.random.default_rng([zlib.crc32(name.encode()), seed]).standard_normal(out[name].shape)
        drawn = base * np.exp(spread * noise) if base else spread * noise
        out[name] = jnp.asarray(drawn.astype(out[name].dtype))
    for name, factor in factors.items():
        out[name] = (out[name] * factor).astype(out[name].dtype)
    return out
```

```python
from contextlib import ExitStack

import concourse.bass as bass
from concourse import mybir

F32 = mybir.dt.float32
BF16 = mybir.dt.bfloat16
I32 = mybir.dt.int32
U8 = mybir.dt.uint8
ALU = mybir.AluOpType
ACT = mybir.ActivationFunctionType
AX_X = mybir.AxisListType.X

P = 128
B, S, D = 8, 256, 256
T = S // P
KT = D // P
H, DH = 16, 64
PAIRS = H // 2
CDH = D // H
HPC = P // CDH
GROUP = 4
E, HID = 8, 1024
TOK = B * S
EPS = 1e-5
BIG = 1e30
XBIG = 1e20
REGION = TOK + P
NTILE = 2 * TOK // P + E - 1
NTAB = NTILE + 1
PAIRED = (NTILE - 3) // 2
L1_ORDER = (0, 2, 1, 3)
ROW = D + E + 1
U = 2 * H
S_RING, P_RING = 4, 4
LAG_T, LAG_V = 3, 4


class Signal:

    def __init__(self, sem, per, off=0):
        self.sem, self.per, self.off = sem, per, off

    def wait(self, eng, b, n):
        eng.wait_ge(self.sem, b * self.per + (n + self.off))

    def wait_alone(self, eng, b, n, passed):
        self.wait(eng, b, n)
        eng.sem_inc(passed.sem, 1)


def build(nc, x, ctx_t, mask, wq, wk, wv, wo, cwq, cwk, cwv, cwo, cbq, cbk, cbv, cbo,
          rw, rb, w1, b1, w2, b2, out):
    stack = ExitStack()
    with stack:
        def sb(name, shape, dt=F32):
            return stack.enter_context(nc.sbuf_tensor(name, shape, dt))

        def sig(name, per, off=0):
            return Signal(stack.enter_context(nc.semaphore(name)), per, off)

        bank = [stack.enter_context(nc.psum_tensor(f"bank{i}", [P, 512], F32)) for i in range(8)]
        dispatched = nc.dram_tensor("dispatched", [E * REGION + P, ROW], F32).ap()

        w_qkv = sb("w_qkv", [P, 3, KT, H * DH])
        wo_sb = sb("wo_sb", [P, PAIRS, D])
        cw = sb("cw", [P, 4, KT, D])
        cbq_sb = sb("cbq_sb", [P, KT])
        cbk_sb = sb("cbk_sb", [P, KT])
        cbv_sb = sb("cbv_sb", [P, D])
        cbo_sb = sb("cbo_sb", [P, D])
        rw_sb = sb("rw_sb", [P, KT, E])
        rb_sb = sb("rb_sb", [P, E])
        ident = sb("ident", [P, P])
        causal = sb("causal", [P, 3 * P])
        before = sb("before", [P, P], BF16)
        ones = sb("ones", [P, P], BF16)
        neg_half = sb("neg_half", [P, T])
        rev = sb("rev", [P, T, E])
        region0 = sb("region0", [P, T, E])
        token = sb("token", [P, T], I32)
        pad_rows = sb("pad_rows", [P, ROW])

        x_in = sb("x_in", [P, T, D])
        ctxT_in = sb("ctxT_in", [P, KT, S])
        mask_in = sb("mask_in", [P, T, S], U8)
        cmask = sb("cmask", [P, T, S])
        xn = sb("xn", [P, T, D])
        xnT = sb("xnT", [P, KT, S])
        q_pad = sb("q_pad", [P, PAIRS, 2, S])
        k_T = sb("k_T", [P, PAIRS, S])
        v_sb = sb("v_sb", [P, T, H * DH])
        prob = sb("prob", [P, P_RING, 512])
        prob_T = sb("prob_T", [P, 2, 512])
        z_T = sb("z_T", [P, PAIRS, S])
        x1 = sb("x1", [P, T, D])
        x1b = sb("x1b", [P, T, D])
        cq_T = sb("cq_T", [P, KT, S])
        cq_pad = sb("cq_pad", [P, KT, HPC, S])
        ck_T = sb("ck_T", [P, KT, S])
        cv_sb = sb("cv_sb", [P, T, H, 32])
        o_T = sb("o_T", [P, H // GROUP, S])
        ctx_sb = sb("ctx_sb", [P, T, H, CDH])
        crec = sb("crec", [P, T, H])
        x2 = sb("x2", [P, T, D])
        rows = sb("rows", [P, T, ROW])
        st = sb("st", [P, T, 6])
        mv = sb("mv", [P, T, 2])
        ve = sb("ve", [P, T])
        rstd = sb("rstd", [P, T])
        nmax = sb("nmax", [P, P_RING, 2])
        psum_ = sb("psum_", [P, P_RING, 2])
        r3 = sb("r3", [P, P_RING, 3])
        lg = sb("lg", [P, T, E])
        lg2 = sb("lg2", [P, T, E])
        eq = sb("eq", [P, T, E])
        oh1 = sb("oh1", [P, T, E])
        oh2 = sb("oh2", [P, T, E])
        wa = sb("wa", [P, T, E])
        hot = sb("hot", [P, T, E], BF16)
        v1 = sb("v1", [P, T])
        v2 = sb("v2", [P, T])
        mi = sb("mi", [P, T])
        e2 = sb("e2", [P, T])
        pw1 = sb("pw1", [P, T])
        pw2 = sb("pw2", [P, T])
        run = sb("run", [P, E])
        rank = sb("rank", [P, T, E])
        slotf = sb("slotf", [P, 2, T])
        slot_i = sb("slot_i", [P, 2, T], I32)

        w1_ring = sb("w1_ring", [P, 2, KT * 2 * HID])
        w2_ring = sb("w2_ring", [P, 2, (HID // P) * D])
        b2_ring = sb("b2_ring", [P, 2, D])
        b1_ring = cq_pad[:].rearrange("p k h s -> p (k h s)").rearrange("p (r n) -> p r n", r=2)
        arena = w_qkv[:].rearrange("p a k n -> p (a k n)")
        hb = [arena[:, 2048 * i:2048 * (i + 1)] for i in range(2)]
        hsil = arena[:, 4096:5120]
        xe_T = [arena[:, 5120 + 256 * i:5376 + 256 * i] for i in range(2)]
        arena2 = q_pad[:].rearrange("p a k n -> p (a k n)")
        hid = [arena2[:, 1024 * i:1024 * (i + 1)] for i in range(2)]
        hid_T = arena2[:, 2048:3072]
        y1 = arena2[:, 3072:3328]
        y2 = [arena2[:, 3328 + 256 * i:3584 + 256 * i] for i in range(2)]
        xe = [sb(f"xe{i}", [P, ROW]) for i in range(2)]
        tails = sb("tails", [P, NTAB, E + 1])
        ids = sb("ids", [P, 1], I32)

        cnt_i = sb("cnt_i", [1, E], I32)
        til_i = sb("til_i", [1, E], I32)
        til_f = sb("til_f", [1, E])
        one8 = sb("one8", [1, E])
        cum_f = sb("cum_f", [1, E])
        cum_i = sb("cum_i", [1, E], I32)
        jj = sb("jj", [1, NTAB])
        ge = sb("ge", [1, NTAB, E])
        get_ = sb("get_", [1, NTAB, E])
        ef = sb("ef", [1, NTAB])
        fin_t = sb("fin_t", [1, NTAB])
        lt8 = sb("lt8", [1, NTAB])
        loc = sb("loc", [1, NTAB])
        e7 = sb("e7", [1, NTAB])
        rowf = sb("rowf", [1, NTAB])
        tile_e = sb("tile_e", [1, NTAB], I32)
        tile_slot = sb("tile_slot", [1, NTAB], I32)
        tile_row = sb("tile_row", [1, NTAB], I32)

        w_in = sig("w_in", 0)
        consts = sig("consts", 0)
        passed = sig("passed", 0)
        x_loaded = sig("x_loaded", 16)
        ctx_loaded = sig("ctx_loaded", 16)
        mask_loaded = sig("mask_loaded", 16)
        xn_ready = sig("xn_ready", 3)
        ve_ready = sig("ve_ready", 3)
        rstd_ready = sig("rstd_ready", 3)
        tr_ready = sig("tr_ready", 4)
        xnT_ready = sig("xnT_ready", 4)
        fill_done = sig("fill_done", 12)
        q_evac = sig("q_evac", 8)
        kv_evac = sig("kv_evac", 8)
        scores_ready = sig("scores_ready", U)
        masked_ready = sig("masked_ready", U, S_RING)
        exp_ready = sig("exp_ready", U)
        recip_ready = sig("recip_ready", H)
        norm_ready = sig("norm_ready", H)
        pt_ready = sig("pt_ready", U, P_RING)
        pt_evac_act = sig("pt_evac_act", U // 4, 4)
        pt_evac_dve = sig("pt_evac_dve", U - U // 4, 4)
        pv_done = sig("pv_done", U, 2)
        o_evac = sig("o_evac", PAIRS + H // GROUP, 2)
        attn_out = sig("attn_out", 1)
        x1_done = sig("x1_done", 1, 1)
        x1b_done = sig("x1b_done", 1)
        ckv_done = sig("ckv_done", 2, 2)
        ck_evac = sig("ck_evac", 2)
        cv_evac = sig("cv_evac", 2)
        cq_done = sig("cq_done", 1)
        cq_evac = sig("cq_evac", 2)
        cq_spread = sig("cq_spread", 16 * HPC)
        cmask_ready = sig("cmask_ready", 1, 1)
        ctx_tr = sig("ctx_tr", 2)
        ctx_ready = sig("ctx_ready", 1)
        cx_out = sig("cx_out", 1)
        x2_ready = sig("x2_ready", 1)
        x2_stored = sig("x2_stored", 16)
        x2_free = sig("x2_free", 1, 1)
        rows_free = sig("rows_free", 1, 1)
        logits = sig("logits", 1)
        d_ready = sig("d_ready", 1)
        e2_ready = sig("e2_ready", 1)
        hot_ready = sig("hot_ready", 1)
        rank_ready = sig("rank_ready", 1)
        rank_used = sig("rank_used", 1, 1)
        slots_ready = sig("slots_ready", 1)
        rows_ready = sig("rows_ready", 1)
        scattered = sig("scattered", 64)
        dve_chain = stack.enter_context(nc.semaphore("dve_chain"))
        tables = sig("tables", 0)
        dve_tail = stack.enter_context(nc.semaphore("dve_tail"))
        pads_done = sig("pads_done", 0)
        w_loaded = sig("w_loaded", 48)
        b1_loaded = sig("b1_loaded", 16)
        tile_done = sig("tile_done", 1, 1)
        xe_loaded = [sig(f"xe_loaded{i}", 16) for i in range(2)]
        tail_copied = sig("tail_copied", 1)
        xt_ready = sig("xt_ready", 1)
        xt_evac = sig("xt_evac", 1, 1)
        l1_ready = sig("l1_ready", 4, 8)
        hb_ready = sig("hb_ready", 4, 4)
        sil_ready = sig("sil_ready", 2)
        hid_ready = sig("hid_ready", 2, 4)
        ht_ready = sig("ht_ready", 2, 4)
        ht_evac = sig("ht_evac", 2, 2)
        y1_ready = sig("y1_ready", 1, 1)
        y2_ready = sig("y2_ready", 1, 1)
        ids_ready = sig("ids_ready", 1, 1)
        added = sig("added", 16)

        NW = 15

        def evacs(u):
            return (u + 1) // 4, u + 1 - (u + 1) // 4

        def wait_evac(eng, b, u):
            if u % 4 == 3:
                pt_evac_act.wait(eng, b, evacs(u)[0])
            else:
                pt_evac_dve.wait(eng, b, evacs(u)[1])

        def blocks(u):
            return 3 if u < H else 4

        block = stack.enter_context(nc.Block())

        @block.sync
        def _(sp):
            def load_x(b):
                x1_done.wait(sp, b, 0)
                sp.dma_start(x_in[:], x[b]).then_inc(x_loaded.sem, 16)

            sp.sem_inc(x2_free.sem, 1)
            load_x(0)
            for i, w in enumerate((wq, wk, wv)):
                sp.dma_start(w_qkv[:, i], w).then_inc(w_in.sem, 16)
            sp.dma_start(wo_sb[:], wo).then_inc(w_in.sem, 16)
            for i, w in enumerate((cwq, cwk, cwv, cwo)):
                sp.dma_start(cw[:, i], w).then_inc(w_in.sem, 16)
            sp.dma_start(cbq_sb[:], cbq).then_inc(w_in.sem, 16)
            sp.dma_start(cbk_sb[:], cbk).then_inc(w_in.sem, 16)
            sp.dma_start(cbv_sb[:], cbv.broadcast_to((P, D))).then_inc(w_in.sem, 16)
            sp.dma_start(cbo_sb[:], cbo.broadcast_to((P, D))).then_inc(w_in.sem, 16)
            sp.dma_start(rw_sb[:], rw).then_inc(w_in.sem, 16)
            sp.dma_start(rb_sb[:], rb.broadcast_to((P, E))).then_inc(w_in.sem, 16)
            sp.wait_ge(consts.sem, 12)
            sp.dma_start(out[TOK:TOK + P, :], pad_rows[:, 0:D]).then_inc(w_in.sem, 16)
            sp.dma_start(dispatched[E * REGION:E * REGION + P, :], pad_rows[:]).then_inc(pads_done.sem, 16)

            def load_w(e):
                slot = e % 2
                sp.dma_start(w1_ring[:, bass.ds(slot, 1), :], w1[bass.ds(e, 1)].rearrange("e p n -> p e n")).then_inc(w_loaded.sem, 16)
                sp.dma_start(w2_ring[:, bass.ds(slot, 1), :], w2[bass.ds(e, 1)].rearrange("e p n -> p e n")).then_inc(w_loaded.sem, 16)
                sp.dma_start(b2_ring[:, bass.ds(slot, 1), :],
                             b2[bass.ds(e, 1), :].rearrange("e n -> () e n").broadcast_to((P, 1, D))).then_inc(w_loaded.sem, 16)

            def load_b1(e):
                sp.dma_start(b1_ring[:, bass.ds(e % 2, 1), :],
                             b1[bass.ds(e, 1), :].rearrange("e n -> () e n").broadcast_to((P, 1, 2 * HID))).then_inc(b1_loaded.sem, 16)

            def came(e):
                w_loaded.wait_alone(sp, e, 48, passed)
                b1_loaded.wait_alone(sp, e, 16, passed)

            load_w(0)

            def batch(b, last=False):
                ckv_done.wait(sp, b, 0)
                sp.dma_start(ctxT_in[:], ctx_t[b]).then_inc(ctx_loaded.sem, 16)
                cmask_ready.wait(sp, b, 0)
                sp.dma_start(mask_in[:], mask[b]).then_inc(mask_loaded.sem, 16)
                if not last:
                    load_x(b + 1)
                cq_evac.wait(sp, b, 2)
                for h8 in range(HPC):
                    r = slice(h8 * CDH, (h8 + 1) * CDH)
                    sp.dma_start(cq_pad[r, :, h8, :], cq_T[r, :, :]).then_inc(cq_spread.sem, 16)
                x2_ready.wait(sp, b, 1)
                sp.dma_start(out[bass.ds(b * S, S), :].rearrange("(t p) d -> p t d", p=P), x2[:]).then_inc(x2_stored.sem, 16)
                x2_stored.wait(sp, b, 16)
                sp.sem_inc(x2_free.sem, 1)

            with sp.Fori(0, B - 1) as b:
                batch(b)
            batch(B - 1, last=True)

            load_b1(0)
            came(0)
            load_w(1)
            load_b1(1)
            sp.wait_ge(tables.sem, 1)
            with sp.Fori(0, E) as e:
                n = sp.value_load(cnt_i[0:1, bass.ds(e, 1)], min_val=0, max_val=TOK)
                sp.dma_start(dispatched[bass.ds(e * REGION + n, P), :], pad_rows[:]).then_inc(pads_done.sem, 16)
            sp.wait_ge(tables.sem, 2)
            with sp.Fori(2, E) as e:
                n = sp.value_load(cum_i[0:1, bass.ds(e - 2, 1)], min_val=0, max_val=NTILE)
                sp.wait_ge(y1_ready.sem, n + 1)
                came(e - 1)
                load_w(e)
                load_b1(e)
            came(E - 1)

        @block.gpsimd
        def _(pool):
            g = nc.gpsimd
            g.memset(ident[:], 0.0).then_inc(consts.sem, 1)
            g.memset(causal[:], 0.0).then_inc(consts.sem, 1)
            g.memset(before[:], 1.0).then_inc(consts.sem, 1)
            g.memset(ones[:], 1.0).then_inc(consts.sem, 1)
            g.memset(neg_half[:], -0.5).then_inc(consts.sem, 1)
            g.memset(pad_rows[:], 0.0).then_inc(consts.sem, 1)
            g.iota(token[:], [[P, T]], base=0, channel_multiplier=1).then_inc(consts.sem, 1)
            pool.wait_ge(consts.sem, 7)
            g.affine_select(out=ident[:], in_=ident[:], compare_op=ALU.not_equal, fill=1.0, base=0,
                            pattern=[[-1, P]], channel_multiplier=1).then_inc(consts.sem, 1)
            for c in (0, 2):
                g.affine_select(out=causal[:, c * P:(c + 1) * P], in_=causal[:, c * P:(c + 1) * P],
                                compare_op=ALU.is_ge, fill=BIG, base=0, pattern=[[-1, P]],
                                channel_multiplier=1).then_inc(consts.sem, 1)
            g.affine_select(out=before[:], in_=before[:], compare_op=ALU.is_gt, fill=0.0, base=0,
                            pattern=[[1, P]], channel_multiplier=-1).then_inc(consts.sem, 1)
            g.iota(pad_rows[:, D + E:D + E + 1].bitcast(I32), [[0, 1]], base=TOK, channel_multiplier=1).then_inc(consts.sem, 1)
            g.iota(rev[:], [[0, T], [-1, E]], base=E, channel_multiplier=0,
                   allow_small_or_imprecise_dtypes=True).then_inc(consts.sem, 1)
            g.iota(region0[:], [[0, T], [REGION, E]], base=0, channel_multiplier=0,
                   allow_small_or_imprecise_dtypes=True).then_inc(consts.sem, 1)
            g.memset(q_pad[:], 0.0).then_inc(consts.sem, 1)
            g.memset(cq_pad[:], 0.0).then_inc(consts.sem, 1)
            g.memset(cv_sb[:], 0.0).then_inc(consts.sem, 1)
            g.memset(run[:], 0.0).then_inc(consts.sem, 1)
            pool.wait_ge(consts.sem, 18)
            g.memset(cv_sb[:, :, :, CDH:CDH + 1], 1.0).then_inc(consts.sem, 1)
            g.iota(jj[:], [[1, NTAB]], base=0, channel_multiplier=0,
                   allow_small_or_imprecise_dtypes=True).then_inc(consts.sem, 1)
            g.memset(one8[:], 1.0).then_inc(consts.sem, 1)
            pool.sem_inc(rows_free.sem, 1)
            pool.sem_inc(cmask_ready.sem, 1)
            pool.wait_ge(w_in.sem, 16 * NW)

            def rsqrt(b, n):
                ve_ready.wait(pool, b, n)
                g.tensor_tensor(rstd[:], ve[:], neg_half[:], ALU.pow).then_inc(rstd_ready.sem, 1)

            with pool.Fori(0, B) as b:
                rsqrt(b, 1)
                mask_loaded.wait(pool, b, 16)
                masked_ready.wait_alone(pool, b, 0, passed)
                g.tensor_scalar(cmask[:], mask_in[:], XBIG, None, ALU.mult).then_inc(cmask_ready.sem, 1)
                for h in range(H):
                    k = h % P_RING
                    recip_ready.wait(pool, b, h + 1)
                    pr = prob[:, k, 0:3 * P].rearrange("p (c n) -> p c n", c=3)
                    rr = r3[:, k, :].rearrange("p (c o) -> p c o", o=1).broadcast_to((P, 3, P))
                    g.tensor_tensor(pr, pr, rr, ALU.mult).then_inc(norm_ready.sem, 1)
                x1_done.wait(pool, b, 1)
                rsqrt(b, 2)
                for t in range(T):
                    ins = g.tensor_tensor(x1b[:, t], x1[:, t], cbo_sb[:], ALU.add)
                ins.then_inc(x1b_done.sem, 1)
                rsqrt(b, 3)
                rows_ready.wait(pool, b, 1)
                slots_ready.wait_alone(pool, b, 1, passed)
                for k in range(2):
                    for t in range(T):
                        g.indirect_dma_start(dispatched[:, :], bass.IndirectOffsetOnAxis(ap=slot_i[:, k, t:t + 1], axis=0),
                                             rows[:, t, :], None).then_inc(scattered.sem, 16)
                scattered.wait(pool, b, 64)
                pool.sem_inc(rows_free.sem, 1)

            pool.wait_ge(x2_stored.sem, 16 * B)

            pool.sem_inc(ids_ready.sem, 1)

            def copy_tail(i, c):
                xe_loaded[c % 2].wait(pool, i, 16 * (c // 2 + 1))
                g.tensor_copy(tails[:, bass.ds(i * 2 + c, 1), :].rearrange("p o n -> p (o n)").bitcast(I32),
                              xe[c % 2][:, D:ROW].bitcast(I32)).then_inc(tail_copied.sem, 1)

            def add_out(j, p, first=False):
                if not first:
                    added.wait_alone(pool, j, 0, passed)
                tail_copied.wait(pool, j, 1)
                g.tensor_copy(ids[:], tails[:, bass.ds(j, 1), E:E + 1].rearrange("p o n -> p (o n)").bitcast(I32)).then_inc(ids_ready.sem, 1)
                y2_ready.wait_alone(pool, j, 1, passed)
                ids_ready.wait_alone(pool, j, 1, passed)
                g.indirect_dma_start(out[:, :], bass.IndirectOffsetOnAxis(ap=ids[:], axis=0),
                                     y2[p], None, compute_op=ALU.add).then_inc(added.sem, 16)

            copy_tail(0, 0)
            copy_tail(0, 1)
            copy_tail(0, 2)
            add_out(0, 0, first=True)
            with pool.Fori(0, PAIRED) as i:
                copy_tail(i, 3)
                add_out(i * 2 + 1, 1)
                copy_tail(i, 4)
                add_out(i * 2 + 2, 0)
            add_out(NTILE - 2, 1)
            add_out(NTILE - 1, 0)
            pool.wait_ge(added.sem, 16 * NTILE)

        @block.scalar
        def _(act):
            a = nc.scalar
            act.sem_inc(o_evac.sem, 2)
            act.sem_inc(pt_evac_act.sem, 4)
            act.wait_ge(w_in.sem, 16 * NW)
            act.wait_ge(consts.sem, 21)

            def evac_xnT(b, n, src):
                tr_ready.wait(act, b, n)
                a.copy(xnT[:].rearrange("p k s -> p (k s)"), src).then_inc(xnT_ready.sem, 1)

            def exps(b, u):
                k = u % P_RING
                masked_ready.wait(act, b, u + 1)
                w = P if u < H else S
                for t in range(T):
                    lo = t * w
                    hi = lo + w if u >= H else (t + 1) * (t + 2) // 2 * P
                    pr = prob[:, k, lo:hi]
                    if u < H:
                        ins = a.activation(pr, pr, ACT.Exp, bias=nmax[:, k, t:t + 1], scale=-1.0,
                                           accum_out=psum_[:, k, t:t + 1])
                    else:
                        ins = a.activation(pr, pr, ACT.Exp, bias=nmax[:, k, t:t + 1], scale=-1.0)
                ins.then_inc(exp_ready.sem, 1)

            def evac_pt(b, u):
                n = blocks(u) * P
                pt_ready.wait(act, b, u + 1)
                pv_done.wait(act, b, u - 1)
                a.copy(prob_T[:, u % 2, 0:n], bank[4 + u % 2][:, 0:n]).then_inc(pt_evac_act.sem, 1)

            def heads(b, u0):
                for s in range(u0, u0 + H + LAG_V + 1):
                    if s < u0 + H:
                        exps(b, s)
                    u = s - LAG_T
                    if u0 <= u < u0 + H and u % 4 == 3:
                        evac_pt(b, u)
                    u = s - LAG_V - 1
                    if u >= u0 and u0 < H and u % 2 == 1:
                        pv_done.wait(act, b, u + 1)
                        j = u // 2
                        a.copy(z_T[:, j], bank[6 + j % 2][:, 0:S]).then_inc(o_evac.sem, 1)
                    if u >= u0 and u0 >= H and u % GROUP == GROUP - 1:
                        pv_done.wait(act, b, u + 1)
                        j = PAIRS + (u - H) // GROUP
                        a.copy(o_T[:, j - PAIRS], bank[6 + j % 2][:, 0:S]).then_inc(o_evac.sem, 1)

            with act.Fori(0, B) as b:
                evac_xnT(b, 1, bank[6][:])
                for f in range(4):
                    fill_done.wait(act, b, 2 * f + 1)
                    src = bank[(2 * f) % 6][:].rearrange("p (c s) -> p c s", c=2)
                    for par in range(2):
                        r = slice(64 * par, 64 * par + 64)
                        a.mul(q_pad[r, 2 * f:2 * f + 2, par, :], src[r], -float(DH) ** -0.5).then_inc(q_evac.sem, 1)
                heads(b, 0)
                for m in range(KT):
                    ckv_done.wait(act, b, 1)
                    a.activation(ck_T[:, m], bank[1][:, m * S:(m + 1) * S], ACT.Identity,
                                 bias=cbk_sb[:, m:m + 1]).then_inc(ck_evac.sem, 1)
                evac_xnT(b, 2, bank[6][:])
                heads(b, H)
                evac_xnT(b, 3, bank[7][:])
                evac_xnT(b, 4, bank[7][:])
                d_ready.wait(act, b, 1)
                a.activation(e2[:], v2[:], ACT.Exp).then_inc(e2_ready.sem, 1)

            act.wait_ge(tables.sem, 2)
            act.wait_ge(pads_done.sem, 16 * (E + 1))
            act.wait_ge(scattered.sem, 64 * B)

            act.sem_inc(xt_evac.sem, 1)
            act.sem_inc(ht_evac.sem, 2)
            act.sem_inc(y2_ready.sem, 1)

            def load_tile(i, c):
                j, p = i * 2 + c, c % 2
                r = act.value_load(tile_row[0:1, bass.ds(j, 1)], min_val=0, max_val=E * REGION)
                act.dma_start(xe[p][:], dispatched[bass.ds(r, P), :]).then_inc(xe_loaded[p].sem, 16)

            def front(j, p):
                xt_ready.wait(act, j, 1)
                l1_ready.wait(act, j, -4)
                a.copy(xe_T[p], bank[6][:, 0:KT * P]).then_inc(xt_evac.sem, 1)

            def silu(j, p, half):
                hb_ready.wait(act, j, 2 * half + 1)
                hid_ready.wait(act, j, -2 + half + 1)
                cols = slice(half * 512, (half + 1) * 512)
                a.activation(hsil[:, cols], hb[p][:, cols], ACT.Silu).then_inc(sil_ready.sem, 1)

            def back(j):
                tile_done.wait(act, j, 0)
                for c in range(2):
                    ht_ready.wait(act, j, c + 1)
                    a.copy(hid_T[:, c * 512:(c + 1) * 512], bank[4 + c][:]).then_inc(ht_evac.sem, 1)

            def scale_y(j, p):
                e = act.value_load(tile_e[0:1, bass.ds(j, 1)], min_val=0, max_val=E - 1)
                y1_ready.wait(act, j, 1)
                tail_copied.wait(act, j, 1)
                ids_ready.wait(act, j, 0)
                w = tails[:].rearrange("p j e -> p (j e)")[:, bass.ds(j * (E + 1) + e, 1)]
                a.mul(y2[p], y1, w).then_inc(y2_ready.sem, 1)

            def step(i, c, next_=True, load=True):
                j, p = i * 2 + c, c % 2
                back(j - 1)
                silu(j, p, 0)
                if next_:
                    front(j + 1, 1 - p)
                silu(j, p, 1)
                if load:
                    tail_copied.wait(act, j, 2)
                    load_tile(i, c + 3)
                scale_y(j - 1, 1 - p)

            load_tile(0, 0)
            load_tile(0, 1)
            front(0, 0)
            tail_copied.wait(act, 0, 1)
            load_tile(0, 2)
            silu(0, 0, 0)
            front(1, 1)
            silu(0, 0, 1)
            tail_copied.wait(act, 0, 2)
            load_tile(0, 3)
            with act.Fori(0, PAIRED) as i:
                step(i, 1)
                step(i, 2)
            step(PAIRED, 1, load=False)
            step(PAIRED, 2, next_=False, load=False)
            back(NTILE - 1)
            scale_y(NTILE - 1, 0)
            xe_loaded[1].wait(act, NTILE // 2, 16)

        @block.vector
        def _(dve):
            v = nc.vector
            dve.sem_inc(masked_ready.sem, S_RING)
            dve.sem_inc(pt_evac_dve.sem, 4)
            dve.sem_inc(x1_done.sem, 1)
            dve.sem_inc(rank_used.sem, 1)
            dve.wait_ge(w_in.sem, 16 * NW)
            dve.wait_ge(consts.sem, 21)

            class Chain:
                per = 0
                n = 0

            def link(b, ins):
                Chain.n += 1
                ins.then_inc(dve_chain, 1)
                dve.wait_ge(dve_chain, b * CHAIN + Chain.n)

            def norm(b, n, src, dst):
                for t in range(T):
                    ins = v.bn_stats(st[:, t], src[:, t])
                link(b, ins)
                dve.sem_inc(passed.sem, 1)
                for t in range(T):
                    ins = v.bn_aggr(mv[:, t], st[:, t])
                link(b, ins)
                v.tensor_scalar(ve[:], mv[:, :, 1], EPS, None, ALU.add).then_inc(ve_ready.sem, 1)
                rstd_ready.wait(dve, b, n)
                for t in range(T):
                    ins = v.tensor_scalar(dst[:, t, 0:D], src[:, t], mv[:, t, 0:1], rstd[:, t:t + 1],
                                          ALU.subtract, ALU.mult)
                ins.then_inc(xn_ready.sem, 1)

            def mask_max(b, u):
                k = u % P_RING
                pt_ready.wait(dve, b, u - P_RING + 1)
                scores_ready.wait_alone(dve, b, u + 1, passed)
                for t in range(T):
                    if u < H:
                        cols, m = (slice(0, P), slice(P, 3 * P))[t], causal
                        ma = m[:, cols]
                    else:
                        cols = slice(t * S, (t + 1) * S)
                        ma = cmask[:, t]
                    ins = v.tensor_tensor_reduce(prob[:, k, cols], bank[u % S_RING][:, cols], ma, 1.0, 3e38,
                                                 ALU.add, ALU.min, nmax[:, k, t:t + 1])
                ins.then_inc(masked_ready.sem, 1)

            def heads(b, u0):
                for s in range(u0, u0 + H + LAG_T):
                    if s < u0 + H:
                        mask_max(b, s)
                    h = s - 1
                    if u0 == 0 and 0 <= h < H:
                        k = h % P_RING
                        exp_ready.wait(dve, b, h + 1)
                        v.reciprocal(r3[:, k, 0:1], psum_[:, k, 0:1])
                        v.reciprocal(r3[:, k, 1:3], psum_[:, k, 1:2].broadcast_to((P, 2))).then_inc(recip_ready.sem, 1)
                    u = s - LAG_T
                    if u0 <= u < u0 + H and u % 4 != 3:
                        n = blocks(u) * P
                        pt_ready.wait(dve, b, u + 1)
                        pv_done.wait(dve, b, u - 1)
                        v.tensor_copy(prob_T[:, u % 2, 0:n], bank[4 + u % 2][:, 0:n]).then_inc(pt_evac_dve.sem, 1)

            CHAIN = 29

            with dve.Fori(0, B) as b:
                Chain.n = 0
                x_loaded.wait(dve, b, 16)
                norm(b, 1, x_in, xn)
                for f in range(4):
                    fill_done.wait(dve, b, 2 * f + 2)
                    v.tensor_copy(k_T[:, 2 * f:2 * f + 2].rearrange("p c s -> p (c s)"),
                                  bank[(2 * f + 1) % 6][:]).then_inc(kv_evac.sem, 1)
                for f in range(4):
                    t, half = divmod(f, 2)
                    fill_done.wait(dve, b, 8 + f + 1)
                    v.tensor_copy(v_sb[:, t, half * 512:(half + 1) * 512], bank[(8 + f) % 6][:]).then_inc(kv_evac.sem, 1)
                heads(b, 0)
                attn_out.wait(dve, b, 1)
                v.tensor_tensor(x1[:].rearrange("p t d -> p (t d)"), bank[7][:],
                                x_in[:].rearrange("p t d -> p (t d)"), ALU.add).then_inc(x1_done.sem, 1)
                x1_done.wait(dve, b, 1)
                norm(b, 2, x1, xn)
                ckv_done.wait(dve, b, 2)
                for t in range(T):
                    v.tensor_tensor(cv_sb[:, t, :, 0:CDH],
                                    bank[2][:, t * D:(t + 1) * D].rearrange("p (h c) -> p h c", c=CDH),
                                    cbv_sb[:].rearrange("p (h c) -> p h c", c=CDH), ALU.add).then_inc(cv_evac.sem, 1)
                cq_done.wait(dve, b, 1)
                for m in range(KT):
                    v.tensor_scalar(cq_T[:, m], bank[0][:, m * S:(m + 1) * S], cbq_sb[:, m:m + 1],
                                    -float(CDH) ** -0.5, ALU.add, ALU.mult).then_inc(cq_evac.sem, 1)
                cmask_ready.wait(dve, b, 1)
                heads(b, H)
                for t in range(T):
                    ctx_tr.wait(dve, b, t + 1)
                    o = bank[4 + t][:].rearrange("p (h c) -> p h c", c=32)
                    link(b, v.reciprocal(crec[:, t], o[:, :, CDH]))
                for t in range(T):
                    o = bank[4 + t][:].rearrange("p (h c) -> p h c", c=32)
                    rc = crec[:, t].rearrange("p (h c) -> p h c", c=1).broadcast_to((P, H, CDH))
                    ins = v.tensor_tensor(ctx_sb[:, t], o[:, :, 0:CDH], rc, ALU.mult)
                ins.then_inc(ctx_ready.sem, 1)
                cx_out.wait(dve, b, 1)
                x1b_done.wait(dve, b, 1)
                x2_free.wait(dve, b, 0)
                rows_free.wait(dve, b, 0)
                v.tensor_tensor(x2[:].rearrange("p t d -> p (t d)"), bank[6][:],
                                x1b[:].rearrange("p t d -> p (t d)"), ALU.add).then_inc(x2_ready.sem, 1)
                x2_ready.wait(dve, b, 1)
                norm(b, 3, x2, rows)

                logits.wait(dve, b, 1)
                rbb = rb_sb[:].rearrange("p (t e) -> p t e", t=1).broadcast_to((P, T, E))
                link(b, v.tensor_tensor(lg[:], bank[0][:, 0:T * E].rearrange("p (t e) -> p t e", t=T), rbb, ALU.add))

                def spread(c):
                    return c[:].rearrange("p (t e) -> p t e", e=1).broadcast_to((P, T, E))

                def top(src, val, hot_):
                    link(b, v.tensor_reduce(val[:], src[:], AX_X, ALU.max))
                    link(b, v.tensor_tensor(eq[:], src[:], spread(val), ALU.is_equal))
                    link(b, v.tensor_tensor(eq[:], eq[:], rev[:], ALU.mult))
                    link(b, v.tensor_reduce(mi[:], eq[:], AX_X, ALU.max))
                    link(b, v.tensor_tensor(hot_[:], rev[:], spread(mi), ALU.is_equal))

                top(lg, v1, oh1)
                link(b, v.scalar_tensor_tensor(lg2[:], oh1[:], -3e38, lg[:], ALU.mult, ALU.add))
                top(lg2, v2, oh2)
                v.tensor_tensor(hot[:], oh1[:], oh2[:], ALU.add).then_inc(hot_ready.sem, 1)
                v.tensor_tensor(v2[:], v2[:], v1[:], ALU.subtract).then_inc(d_ready.sem, 1)
                e2_ready.wait(dve, b, 1)
                link(b, v.tensor_scalar(pw1[:], e2[:], 1.0, None, ALU.add))
                link(b, v.reciprocal(pw1[:], pw1[:]))
                link(b, v.tensor_tensor(pw2[:], e2[:], pw1[:], ALU.mult))
                link(b, v.tensor_tensor(wa[:], oh1[:], spread(pw1), ALU.mult))
                link(b, v.tensor_tensor(eq[:], oh2[:], spread(pw2), ALU.mult))
                v.tensor_copy(rows[:, :, D + E:D + E + 1].bitcast(I32), token[:].rearrange("p (t o) -> p t o", o=1))
                link(b, v.tensor_tensor(rows[:, :, D:D + E], wa[:], eq[:], ALU.add))
                v.tensor_scalar(token[:], token[:], S, None, ALU.add).then_inc(rows_ready.sem, 1)

                rank_ready.wait(dve, b, 1)
                pr = bank[1][:, 0:2 * T * E].rearrange("p (a t e) -> p a t e", a=2, t=T)
                runb = run[:].rearrange("p (t e) -> p t e", t=1).broadcast_to((P, T, E))
                link(b, v.tensor_tensor(rank[:], pr[:, 0], runb, ALU.add))
                v.tensor_tensor(rank[:, 1], pr[:, 1, 0], rank[:, 1], ALU.add)
                v.tensor_tensor(run[:], pr[:, 1, 0], run[:], ALU.add).then_inc(dve_tail, 1)
                dve.wait_ge(dve_tail, b * 2 + 1)
                v.tensor_tensor(run[:], pr[:, 1, 1], run[:], ALU.add).then_inc(rank_used.sem, 1)
                v.tensor_tensor(rank[:], rank[:], region0[:], ALU.add).then_inc(dve_tail, 1)
                dve.wait_ge(dve_tail, b * 2 + 2)
                v.tensor_tensor(wa[:], oh1[:], rank[:], ALU.mult)
                link(b, v.tensor_tensor(eq[:], oh2[:], rank[:], ALU.mult))
                v.tensor_reduce(slotf[:, 0], wa[:], AX_X, ALU.add)
                link(b, v.tensor_reduce(slotf[:, 1], eq[:], AX_X, ALU.add))
                v.tensor_copy(slot_i[:], slotf[:]).then_inc(slots_ready.sem, 1)
                assert Chain.n == CHAIN

            def step(ins):
                Chain.n += 1
                ins.then_inc(dve_chain, 1)
                dve.wait_ge(dve_chain, Chain.n)

            Chain.n = B * CHAIN
            rank_used.wait(dve, B - 1, 1)
            step(v.tensor_copy(cnt_i[:], run[0:1, :]))
            v.sem_inc(tables.sem, 1)
            step(v.tensor_scalar(til_f[:], run[0:1, :], float(P - 1), None, ALU.add))
            step(v.tensor_copy(til_i[:], til_f[:]))
            step(v.tensor_scalar(til_i[:], til_i[:], 7, None, ALU.arith_shift_right))
            step(v.tensor_copy(til_f[:], til_i[:]))
            step(v.tensor_tensor_scan(cum_f[:], one8[:], til_f[:], 0.0, ALU.mult, ALU.add))
            step(v.tensor_copy(cum_i[:], cum_f[:]))
            jb = jj[:].rearrange("p (j e) -> p j e", e=1).broadcast_to((1, NTAB, E))
            cb = cum_f[:].rearrange("p (j e) -> p j e", j=1).broadcast_to((1, NTAB, E))
            tb = til_f[:].rearrange("p (j e) -> p j e", j=1).broadcast_to((1, NTAB, E))
            step(v.tensor_tensor(ge[:], jb, cb, ALU.is_ge))
            step(v.tensor_tensor(get_[:], ge[:], tb, ALU.mult))
            step(v.tensor_reduce(ef[:], ge[:], AX_X, ALU.add))
            step(v.tensor_reduce(fin_t[:], get_[:], AX_X, ALU.add))
            step(v.tensor_tensor(loc[:], jj[:], fin_t[:], ALU.subtract))
            step(v.tensor_scalar(lt8[:], ef[:], float(E), float(P), ALU.is_lt, ALU.mult))
            step(v.tensor_tensor(loc[:], loc[:], lt8[:], ALU.mult))
            step(v.scalar_tensor_tensor(rowf[:], ef[:], float(REGION), loc[:], ALU.mult, ALU.add))
            step(v.tensor_copy(tile_row[:], rowf[:]))
            step(v.tensor_scalar(e7[:], ef[:], float(E - 1), None, ALU.min))
            step(v.tensor_copy(tile_e[:], e7[:]))
            step(v.tensor_scalar(tile_slot[:], tile_e[:], 1, None, ALU.bitwise_and))
            v.sem_inc(tables.sem, 1)
            dve.sem_inc(hb_ready.sem, 4)
            dve.sem_inc(hid_ready.sem, 4)
            dve.sem_inc(y1_ready.sem, 1)

            def hidden(j, p):
                e = dve.value_load(tile_e[0:1, bass.ds(j, 1)], min_val=0, max_val=E - 1)
                slot = dve.value_load(tile_slot[0:1, bass.ds(j, 1)], min_val=0, max_val=1)
                b1_loaded.wait(dve, e, 16)
                hid_ready.wait(dve, j, -2)
                ht_ready.wait(dve, j, -2)
                for n, c in enumerate(L1_ORDER):
                    l1_ready.wait(dve, j, n + 1)
                    v.tensor_tensor(hb[p][:, c * 512:(c + 1) * 512], bank[c][:],
                                    b1_ring[:, bass.ds(slot, 1), c * 512:(c + 1) * 512].rearrange("p o n -> p (o n)"),
                                    ALU.add).then_inc(hb_ready.sem, 1)
                    if n % 2 == 1:
                        half = n // 2
                        hb_ready.wait(dve, j, n + 1)
                        sil_ready.wait(dve, j, half + 1)
                        cols = slice(half * 512, (half + 1) * 512)
                        v.tensor_tensor(hid[p][:, cols], hsil[:, cols], hb[p][:, HID + half * 512:HID + (half + 1) * 512],
                                        ALU.mult).then_inc(hid_ready.sem, 1)

            def bias_y(j):
                slot = dve.value_load(tile_slot[0:1, bass.ds(j, 1)], min_val=0, max_val=1)
                tile_done.wait(dve, j, 1)
                y2_ready.wait(dve, j, 0)
                v.tensor_tensor(y1, bank[7][:, 0:D], b2_ring[:, bass.ds(slot, 1), :].rearrange("p o n -> p (o n)"),
                                ALU.add).then_inc(y1_ready.sem, 1)

            hidden(0, 0)
            with dve.Fori(0, PAIRED + 1) as i:
                hidden(i * 2 + 1, 1)
                bias_y(i * 2)
                hidden(i * 2 + 2, 0)
                bias_y(i * 2 + 1)
            bias_y(NTILE - 1)

        @block.tensor
        def _(pe):
            t_ = nc.tensor
            pe.sem_inc(pt_ready.sem, P_RING)
            pe.sem_inc(pv_done.sem, 2)
            pe.sem_inc(ckv_done.sem, 2)
            pe.sem_inc(tile_done.sem, 1)
            pe.wait_ge(w_in.sem, 16 * NW)
            pe.wait_ge(consts.sem, 21)

            def turn(b, src, dst, n):
                for k in range(KT):
                    for t in range(T):
                        ins = t_.transpose(dst[:, k * S + t * P:k * S + (t + 1) * P], src[:, t, k * P:(k + 1) * P], ident[:])
                ins.then_inc(tr_ready.sem, 1)

            def scores(b, u):
                bk = bank[u % S_RING]
                masked_ready.wait(pe, b, u - S_RING + 1)
                if u < H:
                    m, par = divmod(u, 2)
                    t_.matmul(bk[:, 0:P], q_pad[:, m, par, 0:P], k_T[:, m, 0:P], start=True, stop=True)
                    t_.matmul(bk[:, P:3 * P], q_pad[:, m, par, P:S], k_T[:, m, :], start=True, stop=True).then_inc(scores_ready.sem, 1)
                else:
                    m, h8 = divmod(u - H, HPC)
                    for t in range(T):
                        ins = t_.matmul(bk[:, t * S:(t + 1) * S], cq_pad[:, m, h8, t * P:(t + 1) * P], ck_T[:, m, :], start=True, stop=True)
                    ins.then_inc(scores_ready.sem, 1)

            def probs_T(b, u):
                wait_evac(pe, b, u - 2)
                if u < H:
                    norm_ready.wait(pe, b, u + 1)
                else:
                    exp_ready.wait(pe, b, u + 1)
                for c in range(blocks(u)):
                    to = c if u < H else (c % 2) * 2 + c // 2
                    ins = t_.transpose(bank[4 + u % 2][:, to * P:(to + 1) * P], prob[:, u % P_RING, c * P:(c + 1) * P], ident[:])
                ins.then_inc(pt_ready.sem, 1)

            def times_v(b, u):
                pT = prob_T[:, u % 2]
                wait_evac(pe, b, u)
                if u < H:
                    j, par = divmod(u, 2)
                    if par == 0:
                        o_evac.wait(pe, b, j - 1)
                    o = bank[6 + j % 2][64 * par:64 * par + 64]
                    t_.matmul(o[:, 0:S], v_sb[:, 0, u * DH:(u + 1) * DH], pT[:, 0:S], start=True, stop=False)
                    ins = t_.matmul(o[:, P:S], v_sb[:, 1, u * DH:(u + 1) * DH], pT[:, S:S + P], start=False, stop=True)
                else:
                    h = u - H
                    j, c = PAIRS + h // GROUP, h % GROUP
                    if c == 0:
                        o_evac.wait(pe, b, j - 1)
                    o = bank[6 + j % 2][32 * c:32 * c + 32]
                    for k in range(T):
                        ins = t_.matmul(o[:, 0:S], cv_sb[:, k, h, :], pT[:, k * S:(k + 1) * S], start=k == 0, stop=k == T - 1)
                ins.then_inc(pv_done.sem, 1)

            def heads(b, u0):
                for s in range(u0, u0 + H + LAG_V):
                    if s < u0 + H:
                        scores(b, s)
                    if u0 <= s - LAG_T < u0 + H:
                        probs_T(b, s - LAG_T)
                    if u0 <= s - LAG_V < u0 + H:
                        times_v(b, s - LAG_V)

            with pe.Fori(0, B) as b:
                xn_ready.wait(pe, b, 1)
                turn(b, xn, bank[6], 1)
                xnT_ready.wait(pe, b, 1)
                rank_used.wait(pe, b, 0)
                for n in range(12):
                    bk = bank[n % 6]
                    if n >= 6:
                        o = n - 6
                        if o % 2 == 0:
                            q_evac.wait(pe, b, o + 2)
                        else:
                            kv_evac.wait(pe, b, (o + 1) // 2)
                    if n < 8:
                        f, which = n // 2, n % 2
                        for c in range(2):
                            for k in range(KT):
                                ins = t_.matmul(bk[:, c * S:(c + 1) * S], w_qkv[:, which, k, (2 * f + c) * P:(2 * f + c + 1) * P],
                                                xnT[:, k, :], start=k == 0, stop=k == KT - 1)
                    else:
                        t, half = divmod(n - 8, 2)
                        for k in range(KT):
                            ins = t_.matmul(bk[:], xnT[:, k, t * P:(t + 1) * P], w_qkv[:, 2, k, half * 512:(half + 1) * 512],
                                            start=k == 0, stop=k == KT - 1)
                    ins.then_inc(fill_done.sem, 1)
                q_evac.wait(pe, b, 8)
                kv_evac.wait(pe, b, 8)
                heads(b, 0)
                o_evac.wait(pe, b, PAIRS)
                for t in range(T):
                    for m in range(PAIRS):
                        ins = t_.matmul(bank[7][:, t * D:(t + 1) * D], z_T[:, m, t * P:(t + 1) * P], wo_sb[:, m, :],
                                        start=m == 0, stop=m == PAIRS - 1)
                ins.then_inc(attn_out.sem, 1)
                ctx_loaded.wait(pe, b, 16)
                for m in range(KT):
                    for k in range(KT):
                        ins = t_.matmul(bank[1][:, m * S:(m + 1) * S], cw[:, 1, k, m * P:(m + 1) * P], ctxT_in[:, k, :],
                                        start=k == 0, stop=k == KT - 1)
                ins.then_inc(ckv_done.sem, 1)
                for t in range(T):
                    for k in range(KT):
                        ins = t_.matmul(bank[2][:, t * D:(t + 1) * D], ctxT_in[:, k, t * P:(t + 1) * P], cw[:, 2, k, :],
                                        start=k == 0, stop=k == KT - 1)
                ins.then_inc(ckv_done.sem, 1)
                xn_ready.wait(pe, b, 2)
                turn(b, xn, bank[6], 2)
                xnT_ready.wait(pe, b, 2)
                for m in range(KT):
                    for k in range(KT):
                        ins = t_.matmul(bank[0][:, m * S:(m + 1) * S], cw[:, 0, k, m * P:(m + 1) * P], xnT[:, k, :],
                                        start=k == 0, stop=k == KT - 1)
                ins.then_inc(cq_done.sem, 1)
                ck_evac.wait(pe, b, 2)
                cv_evac.wait(pe, b, 2)
                cq_spread.wait(pe, b, 16 * HPC)
                heads(b, H)
                o_evac.wait(pe, b, PAIRS + H // GROUP)
                for t in range(T):
                    for g in range(H // GROUP):
                        ins = t_.transpose(bank[4 + t][:, g * P:(g + 1) * P], o_T[:, g, t * P:(t + 1) * P], ident[:])
                    ins.then_inc(ctx_tr.sem, 1)
                ctx_ready.wait(pe, b, 1)
                turn(b, ctx_sb[:].rearrange("p t h c -> p t (h c)"), bank[7], 3)
                xnT_ready.wait(pe, b, 3)
                for t in range(T):
                    for k in range(KT):
                        ins = t_.matmul(bank[6][:, t * D:(t + 1) * D], xnT[:, k, t * P:(t + 1) * P], cw[:, 3, k, :],
                                        start=k == 0, stop=k == KT - 1)
                ins.then_inc(cx_out.sem, 1)
                xn_ready.wait(pe, b, 3)
                turn(b, rows[:, :, 0:D], bank[7], 4)
                xnT_ready.wait(pe, b, 4)
                for t in range(T):
                    for k in range(KT):
                        ins = t_.matmul(bank[0][:, t * E:(t + 1) * E], xnT[:, k, t * P:(t + 1) * P], rw_sb[:, k, :],
                                        start=k == 0, stop=k == KT - 1)
                ins.then_inc(logits.sem, 1)
                hot_ready.wait(pe, b, 1)
                hot2 = hot[:].rearrange("p t e -> p (t e)")
                t_.matmul(bank[1][:, 0:T * E], before[:], hot2, start=True, stop=True)
                t_.matmul(bank[1][:, T * E:2 * T * E], ones[:], hot2, start=True, stop=True).then_inc(rank_ready.sem, 1)

            pe.sem_inc(l1_ready.sem, 8)
            pe.sem_inc(ht_ready.sem, 4)
            pe.wait_ge(tables.sem, 2)

            def turn_x(i, c):
                j, p = i * 2 + c, c % 2
                xe_loaded[p].wait(pe, i, 16 * (c // 2 + 1))
                xt_evac.wait(pe, j, 0)
                for k in range(KT):
                    ins = t_.transpose(bank[6][:, k * P:(k + 1) * P], xe[p][:, k * P:(k + 1) * P], ident[:])
                ins.then_inc(xt_ready.sem, 1)

            def layer1(j, p, slot, n):
                c = L1_ORDER[n]
                hb_ready.wait(pe, j, -4 + n + 1)
                for k in range(KT):
                    ins = t_.matmul(bank[c][:], xe_T[p][:, k * P:(k + 1) * P],
                                    w1_ring[:, bass.ds(slot, 1), k * 2 * HID + c * 512:k * 2 * HID + (c + 1) * 512].rearrange("p o n -> p (o n)"),
                                    start=k == 0, stop=k == KT - 1)
                ins.then_inc(l1_ready.sem, 1)

            def turn_h(j, p):
                for c in range(2):
                    hid_ready.wait(pe, j, c + 1)
                    ht_evac.wait(pe, j, -2 + c + 1)
                    for q in range(4):
                        k = 4 * c + q
                        ins = t_.transpose(bank[4 + c][:, q * P:(q + 1) * P], hid[p][:, k * P:(k + 1) * P], ident[:])
                    ins.then_inc(ht_ready.sem, 1)

            def layer2(j):
                slot = pe.value_load(tile_slot[0:1, bass.ds(j, 1)], min_val=0, max_val=1)
                y1_ready.wait(pe, j, 0)
                for k in range(8):
                    if k % 4 == 0:
                        ht_evac.wait(pe, j, k // 4 + 1)
                    ins = t_.matmul(bank[7][:, 0:D], hid_T[:, k * P:(k + 1) * P],
                                    w2_ring[:, bass.ds(slot, 1), k * D:(k + 1) * D].rearrange("p o n -> p (o n)"),
                                    start=k == 0, stop=k == 7)
                ins.then_inc(tile_done.sem, 1)

            def step(i, c, prev=True, next_=True):
                j, p = i * 2 + c, c % 2
                e = pe.value_load(tile_e[0:1, bass.ds(j, 1)], min_val=0, max_val=E - 1)
                slot = pe.value_load(tile_slot[0:1, bass.ds(j, 1)], min_val=0, max_val=1)
                w_loaded.wait(pe, e, 48)
                xt_evac.wait(pe, j, 1)
                layer1(j, p, slot, 0)
                if prev:
                    turn_h(j - 1, 1 - p)
                layer1(j, p, slot, 1)
                if next_:
                    turn_x(i, c + 1)
                layer1(j, p, slot, 2)
                layer1(j, p, slot, 3)
                if prev:
                    layer2(j - 1)

            turn_x(0, 0)
            step(0, 0, prev=False)
            with pe.Fori(0, PAIRED) as i:
                step(i, 1)
                step(i, 2)
            step(PAIRED, 1)
            step(PAIRED, 2, next_=False)
            turn_h(NTILE - 1, 0)
            layer2(NTILE - 1)


def kernel(**inputs):
    import numpy as _np
    import concourse.bacc as _bacc
    from concourse import mybir as _mybir
    from concourse.bass_utils import run_bass_kernel_spmd as _run

    a = {k.replace("L0_", ""): _np.asarray(v) for k, v in inputs.items()}

    def by_rows(w, lead=()):
        *_, r, n = w.shape
        w = w.reshape(*w.shape[:-2], r // 128, 128, n)
        return _np.ascontiguousarray(_np.swapaxes(w, -3, -2))

    arrays = {
        "x": by_rows(a["x"]),
        "ctx_t": by_rows(_np.swapaxes(a["ctx_1024"], 1, 2)),
        "mask": by_rows(a["mask_BxSxS2_bk1"]),
        "wq": by_rows(a["attn_W_Q"].reshape(1024, 256).T),
        "wk": by_rows(a["attn_W_K"].reshape(1024, 256).T),
        "wv": by_rows(a["attn_W_V"].reshape(1024, 256).T),
        "wo": by_rows(a["attn_W_O"].T),
        "cwq": by_rows(a["xattn_wq"].T),
        "cwk": by_rows(a["xattn_wk"].T),
        "cwv": by_rows(a["xattn_wv"].T),
        "cwo": by_rows(a["xattn_wo"].T),
        "cbq": _np.ascontiguousarray(a["xattn_bq"].reshape(2, 128).T),
        "cbk": _np.ascontiguousarray(a["xattn_bk"].reshape(2, 128).T),
        "cbv": a["xattn_bv"].reshape(1, 256),
        "cbo": a["xattn_bo"].reshape(1, 256),
        "rw": by_rows(a["ffn_router_w"].T),
        "rb": a["ffn_router_b"].reshape(1, 8),
        "w1": by_rows(_np.swapaxes(a["ffn_w1"], 1, 2)).reshape(8, 128, -1),
        "b1": a["ffn_b1"],
        "w2": by_rows(_np.swapaxes(a["ffn_w2"], 1, 2)).reshape(8, 128, -1),
        "b2": a["ffn_b2"],
    }
    nc = _bacc.Bacc("TRN2", target_bir_lowering=False, num_devices=1)
    args = [nc.dram_tensor(f"in_{n}_dram", v.shape, _mybir.dt.from_np(v.dtype), kind="ExternalInput").ap()
            for n, v in arrays.items()]
    out = nc.dram_tensor("out_0_dram", (TOK + P, D), F32, kind="ExternalOutput").ap()
    build(nc, *args, out)
    r = _run(nc, [{f"in_{n}_dram": v for n, v in arrays.items()}], core_ids=[0])
    return r.results[0]["out_0_dram"][:TOK].reshape(B, S, D)
```

```python
from contextlib import ExitStack

import concourse.bass as bass
from concourse import mybir

F32 = mybir.dt.float32
BF16 = mybir.dt.bfloat16
I32 = mybir.dt.int32
U8 = mybir.dt.uint8
ALU = mybir.AluOpType
ACT = mybir.ActivationFunctionType
AX_X = mybir.AxisListType.X

P = 128
B, S, D = 8, 256, 256
T = S // P
KT = D // P
H, DH = 16, 64
PAIRS = H // 2
CDH = D // H
HPC = P // CDH
GROUP = 4
E, HID = 8, 1024
TOK = B * S
EPS = 1e-5
BIG = 1e30
XBIG = 1e20
REGION = TOK + P
NTILE = 2 * TOK // P + E - 1
NTAB = NTILE + 1
PAIRED = (NTILE - 3) // 2
L1_ORDER = (0, 2, 1, 3)
ROW = D + E + 1
U = 2 * H
S_RING, P_RING = 3, 4
T_RING = 4
QK_FILLS, FILLS = 8, 12
ROUTER_AT = {0: (0, 1), 1: (2,), 2: (3,), 7: (4, 5), 8: (6, 7), 9: (8, 9), 10: (10, 11), 11: (12, 13),
             12: (14, 15, 16), 14: (17, 18), 15: (19, 20), 16: (21, 22), 17: (23, 24), 18: (25, 26, 27)}
ROUTER_STEPS = 28
RSTD_AT, TURN_AT, EVAC_AT, LOGITS_AT, EXP_AT, RANK_AT = 0, 4, 4, 6, 13, 15
LAG_T, LAG_V = 3, 4


class Signal:

    def __init__(self, sem, per, off=0):
        self.sem, self.per, self.off = sem, per, off

    def at(self, b, n):
        return b * self.per + (n + self.off)


def build(nc, x, ctx_t, mask, wq, wk, wv, wo, cwq, cwk, cwv, cwo, cbq, cbk, cbv, cbo,
          rw, rb, w1, b1, w2, b2, out):
    stack = ExitStack()
    with stack:
        def sb(name, shape, dt=F32):
            return stack.enter_context(nc.sbuf_tensor(name, shape, dt))

        def sig(name, per, off=0):
            return Signal(stack.enter_context(nc.semaphore(name)), per, off)

        bank = [stack.enter_context(nc.psum_tensor(f"bank{i}", [P, 512], F32)) for i in range(8)]
        dispatched = nc.dram_tensor("dispatched", [E * REGION + P, ROW], F32).ap()

        w_qkv = sb("w_qkv", [P, 3, KT, H * DH])
        wo_sb = sb("wo_sb", [P, PAIRS, D])
        cw = sb("cw", [P, 4, KT, D])
        cbq_sb = sb("cbq_sb", [P, KT])
        cbk_sb = sb("cbk_sb", [P, KT])
        cbv_sb = sb("cbv_sb", [P, D])
        cbo_sb = sb("cbo_sb", [P, D])
        rw_sb = sb("rw_sb", [P, KT, E])
        rb_sb = sb("rb_sb", [P, E])
        ident = sb("ident", [P, P])
        causal = sb("causal", [P, 3 * P])
        before = sb("before", [P, P], BF16)
        ones = sb("ones", [P, P], BF16)
        neg_half = sb("neg_half", [P, T])
        rev = sb("rev", [P, T, E])
        region0 = sb("region0", [P, T, E])
        token = sb("token", [P, T], I32)
        pad_rows = sb("pad_rows", [P, ROW])

        x_in = sb("x_in", [P, T, D])
        x_norm = sb("x_norm", [P, T, D])
        x_norm_T = sb("x_norm_T", [P, KT, S])
        ctxT_in = sb("ctxT_in", [P, KT, S])
        mask_in = sb("mask_in", [P, T, S], U8)
        cmask = sb("cmask", [P, T, S])
        xn = sb("xn", [P, T, D])
        xnT = sb("xnT", [P, KT, S])
        q_pad = sb("q_pad", [P, PAIRS, 2, S])
        k_T = sb("k_T", [P, PAIRS, S])
        v_sb = sb("v_sb", [P, T, H * DH])
        prob = sb("prob", [P, P_RING, 512])
        prob_T = sb("prob_T", [P, T_RING, 512])
        z_T = sb("z_T", [P, PAIRS, S])
        x1 = sb("x1", [P, T, D])
        cq_T = sb("cq_T", [P, KT, S])
        cq_pad = sb("cq_pad", [P, KT, HPC, S])
        ck_T = sb("ck_T", [P, KT, S])
        cv_sb = sb("cv_sb", [P, T, H, 32])
        o_T = sb("o_T", [P, H // GROUP, S])
        ctx_sb = sb("ctx_sb", [P, T, H, CDH])
        crec = sb("crec", [P, T, H])
        x2 = sb("x2", [P, T, D])
        rows = sb("rows", [P, T, ROW])
        st = sb("st", [P, T, 6])
        mv = sb("mv", [P, T, 2])
        ve = sb("ve", [P, T])
        rstd = sb("rstd", [P, T])
        nmax = sb("nmax", [P, P_RING, 2])
        psum_ = sb("psum_", [P, P_RING, 2])
        r3 = sb("r3", [P, P_RING, 3])
        lg = sb("lg", [P, T, E])
        lg2 = sb("lg2", [P, T, E])
        eq = sb("eq", [P, T, E])
        oh1 = sb("oh1", [P, T, E])
        oh2 = sb("oh2", [P, T, E])
        wa = sb("wa", [P, T, E])
        hot = sb("hot", [P, T, E], BF16)
        v1 = sb("v1", [P, T])
        v2 = sb("v2", [P, T])
        mi = sb("mi", [P, T])
        e2 = sb("e2", [P, T])
        pw1 = sb("pw1", [P, T])
        pw2 = sb("pw2", [P, T])
        run = sb("run", [P, E])
        rank = sb("rank", [P, T, E])
        slotf = sb("slotf", [P, 2, T])
        slot_i = sb("slot_i", [P, 2, T], I32)

        w1_ring = sb("w1_ring", [P, 2, KT * 2 * HID])
        w2_ring = sb("w2_ring", [P, 2, (HID // P) * D])
        b2_ring = sb("b2_ring", [P, 2, D])
        b1_ring = cq_pad[:].rearrange("p k h s -> p (k h s)").rearrange("p (r n) -> p r n", r=2)
        arena = w_qkv[:].rearrange("p a k n -> p (a k n)")
        hb = [arena[:, 2048 * i:2048 * (i + 1)] for i in range(2)]
        hsil = arena[:, 4096:5120]
        xe_T = [arena[:, 5120 + 256 * i:5376 + 256 * i] for i in range(2)]
        arena2 = q_pad[:].rearrange("p a k n -> p (a k n)")
        hid = [arena2[:, 1024 * i:1024 * (i + 1)] for i in range(2)]
        hid_T = arena2[:, 2048:3072]
        y1 = arena2[:, 3072:3328]
        y2 = [arena2[:, 3328 + 256 * i:3584 + 256 * i] for i in range(2)]
        xe = [buf[:].rearrange("p a b -> p (a b)")[:, 0:ROW] for buf in (ctxT_in, x_in)]
        tails = x_norm_T[:].rearrange("p a b -> p (a b)")[:, 0:NTAB * (E + 1)].rearrange("p (j e) -> p j e", j=NTAB)
        ids = sb("ids", [P, 1], I32)

        cnt_i = sb("cnt_i", [1, E], I32)
        til_i = sb("til_i", [1, E], I32)
        til_f = sb("til_f", [1, E])
        one8 = sb("one8", [1, E])
        cum_f = sb("cum_f", [1, E])
        cum_i = sb("cum_i", [1, E], I32)
        jj = sb("jj", [1, NTAB])
        ge, get_ = (prob[0:1, i, 0:NTAB * E].rearrange("p (j e) -> p j e", j=NTAB) for i in range(2))
        ef = sb("ef", [1, NTAB])
        fin_t = sb("fin_t", [1, NTAB])
        lt8 = sb("lt8", [1, NTAB])
        loc = sb("loc", [1, NTAB])
        e7 = sb("e7", [1, NTAB])
        rowf = sb("rowf", [1, NTAB])
        tile_e = sb("tile_e", [1, NTAB], I32)
        tile_slot = sb("tile_slot", [1, NTAB], I32)
        tile_row = sb("tile_row", [1, NTAB], I32)

        w_in = sig("w_in", 0)
        consts = sig("consts", 0)
        passed = sig("passed", 0)
        x_loaded = sig("x_loaded", 16)
        x_norm_loaded = sig("x_norm_loaded", 16)
        ctx_loaded = sig("ctx_loaded", 16)
        mask_loaded = sig("mask_loaded", 16)
        ln_chain = [sig(f"ln{i}_chain", 2) for i in (1, 2, 3)]
        var_ready = [sig(f"var{i}_ready", 1) for i in (1, 2, 3)]
        rstd_ready = [sig(f"rstd{i}_ready", 1) for i in (1, 2, 3)]
        xn_ready = [sig(f"xn{i}_ready", 1) for i in (1, 2, 3)]
        turned = [sig(f"turned{i}", 1) for i in (1, 2, 3)] + [sig("ctx_turned", 1)]
        xnT_ready = [sig(f"xn{i}T_ready", 1) for i in (1, 2, 3)] + [sig("ctxT_ready", 1)]
        fill_done = sig("fill_done", FILLS)
        q_evac = sig("q_evac", 8)
        kv_evac = sig("kv_evac", 8)
        scores_ready = sig("scores_ready", U)
        masked_ready = sig("masked_ready", U, 3)
        exp_ready = sig("exp_ready", U)
        recip_ready = sig("recip_ready", H)
        norm_ready = sig("norm_ready", H)
        pt_ready = sig("pt_ready", U, P_RING)
        pt_evac_act = sig("pt_evac_act", U // 4, 4)
        pt_evac_dve = sig("pt_evac_dve", U - U // 4, 4)
        pv_done = sig("pv_done", U, T_RING)
        o_evac = sig("o_evac", PAIRS + H // GROUP, 2)
        attn_out = sig("attn_out", 1)
        x1_done = sig("x1_done", 1)
        x1b_done = sig("x1b_done", 1)
        ckv_done = sig("ckv_done", 2)
        ck_evac = sig("ck_evac", 2)
        cv_evac = sig("cv_evac", 2)
        cq_done = sig("cq_done", 1)
        cq_evac = sig("cq_evac", 2)
        cq_spread = sig("cq_spread", 16 * HPC)
        cmask_ready = sig("cmask_ready", 1)
        ctx_tr = sig("ctx_tr", 2)
        crec_ready = sig("crec_ready", 2)
        ctx_ready = sig("ctx_ready", 1)
        cx_out = sig("cx_out", 1)
        x2_ready = sig("x2_ready", 1, 1)
        x2_stored = sig("x2_stored", 16)
        x2_free = sig("x2_free", 1, 1)
        rows_free = sig("rows_free", 1, 1)
        router_chain = sig("router_chain", ROUTER_STEPS)
        logits = sig("logits", 1)
        d_ready = sig("d_ready", 1)
        e2_ready = sig("e2_ready", 1)
        hot_ready = sig("hot_ready", 1)
        rank_ready = sig("rank_ready", 1)
        rank_used = sig("rank_used", 1, 1)
        slots_ready = sig("slots_ready", 1)
        rows_ready = sig("rows_ready", 1)
        scattered = sig("scattered", 64)
        tables = sig("tables", 0)
        table_chain = stack.enter_context(nc.semaphore("table_chain"))
        pads_done = sig("pads_done", 0)
        w_loaded = sig("w_loaded", 48)
        b1_loaded = sig("b1_loaded", 16)
        tile_done = sig("tile_done", 1, 1)
        xe_loaded = [sig(f"xe_loaded{i}", 16) for i in range(2)]
        tail_copied = sig("tail_copied", 1)
        xt_ready = sig("xt_ready", 1)
        xt_evac = sig("xt_evac", 1, 1)
        l1_ready = sig("l1_ready", 4, 8)
        hb_ready = sig("hb_ready", 4, 4)
        sil_ready = sig("sil_ready", 2)
        hid_ready = sig("hid_ready", 2, 4)
        ht_ready = sig("ht_ready", 2, 4)
        ht_evac = sig("ht_evac", 2, 2)
        y1_ready = sig("y1_ready", 1, 1)
        y2_ready = sig("y2_ready", 1, 1)
        ids_ready = sig("ids_ready", 1, 1)
        added = sig("added", 16)

        NW = 15

        def evacs(u):
            return (u + 1) // 4, u + 1 - (u + 1) // 4

        def wait_evac(eng, b, u):
            if u % 4 == 3:
                eng.wait_ge(pt_evac_act.sem, pt_evac_act.at(b, evacs(u)[0]))
            else:
                eng.wait_ge(pt_evac_dve.sem, pt_evac_dve.at(b, evacs(u)[1]))

        def blocks(u):
            return 3 if u < H else 4

        def fill_bank(n):
            return bank[(n + 3) % 6] if n < QK_FILLS else bank[n - QK_FILLS]

        block = stack.enter_context(nc.Block())

        @block.sync
        def _(sp):
            sp.sem_inc(x2_free.sem, 1)
            sp.dma_start(x_norm[:], x[0]).then_inc(x_norm_loaded.sem, 16)
            for i, w in enumerate((wq, wk, wv)):
                sp.dma_start(w_qkv[:, i], w).then_inc(w_in.sem, 16)
            sp.dma_start(wo_sb[:], wo).then_inc(w_in.sem, 16)
            for i, w in enumerate((cwq, cwk, cwv, cwo)):
                sp.dma_start(cw[:, i], w).then_inc(w_in.sem, 16)
            sp.dma_start(cbq_sb[:], cbq).then_inc(w_in.sem, 16)
            sp.dma_start(cbk_sb[:], cbk).then_inc(w_in.sem, 16)
            sp.dma_start(cbv_sb[:], cbv.broadcast_to((P, D))).then_inc(w_in.sem, 16)
            sp.dma_start(cbo_sb[:], cbo.broadcast_to((P, D))).then_inc(w_in.sem, 16)
            sp.dma_start(rw_sb[:], rw).then_inc(w_in.sem, 16)
            sp.dma_start(rb_sb[:], rb.broadcast_to((P, E))).then_inc(w_in.sem, 16)
            sp.wait_ge(consts.sem, 12)
            sp.dma_start(out[TOK:TOK + P, :], pad_rows[:, 0:D]).then_inc(w_in.sem, 16)
            sp.dma_start(dispatched[E * REGION:E * REGION + P, :], pad_rows[:]).then_inc(pads_done.sem, 16)

            def load_w(e):
                slot = e % 2
                sp.dma_start(w1_ring[:, bass.ds(slot, 1), :], w1[bass.ds(e, 1)].rearrange("e p n -> p e n")).then_inc(w_loaded.sem, 16)
                sp.dma_start(w2_ring[:, bass.ds(slot, 1), :], w2[bass.ds(e, 1)].rearrange("e p n -> p e n")).then_inc(w_loaded.sem, 16)
                sp.dma_start(b2_ring[:, bass.ds(slot, 1), :],
                             b2[bass.ds(e, 1), :].rearrange("e n -> () e n").broadcast_to((P, 1, D))).then_inc(w_loaded.sem, 16)

            def load_b1(e):
                sp.dma_start(b1_ring[:, bass.ds(e % 2, 1), :],
                             b1[bass.ds(e, 1), :].rearrange("e n -> () e n").broadcast_to((P, 1, 2 * HID))).then_inc(b1_loaded.sem, 16)

            def came(e):
                sp.wait_ge(w_loaded.sem, w_loaded.at(e, 48))
                sp.sem_inc(passed.sem, 1)
                sp.wait_ge(b1_loaded.sem, b1_loaded.at(e, 16))
                sp.sem_inc(passed.sem, 1)

            sp.dma_start(x_in[:], x[0]).then_inc(x_loaded.sem, 16)
            sp.dma_start(ctxT_in[:], ctx_t[0]).then_inc(ctx_loaded.sem, 16)
            sp.dma_start(mask_in[:], mask[0]).then_inc(mask_loaded.sem, 16)
            load_w(0)

            def batch(b, last=False):
                if not last:
                    sp.wait_ge(turned[0].sem, turned[0].at(b, 1))
                    sp.dma_start(x_norm[:], x[b + 1]).then_inc(x_norm_loaded.sem, 16)
                    sp.wait_ge(x1_done.sem, x1_done.at(b, 1))
                    sp.dma_start(x_in[:], x[b + 1]).then_inc(x_loaded.sem, 16)
                    sp.wait_ge(ckv_done.sem, ckv_done.at(b, 2))
                    sp.dma_start(ctxT_in[:], ctx_t[b + 1]).then_inc(ctx_loaded.sem, 16)
                sp.wait_ge(cq_evac.sem, cq_evac.at(b, 2))
                for h8 in range(HPC):
                    r = slice(h8 * CDH, (h8 + 1) * CDH)
                    sp.dma_start(cq_pad[r, :, h8, :], cq_T[r, :, :]).then_inc(cq_spread.sem, 16)
                if not last:
                    sp.wait_ge(cmask_ready.sem, cmask_ready.at(b, 1))
                    sp.dma_start(mask_in[:], mask[b + 1]).then_inc(mask_loaded.sem, 16)
                sp.wait_ge(x2_ready.sem, x2_ready.at(b, 1))
                sp.dma_start(out[bass.ds(b * S, S), :].rearrange("(t p) d -> p t d", p=P), x2[:]).then_inc(x2_stored.sem, 16)
                sp.wait_ge(x2_stored.sem, x2_stored.at(b, 16))
                sp.sem_inc(x2_free.sem, 1)

            with sp.Fori(0, B - 1) as b:
                batch(b)
            batch(B - 1, last=True)

            load_b1(0)
            came(0)
            load_w(1)
            load_b1(1)
            sp.wait_ge(tables.sem, 1)
            with sp.Fori(0, E) as e:
                n = sp.value_load(cnt_i[0:1, bass.ds(e, 1)], min_val=0, max_val=TOK)
                sp.dma_start(dispatched[bass.ds(e * REGION + n, P), :], pad_rows[:]).then_inc(pads_done.sem, 16)
            sp.wait_ge(tables.sem, 2)
            with sp.Fori(2, E) as e:
                n = sp.value_load(cum_i[0:1, bass.ds(e - 2, 1)], min_val=0, max_val=NTILE)
                sp.wait_ge(y1_ready.sem, n + 1)
                came(e - 1)
                load_w(e)
                load_b1(e)
            came(E - 1)

        @block.gpsimd
        def _(pool):
            g = nc.gpsimd
            g.memset(ident[:], 0.0).then_inc(consts.sem, 1)
            g.memset(causal[:], 0.0).then_inc(consts.sem, 1)
            g.memset(before[:], 1.0).then_inc(consts.sem, 1)
            g.memset(ones[:], 1.0).then_inc(consts.sem, 1)
            g.memset(neg_half[:], -0.5).then_inc(consts.sem, 1)
            g.memset(pad_rows[:], 0.0).then_inc(consts.sem, 1)
            g.iota(token[:], [[P, T]], base=0, channel_multiplier=1).then_inc(consts.sem, 1)
            pool.wait_ge(consts.sem, 7)
            g.affine_select(out=ident[:], in_=ident[:], compare_op=ALU.not_equal, fill=1.0, base=0,
                            pattern=[[-1, P]], channel_multiplier=1).then_inc(consts.sem, 1)
            for c in (0, 2):
                g.affine_select(out=causal[:, c * P:(c + 1) * P], in_=causal[:, c * P:(c + 1) * P],
                                compare_op=ALU.is_ge, fill=BIG, base=0, pattern=[[-1, P]],
                                channel_multiplier=1).then_inc(consts.sem, 1)
            g.affine_select(out=before[:], in_=before[:], compare_op=ALU.is_gt, fill=0.0, base=0,
                            pattern=[[1, P]], channel_multiplier=-1).then_inc(consts.sem, 1)
            g.iota(pad_rows[:, D + E:D + E + 1].bitcast(I32), [[0, 1]], base=TOK, channel_multiplier=1).then_inc(consts.sem, 1)
            g.iota(rev[:], [[0, T], [-1, E]], base=E, channel_multiplier=0,
                   allow_small_or_imprecise_dtypes=True).then_inc(consts.sem, 1)
            g.iota(region0[:], [[0, T], [REGION, E]], base=0, channel_multiplier=0,
                   allow_small_or_imprecise_dtypes=True).then_inc(consts.sem, 1)
            g.memset(q_pad[:], 0.0).then_inc(consts.sem, 1)
            g.memset(cq_pad[:], 0.0).then_inc(consts.sem, 1)
            g.memset(cv_sb[:], 0.0).then_inc(consts.sem, 1)
            g.memset(run[:], 0.0).then_inc(consts.sem, 1)
            pool.wait_ge(consts.sem, 18)
            g.memset(cv_sb[:, :, :, CDH:CDH + 1], 1.0).then_inc(consts.sem, 1)
            g.iota(jj[:], [[1, NTAB]], base=0, channel_multiplier=0,
                   allow_small_or_imprecise_dtypes=True).then_inc(consts.sem, 1)
            g.memset(one8[:], 1.0).then_inc(consts.sem, 1)
            pool.sem_inc(rows_free.sem, 1)
            pool.wait_ge(w_in.sem, 16 * NW)

            def rsqrt(b, n):
                pool.wait_ge(var_ready[n - 1].sem, var_ready[n - 1].at(b, 1))
                g.tensor_tensor(rstd[:], ve[:], neg_half[:], ALU.pow).then_inc(rstd_ready[n - 1].sem, 1)

            def scatter(b):
                pool.wait_ge(rows_ready.sem, rows_ready.at(b, 1))
                pool.wait_ge(slots_ready.sem, slots_ready.at(b, 1))
                pool.sem_inc(passed.sem, 1)
                for k in range(2):
                    for t in range(T):
                        g.indirect_dma_start(dispatched[:, :], bass.IndirectOffsetOnAxis(ap=slot_i[:, k, t:t + 1], axis=0),
                                             rows[:, t, :], None).then_inc(scattered.sem, 16)

            def batch(b, first=False, last=False):
                for h in range(H):
                    k = h % P_RING
                    pool.wait_ge(recip_ready.sem, recip_ready.at(b, h + 1))
                    pr = prob[:, k, 0:3 * P].rearrange("p (c n) -> p c n", c=3)
                    rr = r3[:, k, :].rearrange("p (c o) -> p c o", o=1).broadcast_to((P, 3, P))
                    g.tensor_tensor(pr, pr, rr, ALU.mult).then_inc(norm_ready.sem, 1)
                    if h == RSTD_AT and not first:
                        rsqrt(b - 1, 3)
                if not last:
                    rsqrt(b + 1, 1)
                if not first:
                    scatter(b - 1)
                rsqrt(b, 2)
                pool.wait_ge(xn_ready[1].sem, xn_ready[1].at(b, 1))
                for t in range(T):
                    ins = g.tensor_tensor(x1[:, t], x1[:, t], cbo_sb[:], ALU.add)
                ins.then_inc(x1b_done.sem, 1)
                pool.wait_ge(mask_loaded.sem, mask_loaded.at(b, 16))
                pool.sem_inc(passed.sem, 1)
                g.tensor_scalar(cmask[:], mask_in[:], XBIG, None, ALU.mult).then_inc(cmask_ready.sem, 1)
                if not first:
                    pool.wait_ge(scattered.sem, scattered.at(b - 1, 64))
                    pool.sem_inc(rows_free.sem, 1)

            rsqrt(0, 1)
            batch(0, first=True)
            with pool.Fori(1, B - 1) as b:
                batch(b)
            batch(B - 1, last=True)
            rsqrt(B - 1, 3)
            scatter(B - 1)

            pool.wait_ge(x2_stored.sem, 16 * B)

            pool.sem_inc(ids_ready.sem, 1)

            def copy_tail(i, c):
                pool.wait_ge(xe_loaded[c % 2].sem, xe_loaded[c % 2].at(i, 16 * (c // 2 + 1)))
                g.tensor_copy(tails[:, bass.ds(i * 2 + c, 1), :].rearrange("p o n -> p (o n)").bitcast(I32),
                              xe[c % 2][:, D:ROW].bitcast(I32)).then_inc(tail_copied.sem, 1)

            def add_out(j, p, first=False):
                if not first:
                    pool.wait_ge(added.sem, added.at(j, 0))
                    pool.sem_inc(passed.sem, 1)
                pool.wait_ge(tail_copied.sem, tail_copied.at(j, 1))
                g.tensor_copy(ids[:], tails[:, bass.ds(j, 1), E:E + 1].rearrange("p o n -> p (o n)").bitcast(I32)).then_inc(ids_ready.sem, 1)
                pool.wait_ge(y2_ready.sem, y2_ready.at(j, 1))
                pool.sem_inc(passed.sem, 1)
                pool.wait_ge(ids_ready.sem, ids_ready.at(j, 1))
                pool.sem_inc(passed.sem, 1)
                g.indirect_dma_start(out[:, :], bass.IndirectOffsetOnAxis(ap=ids[:], axis=0),
                                     y2[p], None, compute_op=ALU.add).then_inc(added.sem, 16)

            copy_tail(0, 0)
            copy_tail(0, 1)
            copy_tail(0, 2)
            add_out(0, 0, first=True)
            with pool.Fori(0, PAIRED) as i:
                copy_tail(i, 3)
                add_out(i * 2 + 1, 1)
                copy_tail(i, 4)
                add_out(i * 2 + 2, 0)
            add_out(NTILE - 2, 1)
            add_out(NTILE - 1, 0)
            pool.wait_ge(added.sem, 16 * NTILE)

        @block.scalar
        def _(act):
            a = nc.scalar
            act.sem_inc(o_evac.sem, 2)
            act.sem_inc(pt_evac_act.sem, 4)
            act.wait_ge(w_in.sem, 16 * NW)
            act.wait_ge(consts.sem, 21)

            def evac_xnT(b, n, src):
                act.wait_ge(turned[n - 1].sem, turned[n - 1].at(b, 1))
                dst = x_norm_T if n == 1 else xnT
                a.copy(dst[:].rearrange("p k s -> p (k s)"), src[:]).then_inc(xnT_ready[n - 1].sem, 1)

            def evac_q(b, f):
                act.wait_ge(fill_done.sem, fill_done.at(b, 2 * f + 1))
                src = fill_bank(2 * f)[:].rearrange("p (c s) -> p c s", c=2)
                for par in range(2):
                    r = slice(64 * par, 64 * par + 64)
                    a.mul(q_pad[r, 2 * f:2 * f + 2, par, :], src[r], -float(DH) ** -0.5).then_inc(q_evac.sem, 1)

            def exps(b, u):
                k = u % P_RING
                act.wait_ge(masked_ready.sem, masked_ready.at(b, u + 1))
                w = P if u < H else S
                for t in range(T):
                    lo = t * w
                    hi = lo + w if u >= H else (t + 1) * (t + 2) // 2 * P
                    pr = prob[:, k, lo:hi]
                    if u < H:
                        ins = a.activation(pr, pr, ACT.Exp, bias=nmax[:, k, t:t + 1], scale=-1.0,
                                           accum_out=psum_[:, k, t:t + 1])
                    else:
                        ins = a.activation(pr, pr, ACT.Exp, bias=nmax[:, k, t:t + 1], scale=-1.0)
                ins.then_inc(exp_ready.sem, 1)

            def evac_pt(b, u):
                n = blocks(u) * P
                act.wait_ge(pt_ready.sem, pt_ready.at(b, u + 1))
                act.wait_ge(pv_done.sem, pv_done.at(b, u - T_RING + 1))
                a.copy(prob_T[:, u % T_RING, 0:n], bank[4 + u % 2][:, 0:n]).then_inc(pt_evac_act.sem, 1)

            def heads(b, u0, router=False):
                for s in range(u0, u0 + H + LAG_V + 1):
                    if s < u0 + H:
                        exps(b, s)
                    if router and s == EVAC_AT:
                        evac_xnT(b - 1, 3, bank[3])
                    if router and s == EXP_AT:
                        exp_difference(b - 1)
                    u = s - LAG_T
                    if u0 <= u < u0 + H and u % 4 == 3:
                        evac_pt(b, u)
                    u = s - LAG_V - 1
                    if u >= u0 and u0 < H and u % 2 == 1:
                        act.wait_ge(pv_done.sem, pv_done.at(b, u + 1))
                        j = u // 2
                        a.copy(z_T[:, j], bank[6 + j % 2][:, 0:S]).then_inc(o_evac.sem, 1)
                    if u >= u0 and u0 >= H and u % GROUP == GROUP - 1:
                        act.wait_ge(pv_done.sem, pv_done.at(b, u + 1))
                        j = PAIRS + (u - H) // GROUP
                        a.copy(o_T[:, j - PAIRS], bank[6 + j % 2][:, 0:S]).then_inc(o_evac.sem, 1)

            def exp_difference(b):
                act.wait_ge(d_ready.sem, d_ready.at(b, 1))
                a.activation(e2[:], v2[:], ACT.Exp).then_inc(e2_ready.sem, 1)

            def batch(b, first=False, last=False):
                heads(b, 0, router=not first)
                for m in range(KT):
                    act.wait_ge(ckv_done.sem, ckv_done.at(b, 1))
                    a.activation(ck_T[:, m], bank[1][:, m * S:(m + 1) * S], ACT.Identity,
                                 bias=cbk_sb[:, m:m + 1]).then_inc(ck_evac.sem, 1)
                if not last:
                    evac_xnT(b + 1, 1, bank[7])
                    evac_q(b + 1, 0)
                evac_xnT(b, 2, bank[6])
                if not last:
                    for f in range(1, 4):
                        evac_q(b + 1, f)
                heads(b, H)
                evac_xnT(b, 4, bank[7])

            evac_xnT(0, 1, bank[7])
            for f in range(4):
                evac_q(0, f)
            batch(0, first=True)
            with act.Fori(1, B - 1) as b:
                batch(b)
            batch(B - 1, last=True)
            evac_xnT(B - 1, 3, bank[3])
            exp_difference(B - 1)

            act.wait_ge(tables.sem, 2)
            act.wait_ge(pads_done.sem, 16 * (E + 1))
            act.wait_ge(scattered.sem, 64 * B)

            act.sem_inc(xt_evac.sem, 1)
            act.sem_inc(ht_evac.sem, 2)
            act.sem_inc(y2_ready.sem, 1)

            def load_tile(i, c):
                j, p = i * 2 + c, c % 2
                r = act.value_load(tile_row[0:1, bass.ds(j, 1)], min_val=0, max_val=E * REGION)
                act.dma_start(xe[p], dispatched[bass.ds(r, P), :]).then_inc(xe_loaded[p].sem, 16)

            def front(j, p):
                act.wait_ge(xt_ready.sem, xt_ready.at(j, 1))
                act.wait_ge(l1_ready.sem, l1_ready.at(j, -4))
                a.copy(xe_T[p], bank[6][:, 0:KT * P]).then_inc(xt_evac.sem, 1)

            def silu(j, p, half):
                act.wait_ge(hb_ready.sem, hb_ready.at(j, 2 * half + 1))
                act.wait_ge(hid_ready.sem, hid_ready.at(j, -2 + half + 1))
                cols = slice(half * 512, (half + 1) * 512)
                a.activation(hsil[:, cols], hb[p][:, cols], ACT.Silu).then_inc(sil_ready.sem, 1)

            def back(j):
                act.wait_ge(tile_done.sem, tile_done.at(j, 0))
                for c in range(2):
                    act.wait_ge(ht_ready.sem, ht_ready.at(j, c + 1))
                    a.copy(hid_T[:, c * 512:(c + 1) * 512], bank[4 + c][:]).then_inc(ht_evac.sem, 1)

            def scale_y(j, p):
                e = act.value_load(tile_e[0:1, bass.ds(j, 1)], min_val=0, max_val=E - 1)
                act.wait_ge(y1_ready.sem, y1_ready.at(j, 1))
                act.wait_ge(tail_copied.sem, tail_copied.at(j, 1))
                act.wait_ge(ids_ready.sem, ids_ready.at(j, 0))
                w = x_norm_T[:].rearrange("p a b -> p (a b)")[:, bass.ds(j * (E + 1) + e, 1)]
                a.mul(y2[p], y1, w).then_inc(y2_ready.sem, 1)

            def step(i, c, next_=True, load=True):
                j, p = i * 2 + c, c % 2
                back(j - 1)
                silu(j, p, 0)
                if next_:
                    front(j + 1, 1 - p)
                silu(j, p, 1)
                if load:
                    act.wait_ge(tail_copied.sem, tail_copied.at(j, 2))
                    load_tile(i, c + 3)
                scale_y(j - 1, 1 - p)

            load_tile(0, 0)
            load_tile(0, 1)
            front(0, 0)
            act.wait_ge(tail_copied.sem, tail_copied.at(0, 1))
            load_tile(0, 2)
            silu(0, 0, 0)
            front(1, 1)
            silu(0, 0, 1)
            act.wait_ge(tail_copied.sem, tail_copied.at(0, 2))
            load_tile(0, 3)
            with act.Fori(0, PAIRED) as i:
                step(i, 1)
                step(i, 2)
            step(PAIRED, 1, load=False)
            step(PAIRED, 2, next_=False, load=False)
            back(NTILE - 1)
            scale_y(NTILE - 1, 0)
            act.wait_ge(xe_loaded[1].sem, xe_loaded[1].at(NTILE // 2, 16))

        @block.vector
        def _(dve):
            v = nc.vector
            dve.sem_inc(masked_ready.sem, 3)
            dve.sem_inc(pt_evac_dve.sem, 4)
            dve.sem_inc(x2_ready.sem, 1)
            dve.sem_inc(rank_used.sem, 1)
            dve.wait_ge(w_in.sem, 16 * NW)
            dve.wait_ge(consts.sem, 21)

            def stats(b, n, src):
                for t in range(T):
                    ins = v.bn_stats(st[:, t], src[:, t])
                ins.then_inc(ln_chain[n - 1].sem, 1)

            def aggregate(b, n):
                dve.wait_ge(ln_chain[n - 1].sem, ln_chain[n - 1].at(b, 1))
                dve.sem_inc(passed.sem, 1)
                for t in range(T):
                    ins = v.bn_aggr(mv[:, t], st[:, t])
                ins.then_inc(ln_chain[n - 1].sem, 1)

            def variance(b, n):
                dve.wait_ge(ln_chain[n - 1].sem, ln_chain[n - 1].at(b, 2))
                v.tensor_scalar(ve[:], mv[:, :, 1], EPS, None, ALU.add).then_inc(var_ready[n - 1].sem, 1)

            def normalise(b, n, src, dst):
                dve.wait_ge(rstd_ready[n - 1].sem, rstd_ready[n - 1].at(b, 1))
                for t in range(T):
                    ins = v.tensor_scalar(dst[:, t, 0:D], src[:, t], mv[:, t, 0:1], rstd[:, t:t + 1],
                                          ALU.subtract, ALU.mult)
                ins.then_inc(xn_ready[n - 1].sem, 1)

            def norm(b, n, src, dst):
                stats(b, n, src)
                aggregate(b, n)
                variance(b, n)
                normalise(b, n, src, dst)

            def evac_k(b, f):
                dve.wait_ge(fill_done.sem, fill_done.at(b, 2 * f + 2))
                v.tensor_copy(k_T[:, 2 * f:2 * f + 2].rearrange("p c s -> p (c s)"),
                              fill_bank(2 * f + 1)[:]).then_inc(kv_evac.sem, 1)

            def evac_v(b, f):
                t, half = divmod(f, 2)
                dve.wait_ge(fill_done.sem, fill_done.at(b, QK_FILLS + f + 1))
                v.tensor_copy(v_sb[:, t, half * 512:(half + 1) * 512], fill_bank(QK_FILLS + f)[:]).then_inc(kv_evac.sem, 1)

            def mask_max(b, u):
                k = u % P_RING
                dve.wait_ge(pt_ready.sem, pt_ready.at(b, u - P_RING + 1))
                dve.wait_ge(scores_ready.sem, scores_ready.at(b, u + 1))
                dve.sem_inc(passed.sem, 1)
                for t in range(T):
                    if u < H:
                        cols, m = (slice(0, P), slice(P, 3 * P))[t], causal
                        ma = m[:, cols]
                    else:
                        cols = slice(t * S, (t + 1) * S)
                        ma = cmask[:, t]
                    ins = v.tensor_tensor_reduce(prob[:, k, cols], bank[u % S_RING][:, cols], ma, 1.0, 3e38,
                                                 ALU.add, ALU.min, nmax[:, k, t:t + 1])
                ins.then_inc(masked_ready.sem, 1)

            def spread(c):
                return c[:].rearrange("p (t e) -> p t e", e=1).broadcast_to((P, T, E))

            def router(b, k):
                rc = router_chain
                ranks = bank[3][:, 2 * E * T:4 * E * T].rearrange("p (a t e) -> p a t e", a=2, t=T)
                if k > 3:
                    dve.wait_ge(rc.sem, rc.at(b, k))
                if k == 0:
                    stats(b, 3, x2)
                elif k == 1:
                    aggregate(b, 3)
                elif k == 2:
                    variance(b, 3)
                elif k == 3:
                    dve.wait_ge(rows_free.sem, rows_free.at(b, 0))
                    normalise(b, 3, x2, rows)
                    dve.sem_inc(rc.sem, 4)
                elif k == 4:
                    dve.wait_ge(logits.sem, logits.at(b, 1))
                    rbb = rb_sb[:].rearrange("p (t e) -> p t e", t=1).broadcast_to((P, T, E))
                    v.tensor_tensor(lg[:], bank[3][:, 0:T * E].rearrange("p (t e) -> p t e", t=T), rbb,
                                    ALU.add).then_inc(rc.sem, 1)
                elif k == 5:
                    v.tensor_reduce(v1[:], lg[:], AX_X, ALU.max).then_inc(rc.sem, 1)
                elif k == 6:
                    v.tensor_tensor(eq[:], lg[:], spread(v1), ALU.is_equal).then_inc(rc.sem, 1)
                elif k == 7:
                    v.tensor_tensor(eq[:], eq[:], rev[:], ALU.mult).then_inc(rc.sem, 1)
                elif k == 8:
                    v.tensor_reduce(mi[:], eq[:], AX_X, ALU.max).then_inc(rc.sem, 1)
                elif k == 9:
                    v.tensor_tensor(oh1[:], rev[:], spread(mi), ALU.is_equal).then_inc(rc.sem, 1)
                elif k == 10:
                    v.scalar_tensor_tensor(lg2[:], oh1[:], -3e38, lg[:], ALU.mult, ALU.add).then_inc(rc.sem, 1)
                elif k == 11:
                    v.tensor_reduce(v2[:], lg2[:], AX_X, ALU.max).then_inc(rc.sem, 1)
                elif k == 12:
                    v.tensor_tensor(eq[:], lg2[:], spread(v2), ALU.is_equal).then_inc(rc.sem, 1)
                elif k == 13:
                    v.tensor_tensor(eq[:], eq[:], rev[:], ALU.mult).then_inc(rc.sem, 1)
                elif k == 14:
                    v.tensor_reduce(mi[:], eq[:], AX_X, ALU.max).then_inc(rc.sem, 1)
                elif k == 15:
                    v.tensor_tensor(oh2[:], rev[:], spread(mi), ALU.is_equal).then_inc(rc.sem, 1)
                elif k == 16:
                    v.tensor_tensor(hot[:], oh1[:], oh2[:], ALU.add).then_inc(hot_ready.sem, 1)
                    v.tensor_tensor(v2[:], v2[:], v1[:], ALU.subtract).then_inc(d_ready.sem, 1)
                    dve.sem_inc(rc.sem, 1)
                elif k == 17:
                    dve.wait_ge(e2_ready.sem, e2_ready.at(b, 1))
                    v.tensor_scalar(pw1[:], e2[:], 1.0, None, ALU.add).then_inc(rc.sem, 1)
                elif k == 18:
                    v.reciprocal(pw1[:], pw1[:]).then_inc(rc.sem, 1)
                elif k == 19:
                    v.tensor_tensor(wa[:], oh1[:], spread(pw1), ALU.mult)
                    v.tensor_tensor(pw2[:], e2[:], pw1[:], ALU.mult).then_inc(rc.sem, 1)
                elif k == 20:
                    v.tensor_copy(rows[:, :, D + E:D + E + 1].bitcast(I32), token[:].rearrange("p (t o) -> p t o", o=1))
                    v.tensor_tensor(eq[:], oh2[:], spread(pw2), ALU.mult).then_inc(rc.sem, 1)
                elif k == 21:
                    v.tensor_tensor(rows[:, :, D:D + E], wa[:], eq[:], ALU.add).then_inc(rc.sem, 1)
                elif k == 22:
                    v.tensor_scalar(token[:], token[:], S, None, ALU.add).then_inc(rows_ready.sem, 1)
                    dve.wait_ge(rank_ready.sem, rank_ready.at(b, 1))
                    runb = run[:].rearrange("p (t e) -> p t e", t=1).broadcast_to((P, T, E))
                    v.tensor_tensor(rank[:], ranks[:, 0], runb, ALU.add).then_inc(rc.sem, 1)
                elif k == 23:
                    v.tensor_tensor(rank[:, 1], ranks[:, 1, 0], rank[:, 1], ALU.add)
                    v.tensor_tensor(run[:], ranks[:, 1, 0], run[:], ALU.add).then_inc(rc.sem, 1)
                elif k == 24:
                    v.tensor_tensor(run[:], ranks[:, 1, 1], run[:], ALU.add).then_inc(rank_used.sem, 1)
                    v.tensor_tensor(rank[:], rank[:], region0[:], ALU.add).then_inc(rc.sem, 1)
                elif k == 25:
                    v.tensor_tensor(wa[:], oh1[:], rank[:], ALU.mult)
                    v.tensor_tensor(eq[:], oh2[:], rank[:], ALU.mult).then_inc(rc.sem, 1)
                elif k == 26:
                    v.tensor_reduce(slotf[:, 0], wa[:], AX_X, ALU.add)
                    v.tensor_reduce(slotf[:, 1], eq[:], AX_X, ALU.add).then_inc(rc.sem, 1)
                elif k == 27:
                    v.tensor_copy(slot_i[:], slotf[:]).then_inc(slots_ready.sem, 1)
                    dve.sem_inc(rc.sem, 1)

            def heads(b, u0, with_router=False):
                for s in range(u0, u0 + H + LAG_T):
                    steps = ROUTER_AT.get(s, ()) if with_router else ()
                    if s < u0 + H:
                        mask_max(b, s)
                    for k in steps[:1]:
                        router(b - 1, k)
                    h = s - 1
                    if u0 == 0 and 0 <= h < H:
                        k = h % P_RING
                        dve.wait_ge(exp_ready.sem, exp_ready.at(b, h + 1))
                        v.reciprocal(r3[:, k, 0:1], psum_[:, k, 0:1])
                        v.reciprocal(r3[:, k, 1:3], psum_[:, k, 1:2].broadcast_to((P, 2))).then_inc(recip_ready.sem, 1)
                    u = s - LAG_T
                    if u0 <= u < u0 + H and u % 4 != 3:
                        n = blocks(u) * P
                        dve.wait_ge(pt_ready.sem, pt_ready.at(b, u + 1))
                        dve.wait_ge(pv_done.sem, pv_done.at(b, u - T_RING + 1))
                        v.tensor_copy(prob_T[:, u % T_RING, 0:n], bank[4 + u % 2][:, 0:n]).then_inc(pt_evac_dve.sem, 1)
                    for k in steps[1:]:
                        router(b - 1, k)

            def batch(b, first=False, last=False):
                heads(b, 0, with_router=not first)
                if not last:
                    dve.wait_ge(x_norm_loaded.sem, x_norm_loaded.at(b + 1, 16))
                    dve.sem_inc(passed.sem, 1)
                    norm(b + 1, 1, x_norm, x_norm)
                dve.wait_ge(x_loaded.sem, x_loaded.at(b, 16))
                dve.wait_ge(attn_out.sem, attn_out.at(b, 1))
                v.tensor_tensor(x1[:].rearrange("p t d -> p (t d)"), bank[7][:],
                                x_in[:].rearrange("p t d -> p (t d)"), ALU.add).then_inc(x1_done.sem, 1)
                dve.wait_ge(x1_done.sem, x1_done.at(b, 1))
                dve.sem_inc(passed.sem, 1)
                norm(b, 2, x1, xn)
                dve.wait_ge(ckv_done.sem, ckv_done.at(b, 2))
                for t in range(T):
                    v.tensor_tensor(cv_sb[:, t, :, 0:CDH],
                                    bank[2][:, t * D:(t + 1) * D].rearrange("p (h c) -> p h c", c=CDH),
                                    cbv_sb[:].rearrange("p (h c) -> p h c", c=CDH), ALU.add).then_inc(cv_evac.sem, 1)
                if not last:
                    evac_k(b + 1, 0)
                dve.wait_ge(cq_done.sem, cq_done.at(b, 1))
                for m in range(KT):
                    v.tensor_scalar(cq_T[:, m], bank[0][:, m * S:(m + 1) * S], cbq_sb[:, m:m + 1],
                                    -float(CDH) ** -0.5, ALU.add, ALU.mult).then_inc(cq_evac.sem, 1)
                if not last:
                    for f in range(1, 4):
                        evac_k(b + 1, f)
                dve.wait_ge(cmask_ready.sem, cmask_ready.at(b, 1))
                heads(b, H)
                for t in range(T):
                    dve.wait_ge(ctx_tr.sem, ctx_tr.at(b, t + 1))
                    o = bank[4 + t][:].rearrange("p (h c) -> p h c", c=32)
                    v.reciprocal(crec[:, t], o[:, :, CDH]).then_inc(crec_ready.sem, 1)
                for t in range(T):
                    dve.wait_ge(crec_ready.sem, crec_ready.at(b, t + 1))
                    o = bank[4 + t][:].rearrange("p (h c) -> p h c", c=32)
                    rc = crec[:, t].rearrange("p (h c) -> p h c", c=1).broadcast_to((P, H, CDH))
                    ins = v.tensor_tensor(ctx_sb[:, t], o[:, :, 0:CDH], rc, ALU.mult)
                ins.then_inc(ctx_ready.sem, 1)
                if not last:
                    for f in range(4):
                        evac_v(b + 1, f)
                dve.wait_ge(cx_out.sem, cx_out.at(b, 1))
                dve.wait_ge(x1b_done.sem, x1b_done.at(b, 1))
                dve.wait_ge(x2_free.sem, x2_free.at(b, 0))
                v.tensor_tensor(x2[:].rearrange("p t d -> p (t d)"), bank[6][:],
                                x1[:].rearrange("p t d -> p (t d)"), ALU.add).then_inc(x2_ready.sem, 1)
                dve.wait_ge(x2_ready.sem, x2_ready.at(b, 1))
                dve.sem_inc(passed.sem, 1)

            dve.wait_ge(x_norm_loaded.sem, x_norm_loaded.at(0, 16))
            norm(0, 1, x_norm, x_norm)
            for f in range(4):
                evac_k(0, f)
            for f in range(4):
                evac_v(0, f)
            batch(0, first=True)
            with dve.Fori(1, B - 1) as b:
                batch(b)
            batch(B - 1, last=True)
            for k in range(ROUTER_STEPS):
                router(B - 1, k)

            table_steps = iter(range(1, 32))

            def step(ins):
                ins.then_inc(table_chain, 1)
                dve.wait_ge(table_chain, next(table_steps))

            dve.wait_ge(rank_used.sem, rank_used.at(B - 1, 1))
            step(v.tensor_copy(cnt_i[:], run[0:1, :]))
            v.sem_inc(tables.sem, 1)
            step(v.tensor_scalar(til_f[:], run[0:1, :], float(P - 1), None, ALU.add))
            step(v.tensor_copy(til_i[:], til_f[:]))
            step(v.tensor_scalar(til_i[:], til_i[:], 7, None, ALU.arith_shift_right))
            step(v.tensor_copy(til_f[:], til_i[:]))
            step(v.tensor_tensor_scan(cum_f[:], one8[:], til_f[:], 0.0, ALU.mult, ALU.add))
            step(v.tensor_copy(cum_i[:], cum_f[:]))
            jb = jj[:].rearrange("p (j e) -> p j e", e=1).broadcast_to((1, NTAB, E))
            cb = cum_f[:].rearrange("p (j e) -> p j e", j=1).broadcast_to((1, NTAB, E))
            tb = til_f[:].rearrange("p (j e) -> p j e", j=1).broadcast_to((1, NTAB, E))
            step(v.tensor_tensor(ge, jb, cb, ALU.is_ge))
            step(v.tensor_tensor(get_, ge, tb, ALU.mult))
            step(v.tensor_reduce(ef[:], ge, AX_X, ALU.add))
            step(v.tensor_reduce(fin_t[:], get_, AX_X, ALU.add))
            step(v.tensor_tensor(loc[:], jj[:], fin_t[:], ALU.subtract))
            step(v.tensor_scalar(lt8[:], ef[:], float(E), float(P), ALU.is_lt, ALU.mult))
            step(v.tensor_tensor(loc[:], loc[:], lt8[:], ALU.mult))
            step(v.scalar_tensor_tensor(rowf[:], ef[:], float(REGION), loc[:], ALU.mult, ALU.add))
            step(v.tensor_copy(tile_row[:], rowf[:]))
            step(v.tensor_scalar(e7[:], ef[:], float(E - 1), None, ALU.min))
            step(v.tensor_copy(tile_e[:], e7[:]))
            step(v.tensor_scalar(tile_slot[:], tile_e[:], 1, None, ALU.bitwise_and))
            v.sem_inc(tables.sem, 1)
            dve.sem_inc(hb_ready.sem, 4)
            dve.sem_inc(hid_ready.sem, 4)
            dve.sem_inc(y1_ready.sem, 1)

            def hidden(j, p):
                e = dve.value_load(tile_e[0:1, bass.ds(j, 1)], min_val=0, max_val=E - 1)
                slot = dve.value_load(tile_slot[0:1, bass.ds(j, 1)], min_val=0, max_val=1)
                dve.wait_ge(b1_loaded.sem, b1_loaded.at(e, 16))
                dve.wait_ge(hid_ready.sem, hid_ready.at(j, -2))
                dve.wait_ge(ht_ready.sem, ht_ready.at(j, -2))
                for n, c in enumerate(L1_ORDER):
                    dve.wait_ge(l1_ready.sem, l1_ready.at(j, n + 1))
                    v.tensor_tensor(hb[p][:, c * 512:(c + 1) * 512], bank[c][:],
                                    b1_ring[:, bass.ds(slot, 1), c * 512:(c + 1) * 512].rearrange("p o n -> p (o n)"),
                                    ALU.add).then_inc(hb_ready.sem, 1)
                    if n % 2 == 1:
                        half = n // 2
                        dve.wait_ge(hb_ready.sem, hb_ready.at(j, n + 1))
                        dve.wait_ge(sil_ready.sem, sil_ready.at(j, half + 1))
                        cols = slice(half * 512, (half + 1) * 512)
                        v.tensor_tensor(hid[p][:, cols], hsil[:, cols], hb[p][:, HID + half * 512:HID + (half + 1) * 512],
                                        ALU.mult).then_inc(hid_ready.sem, 1)

            def bias_y(j):
                slot = dve.value_load(tile_slot[0:1, bass.ds(j, 1)], min_val=0, max_val=1)
                dve.wait_ge(tile_done.sem, tile_done.at(j, 1))
                dve.wait_ge(y2_ready.sem, y2_ready.at(j, 0))
                v.tensor_tensor(y1, bank[7][:, 0:D], b2_ring[:, bass.ds(slot, 1), :].rearrange("p o n -> p (o n)"),
                                ALU.add).then_inc(y1_ready.sem, 1)

            hidden(0, 0)
            with dve.Fori(0, PAIRED + 1) as i:
                hidden(i * 2 + 1, 1)
                bias_y(i * 2)
                hidden(i * 2 + 2, 0)
                bias_y(i * 2 + 1)
            bias_y(NTILE - 1)

        @block.tensor
        def _(pe):
            t_ = nc.tensor
            pe.sem_inc(pt_ready.sem, P_RING)
            pe.sem_inc(pv_done.sem, T_RING)
            pe.sem_inc(tile_done.sem, 1)
            pe.wait_ge(w_in.sem, 16 * NW)
            pe.wait_ge(consts.sem, 21)

            def turn(b, n, src, dst):
                for k in range(KT):
                    for t in range(T):
                        ins = t_.transpose(dst[:, k * S + t * P:k * S + (t + 1) * P], src[:, t, k * P:(k + 1) * P], ident[:])
                ins.then_inc(turned[n - 1].sem, 1)

            def fill(b, n):
                if n >= 6:
                    o = {6: 0, 7: 1, 8: 3, 9: 4, 10: 5, 11: 6}[n]
                    if o % 2 == 0:
                        pe.wait_ge(q_evac.sem, q_evac.at(b, o + 2))
                    else:
                        pe.wait_ge(kv_evac.sem, kv_evac.at(b, (o + 1) // 2))
                bk = fill_bank(n)
                if n < QK_FILLS:
                    f, which = n // 2, n % 2
                    for c in range(2):
                        for k in range(KT):
                            ins = t_.matmul(bk[:, c * S:(c + 1) * S], w_qkv[:, which, k, (2 * f + c) * P:(2 * f + c + 1) * P],
                                            x_norm_T[:, k, :], start=k == 0, stop=k == KT - 1)
                else:
                    t, half = divmod(n - QK_FILLS, 2)
                    for k in range(KT):
                        ins = t_.matmul(bk[:], x_norm_T[:, k, t * P:(t + 1) * P], w_qkv[:, 2, k, half * 512:(half + 1) * 512],
                                        start=k == 0, stop=k == KT - 1)
                ins.then_inc(fill_done.sem, 1)

            def scores(b, u):
                bk = bank[u % S_RING]
                pe.wait_ge(masked_ready.sem, masked_ready.at(b, u - S_RING + 1 if u >= S_RING else 0))
                if u < H:
                    m, par = divmod(u, 2)
                    t_.matmul(bk[:, 0:P], q_pad[:, m, par, 0:P], k_T[:, m, 0:P], start=True, stop=True)
                    t_.matmul(bk[:, P:3 * P], q_pad[:, m, par, P:S], k_T[:, m, :], start=True, stop=True).then_inc(scores_ready.sem, 1)
                else:
                    m, h8 = divmod(u - H, HPC)
                    for t in range(T):
                        ins = t_.matmul(bk[:, t * S:(t + 1) * S], cq_pad[:, m, h8, t * P:(t + 1) * P], ck_T[:, m, :], start=True, stop=True)
                    ins.then_inc(scores_ready.sem, 1)

            def probs_T(b, u):
                wait_evac(pe, b, u - 2)
                if u < H:
                    pe.wait_ge(norm_ready.sem, norm_ready.at(b, u + 1))
                else:
                    pe.wait_ge(exp_ready.sem, exp_ready.at(b, u + 1))
                for c in range(blocks(u)):
                    to = c if u < H else (c % 2) * 2 + c // 2
                    ins = t_.transpose(bank[4 + u % 2][:, to * P:(to + 1) * P], prob[:, u % P_RING, c * P:(c + 1) * P], ident[:])
                ins.then_inc(pt_ready.sem, 1)

            def times_v(b, u):
                wait_evac(pe, b, u - 1)
                wait_evac(pe, b, u)
                pT = [prob_T[:, h % T_RING] for h in (u - 1, u)]
                if u < H:
                    j = u // 2
                    pe.wait_ge(o_evac.sem, o_evac.at(b, j - 1))
                    o = [bank[6 + j % 2][64 * i:64 * i + 64] for i in range(2)]
                    for i, h in enumerate((u - 1, u)):
                        t_.matmul(o[i][:, 0:S], v_sb[:, 0, h * DH:(h + 1) * DH], pT[i][:, 0:S], start=True, stop=False)
                    for i, h in enumerate((u - 1, u)):
                        ins = t_.matmul(o[i][:, P:S], v_sb[:, 1, h * DH:(h + 1) * DH], pT[i][:, S:S + P], start=False, stop=True)
                else:
                    h = u - 1 - H
                    j, c = PAIRS + h // GROUP, h % GROUP
                    if c == 0:
                        pe.wait_ge(o_evac.sem, o_evac.at(b, j - 1))
                    o = [bank[6 + j % 2][32 * (c + i):32 * (c + i) + 32] for i in range(2)]
                    for k in range(T):
                        for i in range(2):
                            ins = t_.matmul(o[i][:, 0:S], cv_sb[:, k, h + i, :], pT[i][:, k * S:(k + 1) * S], start=k == 0, stop=k == T - 1)
                ins.then_inc(pv_done.sem, 2)

            def router_turn(b):
                pe.wait_ge(xn_ready[2].sem, xn_ready[2].at(b, 1))
                turn(b, 3, rows[:, :, 0:D], bank[3])

            def router_logits(b):
                pe.wait_ge(xnT_ready[2].sem, xnT_ready[2].at(b, 1))
                for t in range(T):
                    for k in range(KT):
                        ins = t_.matmul(bank[3][:, t * E:(t + 1) * E], xnT[:, k, t * P:(t + 1) * P], rw_sb[:, k, :],
                                        start=k == 0, stop=k == KT - 1)
                ins.then_inc(logits.sem, 1)

            def router_rank(b):
                pe.wait_ge(hot_ready.sem, hot_ready.at(b, 1))
                hot2 = hot[:].rearrange("p t e -> p (t e)")
                t_.matmul(bank[3][:, 2 * T * E:3 * T * E], before[:], hot2, start=True, stop=True)
                t_.matmul(bank[3][:, 3 * T * E:4 * T * E], ones[:], hot2, start=True, stop=True).then_inc(rank_ready.sem, 1)

            def heads(b, u0, router=False):
                for s in range(u0, u0 + H + LAG_V):
                    if s < u0 + H:
                        scores(b, s)
                    if router and s == TURN_AT:
                        router_turn(b - 1)
                    if router and s == LOGITS_AT:
                        router_logits(b - 1)
                    if router and s == RANK_AT:
                        router_rank(b - 1)
                    if u0 <= s - LAG_T < u0 + H:
                        probs_T(b, s - LAG_T)
                    if u0 <= s - LAG_V < u0 + H and (s - LAG_V) % 2 == 1:
                        times_v(b, s - LAG_V)

            def batch(b, first=False, last=False):
                pe.wait_ge(kv_evac.sem, kv_evac.at(b, 8))
                pe.wait_ge(x2_ready.sem, x2_ready.at(b, 0))
                heads(b, 0, router=not first)
                pe.wait_ge(o_evac.sem, o_evac.at(b, PAIRS))
                for t in range(T):
                    for m in range(PAIRS):
                        ins = t_.matmul(bank[7][:, t * D:(t + 1) * D], z_T[:, m, t * P:(t + 1) * P], wo_sb[:, m, :],
                                        start=m == 0, stop=m == PAIRS - 1)
                ins.then_inc(attn_out.sem, 1)
                pe.wait_ge(ctx_loaded.sem, ctx_loaded.at(b, 16))
                for m in range(KT):
                    for k in range(KT):
                        ins = t_.matmul(bank[1][:, m * S:(m + 1) * S], cw[:, 1, k, m * P:(m + 1) * P], ctxT_in[:, k, :],
                                        start=k == 0, stop=k == KT - 1)
                ins.then_inc(ckv_done.sem, 1)
                for t in range(T):
                    for k in range(KT):
                        ins = t_.matmul(bank[2][:, t * D:(t + 1) * D], ctxT_in[:, k, t * P:(t + 1) * P], cw[:, 2, k, :],
                                        start=k == 0, stop=k == KT - 1)
                ins.then_inc(ckv_done.sem, 1)
                if not last:
                    pe.wait_ge(xn_ready[0].sem, xn_ready[0].at(b + 1, 1))
                    pe.wait_ge(x1_done.sem, x1_done.at(b, 1))
                    turn(b + 1, 1, x_norm, bank[7])
                    pe.wait_ge(xnT_ready[0].sem, xnT_ready[0].at(b + 1, 1))
                    pe.wait_ge(rank_used.sem, rank_used.at(b, 0))
                    fill(b + 1, 0)
                pe.wait_ge(xn_ready[1].sem, xn_ready[1].at(b, 1))
                turn(b, 2, xn, bank[6])
                if not last:
                    fill(b + 1, 1)
                pe.wait_ge(xnT_ready[1].sem, xnT_ready[1].at(b, 1))
                for m in range(KT):
                    for k in range(KT):
                        ins = t_.matmul(bank[0][:, m * S:(m + 1) * S], cw[:, 0, k, m * P:(m + 1) * P], xnT[:, k, :],
                                        start=k == 0, stop=k == KT - 1)
                ins.then_inc(cq_done.sem, 1)
                if not last:
                    fill(b + 1, 2)
                pe.wait_ge(cq_evac.sem, cq_evac.at(b, 2))
                pe.wait_ge(ck_evac.sem, ck_evac.at(b, 2))
                pe.wait_ge(cv_evac.sem, cv_evac.at(b, 2))
                if not last:
                    for n in range(3, QK_FILLS):
                        fill(b + 1, n)
                    pe.wait_ge(q_evac.sem, q_evac.at(b + 1, 8))
                    pe.wait_ge(kv_evac.sem, kv_evac.at(b + 1, 4))
                pe.wait_ge(cq_spread.sem, cq_spread.at(b, 16 * HPC))
                heads(b, H)
                pe.wait_ge(o_evac.sem, o_evac.at(b, PAIRS + H // GROUP))
                for t in range(T):
                    for g in range(H // GROUP):
                        ins = t_.transpose(bank[4 + t][:, g * P:(g + 1) * P], o_T[:, g, t * P:(t + 1) * P], ident[:])
                    ins.then_inc(ctx_tr.sem, 1)
                if not last:
                    pe.wait_ge(masked_ready.sem, masked_ready.at(b, U))
                    fill(b + 1, 8)
                    fill(b + 1, 9)
                pe.wait_ge(ctx_ready.sem, ctx_ready.at(b, 1))
                turn(b, 4, ctx_sb[:].rearrange("p t h c -> p t (h c)"), bank[7])
                if not last:
                    fill(b + 1, 10)
                    fill(b + 1, 11)
                pe.wait_ge(xnT_ready[3].sem, xnT_ready[3].at(b, 1))
                for t in range(T):
                    for k in range(KT):
                        ins = t_.matmul(bank[6][:, t * D:(t + 1) * D], xnT[:, k, t * P:(t + 1) * P], cw[:, 3, k, :],
                                        start=k == 0, stop=k == KT - 1)
                ins.then_inc(cx_out.sem, 1)

            pe.wait_ge(xn_ready[0].sem, xn_ready[0].at(0, 1))
            turn(0, 1, x_norm, bank[7])
            pe.wait_ge(xnT_ready[0].sem, xnT_ready[0].at(0, 1))
            for n in range(FILLS):
                fill(0, n)
            batch(0, first=True)
            with pe.Fori(1, B - 1) as b:
                batch(b)
            batch(B - 1, last=True)
            router_turn(B - 1)
            router_logits(B - 1)
            router_rank(B - 1)

            pe.sem_inc(l1_ready.sem, 8)
            pe.sem_inc(ht_ready.sem, 4)
            pe.wait_ge(tables.sem, 2)

            def turn_x(i, c):
                j, p = i * 2 + c, c % 2
                pe.wait_ge(xe_loaded[p].sem, xe_loaded[p].at(i, 16 * (c // 2 + 1)))
                pe.wait_ge(xt_evac.sem, xt_evac.at(j, 0))
                for k in range(KT):
                    ins = t_.transpose(bank[6][:, k * P:(k + 1) * P], xe[p][:, k * P:(k + 1) * P], ident[:])
                ins.then_inc(xt_ready.sem, 1)

            def layer1(j, p, slot, n):
                c = L1_ORDER[n]
                pe.wait_ge(hb_ready.sem, hb_ready.at(j, -4 + n + 1))
                for k in range(KT):
                    ins = t_.matmul(bank[c][:], xe_T[p][:, k * P:(k + 1) * P],
                                    w1_ring[:, bass.ds(slot, 1), k * 2 * HID + c * 512:k * 2 * HID + (c + 1) * 512].rearrange("p o n -> p (o n)"),
                                    start=k == 0, stop=k == KT - 1)
                ins.then_inc(l1_ready.sem, 1)

            def turn_h(j, p):
                for c in range(2):
                    pe.wait_ge(hid_ready.sem, hid_ready.at(j, c + 1))
                    pe.wait_ge(ht_evac.sem, ht_evac.at(j, -2 + c + 1))
                    for q in range(4):
                        k = 4 * c + q
                        ins = t_.transpose(bank[4 + c][:, q * P:(q + 1) * P], hid[p][:, k * P:(k + 1) * P], ident[:])
                    ins.then_inc(ht_ready.sem, 1)

            def layer2(j):
                slot = pe.value_load(tile_slot[0:1, bass.ds(j, 1)], min_val=0, max_val=1)
                pe.wait_ge(y1_ready.sem, y1_ready.at(j, 0))
                for k in range(8):
                    if k % 4 == 0:
                        pe.wait_ge(ht_evac.sem, ht_evac.at(j, k // 4 + 1))
                    ins = t_.matmul(bank[7][:, 0:D], hid_T[:, k * P:(k + 1) * P],
                                    w2_ring[:, bass.ds(slot, 1), k * D:(k + 1) * D].rearrange("p o n -> p (o n)"),
                                    start=k == 0, stop=k == 7)
                ins.then_inc(tile_done.sem, 1)

            def step(i, c, prev=True, next_=True):
                j, p = i * 2 + c, c % 2
                e = pe.value_load(tile_e[0:1, bass.ds(j, 1)], min_val=0, max_val=E - 1)
                slot = pe.value_load(tile_slot[0:1, bass.ds(j, 1)], min_val=0, max_val=1)
                pe.wait_ge(w_loaded.sem, w_loaded.at(e, 48))
                pe.wait_ge(xt_evac.sem, xt_evac.at(j, 1))
                layer1(j, p, slot, 0)
                if prev:
                    turn_h(j - 1, 1 - p)
                layer1(j, p, slot, 1)
                if next_:
                    turn_x(i, c + 1)
                layer1(j, p, slot, 2)
                layer1(j, p, slot, 3)
                if prev:
                    layer2(j - 1)

            turn_x(0, 0)
            step(0, 0, prev=False)
            with pe.Fori(0, PAIRED) as i:
                step(i, 1)
                step(i, 2)
            step(PAIRED, 1)
            step(PAIRED, 2, next_=False)
            turn_h(NTILE - 1, 0)
            layer2(NTILE - 1)


def kernel(**inputs):
    import numpy as _np
    import concourse.bacc as _bacc
    from concourse import mybir as _mybir
    from concourse.bass_utils import run_bass_kernel_spmd as _run

    a = {k.replace("L0_", ""): _np.asarray(v) for k, v in inputs.items()}

    def by_rows(w, lead=()):
        *_, r, n = w.shape
        w = w.reshape(*w.shape[:-2], r // 128, 128, n)
        return _np.ascontiguousarray(_np.swapaxes(w, -3, -2))

    arrays = {
        "x": by_rows(a["x"]),
        "ctx_t": by_rows(_np.swapaxes(a["ctx_1024"], 1, 2)),
        "mask": by_rows(a["mask_BxSxS2_bk1"]),
        "wq": by_rows(a["attn_W_Q"].reshape(1024, 256).T),
        "wk": by_rows(a["attn_W_K"].reshape(1024, 256).T),
        "wv": by_rows(a["attn_W_V"].reshape(1024, 256).T),
        "wo": by_rows(a["attn_W_O"].T),
        "cwq": by_rows(a["xattn_wq"].T),
        "cwk": by_rows(a["xattn_wk"].T),
        "cwv": by_rows(a["xattn_wv"].T),
        "cwo": by_rows(a["xattn_wo"].T),
        "cbq": _np.ascontiguousarray(a["xattn_bq"].reshape(2, 128).T),
        "cbk": _np.ascontiguousarray(a["xattn_bk"].reshape(2, 128).T),
        "cbv": a["xattn_bv"].reshape(1, 256),
        "cbo": a["xattn_bo"].reshape(1, 256),
        "rw": by_rows(a["ffn_router_w"].T),
        "rb": a["ffn_router_b"].reshape(1, 8),
        "w1": by_rows(_np.swapaxes(a["ffn_w1"], 1, 2)).reshape(8, 128, -1),
        "b1": a["ffn_b1"],
        "w2": by_rows(_np.swapaxes(a["ffn_w2"], 1, 2)).reshape(8, 128, -1),
        "b2": a["ffn_b2"],
    }
    nc = _bacc.Bacc("TRN2", target_bir_lowering=False, num_devices=1)
    args = [nc.dram_tensor(f"in_{n}_dram", v.shape, _mybir.dt.from_np(v.dtype), kind="ExternalInput").ap()
            for n, v in arrays.items()]
    out = nc.dram_tensor("out_0_dram", (TOK + P, D), F32, kind="ExternalOutput").ap()
    build(nc, *args, out)
    r = _run(nc, [{f"in_{n}_dram": v for n, v in arrays.items()}], core_ids=[0])
    return r.results[0]["out_0_dram"][:TOK].reshape(B, S, D)
```

```python
from contextlib import ExitStack

import concourse.bass as bass
from concourse import mybir

F32 = mybir.dt.float32
F32R = mybir.dt.float32r
BF16 = mybir.dt.bfloat16
I32 = mybir.dt.int32
U8 = mybir.dt.uint8
ALU = mybir.AluOpType
ACT = mybir.ActivationFunctionType
AX_X = mybir.AxisListType.X

P = 128
B, S, D = 8, 256, 256
T = S // P
KT = D // P
H, DH = 16, 64
PAIRS = H // 2
CDH = D // H
HPC = P // CDH
GROUP = 4
E, HID = 8, 1024
TOK = B * S
EPS = 1e-5
BIG = 1e30
XBIG = 1e20
REGION = TOK + P
NTILE = 2 * TOK // P + E - 1
NTAB = NTILE + 1
PAIRED = (NTILE - 3) // 2
L1_ORDER = (0, 2, 1, 3)
ROW = D + E + 1
PARTS = ((0, 0), (0, 1), (1, 0))
U = 2 * H
S_RING, P_RING = 3, 4
T_RING = 4
QK_FILLS, FILLS = 8, 12
FILL_BANK = (3, 4, 5, 0, 1, 2, 3, 1, 2, 0, 3, 5)
ROUTER_AT = {0: (0, 1), 1: (2,), 2: (3,), 7: (4, 5), 8: (6, 7), 9: (8, 9), 10: (10, 11), 11: (12, 13),
             12: (14, 15, 16), 14: (17, 18), 15: (19, 20), 16: (21, 22), 17: (23, 24), 18: (25, 26, 27)}
ROUTER_STEPS = 28
RSTD_AT, TURN_AT, EVAC_AT, LOGITS_AT, EXP_AT, RANK_AT = 0, 4, 4, 6, 13, 15
LAG_T, LAG_V = 3, 5


class Signal:

    def __init__(self, sem, per, off=0):
        self.sem, self.per, self.off = sem, per, off

    def at(self, b, n):
        return b * self.per + (n + self.off)


def build(nc, x, ctx_t, mask, wq, wk, wv, wo, cwq, cwk, cwv, cwo, cbq, cbk, cbv, cbo,
          rw, rb, w1, b1, w2, b2, out):
    stack = ExitStack()
    with stack:
        def sb(name, shape, dt=F32):
            return stack.enter_context(nc.sbuf_tensor(name, shape, dt))

        def sig(name, per, off=0):
            return Signal(stack.enter_context(nc.semaphore(name)), per, off)

        bank = [stack.enter_context(nc.psum_tensor(f"bank{i}", [P, 512], F32)) for i in range(8)]
        dispatched = nc.dram_tensor("dispatched", [E * REGION + P, ROW], F32).ap()

        w_qkv = sb("w_qkv", [P, 3, KT, H * DH])
        wo_sb = sb("wo_sb", [P, PAIRS, D])
        cw = sb("cw", [P, 4, KT, D])
        cbq_sb = sb("cbq_sb", [P, KT])
        cbk_sb = sb("cbk_sb", [P, KT])
        cbv_sb = sb("cbv_sb", [P, D])
        cbo_sb = sb("cbo_sb", [P, D])
        rw_sb = sb("rw_sb", [P, KT, E])
        rb_sb = sb("rb_sb", [P, E])
        ident = sb("ident", [P, P])
        causal = sb("causal", [P, 3 * P])
        before = sb("before", [P, P], BF16)
        ones = sb("ones", [P, P], BF16)
        neg_half = sb("neg_half", [P, T])
        rev = sb("rev", [P, T, E])
        region0 = sb("region0", [P, T, E])
        token = sb("token", [P, T], I32)
        pad_rows = sb("pad_rows", [P, ROW])

        x_in = sb("x_in", [P, T, D])
        x_norm = sb("x_norm", [P, T, D])
        x_norm_T = sb("x_norm_T", [P, 2, KT, S], F32R)
        ctxT_in = sb("ctxT_in", [P, KT, S])
        mask_in = sb("mask_in", [P, T, S], U8)
        cmask = sb("cmask", [P, T, S])
        xn = sb("xn", [P, T, D])
        xnT = sb("xnT", [P, KT, S])
        q_pad = sb("q_pad", [P, PAIRS, 2, S])
        k_T = sb("k_T", [P, PAIRS, S])
        v_sb = sb("v_sb", [P, T, H * DH])
        z_T = sb("z_T", [P, PAIRS, S])
        x1 = sb("x1", [P, T, D])
        cq_T = sb("cq_T", [P, KT, S])
        cq_pad = sb("cq_pad", [P, KT, HPC, S])
        ck_T = sb("ck_T", [P, KT, S])
        cv_sb = sb("cv_sb", [P, T, H, 32])
        o_T = sb("o_T", [P, H // GROUP, S])
        ctx_sb = sb("ctx_sb", [P, T, H, CDH])
        crec = sb("crec", [P, T, H])
        x2 = sb("x2", [P, T, D])
        rows = sb("rows", [P, T, ROW])
        st = sb("st", [P, T, 6])
        mv = sb("mv", [P, T, 2])
        ve = sb("ve", [P, T])
        rstd = sb("rstd", [P, T])
        nmax = sb("nmax", [P, P_RING, 2])
        psum_ = sb("psum_", [P, P_RING, 2])
        recip = sb("recip", [P, P_RING, 2])
        lg = sb("lg", [P, T, E])
        lg2 = sb("lg2", [P, T, E])
        eq = sb("eq", [P, T, E])
        oh1 = sb("oh1", [P, T, E])
        oh2 = sb("oh2", [P, T, E])
        wa = sb("wa", [P, T, E])
        hot = sb("hot", [P, T, E], BF16)
        v1 = sb("v1", [P, T])
        v2 = sb("v2", [P, T])
        mi = sb("mi", [P, T])
        e2 = sb("e2", [P, T])
        pw1 = sb("pw1", [P, T])
        pw2 = sb("pw2", [P, T])
        run = sb("run", [P, E])
        rank = sb("rank", [P, T, E])
        slotf = sb("slotf", [P, 2, T])
        slot_i = sb("slot_i", [P, 2, T], I32)

        b2_ring = sb("b2_ring", [P, 2, D])
        with ExitStack() as attention:
            w_split, prob, prob_T = (attention.enter_context(nc.sbuf_tensor(name, shape, dt)) for name, shape, dt in (
                ("w_split", [P, 2, 3, KT * H * DH], F32R),
                ("prob", [P, P_RING, 512], F32), ("prob_T", [P, T_RING, 512], F32)))
        w1_ring = sb("w1_ring", [P, 2, KT * 2 * HID])
        w2_ring = sb("w2_ring", [P, 2, (HID // P) * D])
        arena2 = sb("arena2", [P, 4096])
        b1_ring = cq_pad[:].rearrange("p k h s -> p (k h s)").rearrange("p (r n) -> p r n", r=2)
        arena = w_qkv[:].rearrange("p a k n -> p (a k n)")
        hb = [arena[:, 2048 * i:2048 * (i + 1)] for i in range(2)]
        hsil = arena[:, 4096:5120]
        xe_T = [arena[:, 5120 + 256 * i:5376 + 256 * i] for i in range(2)]
        hid = [arena2[:, 1024 * i:1024 * (i + 1)] for i in range(2)]
        hid_T = arena2[:, 2048:3072]
        y1 = arena2[:, 3072:3328]
        y2 = [arena2[:, 3328 + 256 * i:3584 + 256 * i] for i in range(2)]
        xe = [buf[:].rearrange("p a b -> p (a b)")[:, 0:ROW] for buf in (ctxT_in, x_in)]
        tails = xnT[:].rearrange("p a b -> p (a b)")[:, 0:NTAB * (E + 1)].rearrange("p (j e) -> p j e", j=NTAB)
        ids = sb("ids", [P, 1], I32)

        cnt_i = sb("cnt_i", [1, E], I32)
        til_i = sb("til_i", [1, E], I32)
        til_f = sb("til_f", [1, E])
        one8 = sb("one8", [1, E])
        cum_f = sb("cum_f", [1, E])
        cum_i = sb("cum_i", [1, E], I32)
        jj = sb("jj", [1, NTAB])
        ge, get_ = (v_sb[0:1, i, 0:NTAB * E].rearrange("p (j e) -> p j e", j=NTAB) for i in range(2))
        ef = sb("ef", [1, NTAB])
        fin_t = sb("fin_t", [1, NTAB])
        lt8 = sb("lt8", [1, NTAB])
        loc = sb("loc", [1, NTAB])
        e7 = sb("e7", [1, NTAB])
        rowf = sb("rowf", [1, NTAB])
        tile_e = sb("tile_e", [1, NTAB], I32)
        tile_slot = sb("tile_slot", [1, NTAB], I32)
        tile_row = sb("tile_row", [1, NTAB], I32)

        qk_in = sig("qk_in", 0)
        v_in = sig("v_in", 0)
        w_in = sig("w_in", 0)
        ident_ready = sig("ident_ready", 0)
        q_zeroed = sig("q_zeroed", 0)
        w_high = sig("w_high", 0)
        w_low = sig("w_low", 0)
        consts = sig("consts", 0)
        passed = sig("passed", 0)
        x_loaded = sig("x_loaded", 16)
        x_norm_loaded = sig("x_norm_loaded", 16)
        ctx_loaded = sig("ctx_loaded", 16)
        mask_loaded = sig("mask_loaded", 16)
        ln_chain = [sig(f"ln{i}_chain", 2) for i in (1, 2, 3)]
        var_ready = [sig(f"var{i}_ready", 1) for i in (1, 2, 3)]
        rstd_ready = [sig(f"rstd{i}_ready", 1) for i in (1, 2, 3)]
        xn_ready = [sig(f"xn{i}_ready", 1) for i in (1, 2, 3)]
        turned = [sig(f"turned{i}", 1) for i in (1, 2, 3)] + [sig("ctx_turned", 1)]
        xnT_ready = [sig(f"xn{i}T_ready", 1) for i in (1, 2, 3)] + [sig("ctxT_ready", 1)]
        x_norm_low = sig("x_norm_low", 1)
        fill_done = sig("fill_done", FILLS)
        q_evac = sig("q_evac", 8)
        kv_evac = sig("kv_evac", 8)
        scores_ready = sig("scores_ready", U)
        masked_ready = sig("masked_ready", U, 3)
        exp_ready = sig("exp_ready", U)
        recip_ready = sig("recip_ready", H)
        norm_ready = sig("norm_ready", H)
        pt_ready = sig("pt_ready", U, P_RING)
        pt_evac_act = sig("pt_evac_act", U // 4, 4)
        pt_evac_dve = sig("pt_evac_dve", U - U // 4, 4)
        pv_done = sig("pv_done", U, T_RING)
        o_evac = sig("o_evac", PAIRS + H // GROUP, 2)
        attn_out = sig("attn_out", 1)
        x1_done = sig("x1_done", 1)
        x1b_done = sig("x1b_done", 1)
        ckv_done = sig("ckv_done", 2)
        ck_evac = sig("ck_evac", 2)
        cv_evac = sig("cv_evac", 2)
        cq_done = sig("cq_done", 1)
        cq_evac = sig("cq_evac", 2)
        cq_spread = [sig(f"cq_spread{h8}", 16) for h8 in range(HPC)]
        cmask_ready = sig("cmask_ready", 1)
        ctx_tr = sig("ctx_tr", 2)
        crec_ready = sig("crec_ready", 2)
        ctx_ready = sig("ctx_ready", 1)
        cx_out = sig("cx_out", 1)
        x2_ready = sig("x2_ready", 1, 1)
        x2_stored = sig("x2_stored", 16)
        x2_free = sig("x2_free", 1, 1)
        rows_free = sig("rows_free", 1, 1)
        router_chain = sig("router_chain", ROUTER_STEPS)
        logits = sig("logits", 1)
        d_ready = sig("d_ready", 1)
        e2_ready = sig("e2_ready", 1)
        hot_ready = sig("hot_ready", 1)
        rank_ready = sig("rank_ready", 1)
        rank_used = sig("rank_used", 1, 1)
        slots_ready = sig("slots_ready", 1)
        rows_ready = sig("rows_ready", 1)
        scattered = sig("scattered", 64)
        tables = sig("tables", 0)
        table_chain = stack.enter_context(nc.semaphore("table_chain"))
        pads_done = sig("pads_done", 0)
        w_loaded = sig("w_loaded", 48)
        b1_loaded = sig("b1_loaded", 16)
        tile_done = sig("tile_done", 1, 1)
        xe_loaded = [sig(f"xe_loaded{i}", 16) for i in range(2)]
        tail_copied = sig("tail_copied", 1)
        xt_ready = sig("xt_ready", 1)
        xt_evac = sig("xt_evac", 1, 1)
        l1_ready = sig("l1_ready", 4, 8)
        hb_ready = sig("hb_ready", 4, 4)
        sil_ready = sig("sil_ready", 2)
        hid_ready = sig("hid_ready", 2, 4)
        ht_ready = sig("ht_ready", 2, 4)
        ht_evac = sig("ht_evac", 2, 2)
        y1_ready = sig("y1_ready", 1, 1)
        y2_ready = sig("y2_ready", 1, 1)
        ids_ready = sig("ids_ready", 1, 1)
        added = sig("added", 16)

        NW = 12

        def evacs(u):
            return (u + 1) // 4, u + 1 - (u + 1) // 4

        def wait_evac(eng, b, u):
            if u % 4 == 3:
                eng.wait_ge(pt_evac_act.sem, pt_evac_act.at(b, evacs(u)[0]))
            else:
                eng.wait_ge(pt_evac_dve.sem, pt_evac_dve.at(b, evacs(u)[1]))

        def blocks(u):
            return 3 if u < H else 4

        def before_ring(u, ring):
            return u - ring + 1 if u % H >= ring else u - u % H

        def fill_bank(n):
            return bank[FILL_BANK[n]]

        block = stack.enter_context(nc.Block())

        @block.sync
        def _(sp):
            sp.sem_inc(x2_free.sem, 1)
            sp.dma_start(x_norm[:], x[0]).then_inc(x_norm_loaded.sem, 16)
            sp.dma_start(w_qkv[:, 0], wq).then_inc(qk_in.sem, 16)
            sp.dma_start(w_qkv[:, 1], wk).then_inc(qk_in.sem, 16)
            sp.dma_start(w_qkv[:, 2], wv).then_inc(v_in.sem, 16)
            sp.dma_start(wo_sb[:], wo).then_inc(w_in.sem, 16)
            for i, w in enumerate((cwq, cwk, cwv, cwo)):
                sp.dma_start(cw[:, i], w).then_inc(w_in.sem, 16)
            sp.dma_start(cbq_sb[:], cbq).then_inc(w_in.sem, 16)
            sp.dma_start(cbk_sb[:], cbk).then_inc(w_in.sem, 16)
            sp.dma_start(cbv_sb[:], cbv.broadcast_to((P, D))).then_inc(w_in.sem, 16)
            sp.dma_start(cbo_sb[:], cbo.broadcast_to((P, D))).then_inc(w_in.sem, 16)
            sp.dma_start(rw_sb[:], rw).then_inc(w_in.sem, 16)
            sp.dma_start(rb_sb[:], rb.broadcast_to((P, E))).then_inc(w_in.sem, 16)
            sp.wait_ge(consts.sem, 9)
            sp.dma_start(out[TOK:TOK + P, :], pad_rows[:, 0:D]).then_inc(w_in.sem, 16)
            sp.dma_start(dispatched[E * REGION:E * REGION + P, :], pad_rows[:]).then_inc(pads_done.sem, 16)

            def load_w(e):
                slot = e % 2
                sp.dma_start(w1_ring[:, bass.ds(slot, 1), :], w1[bass.ds(e, 1)].rearrange("e p n -> p e n")).then_inc(w_loaded.sem, 16)
                sp.dma_start(w2_ring[:, bass.ds(slot, 1), :], w2[bass.ds(e, 1)].rearrange("e p n -> p e n")).then_inc(w_loaded.sem, 16)
                sp.dma_start(b2_ring[:, bass.ds(slot, 1), :],
                             b2[bass.ds(e, 1), :].rearrange("e n -> () e n").broadcast_to((P, 1, D))).then_inc(w_loaded.sem, 16)

            def load_b1(e):
                sp.dma_start(b1_ring[:, bass.ds(e % 2, 1), :],
                             b1[bass.ds(e, 1), :].rearrange("e n -> () e n").broadcast_to((P, 1, 2 * HID))).then_inc(b1_loaded.sem, 16)

            def came(e):
                sp.wait_ge(w_loaded.sem, w_loaded.at(e, 48))
                sp.sem_inc(passed.sem, 1)
                sp.wait_ge(b1_loaded.sem, b1_loaded.at(e, 16))
                sp.sem_inc(passed.sem, 1)

            sp.dma_start(x_in[:], x[0]).then_inc(x_loaded.sem, 16)
            sp.dma_start(ctxT_in[:], ctx_t[0]).then_inc(ctx_loaded.sem, 16)
            sp.dma_start(mask_in[:], mask[0]).then_inc(mask_loaded.sem, 16)
            def batch(b, last=False):
                if not last:
                    sp.wait_ge(turned[0].sem, turned[0].at(b, 1))
                    sp.dma_start(x_norm[:], x[b + 1]).then_inc(x_norm_loaded.sem, 16)
                    sp.wait_ge(x1_done.sem, x1_done.at(b, 1))
                    sp.dma_start(x_in[:], x[b + 1]).then_inc(x_loaded.sem, 16)
                    sp.wait_ge(ckv_done.sem, ckv_done.at(b, 2))
                    sp.dma_start(ctxT_in[:], ctx_t[b + 1]).then_inc(ctx_loaded.sem, 16)
                sp.wait_ge(cq_evac.sem, cq_evac.at(b, 2))
                for h8 in range(HPC):
                    r = slice(h8 * CDH, (h8 + 1) * CDH)
                    sp.dma_start(cq_pad[r, :, h8, :], cq_T[r, :, :]).then_inc(cq_spread[h8].sem, 16)
                if not last:
                    sp.wait_ge(cmask_ready.sem, cmask_ready.at(b, 1))
                    sp.dma_start(mask_in[:], mask[b + 1]).then_inc(mask_loaded.sem, 16)
                else:
                    load_w(0)
                sp.wait_ge(x2_ready.sem, x2_ready.at(b, 1))
                sp.dma_start(out[bass.ds(b * S, S), :].rearrange("(t p) d -> p t d", p=P), x2[:]).then_inc(x2_stored.sem, 16)
                sp.wait_ge(x2_stored.sem, x2_stored.at(b, 16))
                sp.sem_inc(x2_free.sem, 1)

            with sp.Fori(0, B - 1) as b:
                batch(b)
            batch(B - 1, last=True)

            load_b1(0)
            sp.wait_ge(tables.sem, 1)
            with sp.Fori(0, E // 2) as e:
                n = sp.value_load(cnt_i[0:1, bass.ds(e, 1)], min_val=0, max_val=TOK)
                sp.dma_start(dispatched[bass.ds(e * REGION + n, P), :], pad_rows[:]).then_inc(pads_done.sem, 16)
            came(0)
            sp.wait_ge(xt_ready.sem, 1)
            load_w(1)
            load_b1(1)
            sp.wait_ge(tables.sem, 2)
            with sp.Fori(2, E) as e:
                n = sp.value_load(cum_i[0:1, bass.ds(e - 2, 1)], min_val=0, max_val=NTILE)
                sp.wait_ge(y1_ready.sem, n + 1)
                came(e - 1)
                load_w(e)
                load_b1(e)
            came(E - 1)

        @block.gpsimd
        def _(pool):
            g = nc.gpsimd
            g.memset(ident[:], 0.0).then_inc(ident_ready.sem, 1)
            g.memset(neg_half[:], -0.5).then_inc(ident_ready.sem, 1)
            pool.wait_ge(ident_ready.sem, 2)
            g.affine_select(out=ident[:], in_=ident[:], compare_op=ALU.not_equal, fill=1.0, base=0,
                            pattern=[[-1, P]], channel_multiplier=1).then_inc(ident_ready.sem, 1)
            g.memset(q_pad[:], 0.0).then_inc(q_zeroed.sem, 1)

            def rsqrt(b, n):
                pool.wait_ge(var_ready[n - 1].sem, var_ready[n - 1].at(b, 1))
                g.tensor_tensor(rstd[:], ve[:], neg_half[:], ALU.pow).then_inc(rstd_ready[n - 1].sem, 1)

            rsqrt(0, 1)
            g.memset(causal[:], 0.0).then_inc(consts.sem, 1)
            g.memset(before[:], 1.0).then_inc(consts.sem, 1)
            g.memset(ones[:], 1.0).then_inc(consts.sem, 1)
            g.memset(pad_rows[:], 0.0).then_inc(consts.sem, 1)
            g.iota(token[:], [[P, T]], base=0, channel_multiplier=1).then_inc(consts.sem, 1)
            pool.wait_ge(consts.sem, 5)
            for c in (0, 2):
                g.affine_select(out=causal[:, c * P:(c + 1) * P], in_=causal[:, c * P:(c + 1) * P],
                                compare_op=ALU.is_ge, fill=BIG, base=0, pattern=[[-1, P]],
                                channel_multiplier=1).then_inc(consts.sem, 1)
            g.affine_select(out=before[:], in_=before[:], compare_op=ALU.is_gt, fill=0.0, base=0,
                            pattern=[[1, P]], channel_multiplier=-1).then_inc(consts.sem, 1)
            g.iota(pad_rows[:, D + E:D + E + 1].bitcast(I32), [[0, 1]], base=TOK, channel_multiplier=1).then_inc(consts.sem, 1)
            g.iota(rev[:], [[0, T], [-1, E]], base=E, channel_multiplier=0,
                   allow_small_or_imprecise_dtypes=True).then_inc(consts.sem, 1)
            g.iota(region0[:], [[0, T], [REGION, E]], base=0, channel_multiplier=0,
                   allow_small_or_imprecise_dtypes=True).then_inc(consts.sem, 1)
            g.memset(cq_pad[:], 0.0).then_inc(consts.sem, 1)
            g.memset(cv_sb[:], 0.0).then_inc(consts.sem, 1)
            g.memset(run[:], 0.0).then_inc(consts.sem, 1)
            pool.wait_ge(consts.sem, 14)
            g.memset(cv_sb[:, :, :, CDH:CDH + 1], 1.0).then_inc(consts.sem, 1)
            g.iota(jj[:], [[1, NTAB]], base=0, channel_multiplier=0,
                   allow_small_or_imprecise_dtypes=True).then_inc(consts.sem, 1)
            g.memset(one8[:], 1.0).then_inc(consts.sem, 1)
            pool.sem_inc(rows_free.sem, 1)
            pool.wait_ge(w_in.sem, 16 * NW)

            def scatter(b):
                pool.wait_ge(rows_ready.sem, rows_ready.at(b, 1))
                pool.wait_ge(slots_ready.sem, slots_ready.at(b, 1))
                pool.sem_inc(passed.sem, 1)
                for k in range(2):
                    for t in range(T):
                        g.indirect_dma_start(dispatched[:, :], bass.IndirectOffsetOnAxis(ap=slot_i[:, k, t:t + 1], axis=0),
                                             rows[:, t, :], None).then_inc(scattered.sem, 16)

            def batch(b, first=False, last=False):
                for h in range(H):
                    k = h % P_RING
                    pool.wait_ge(recip_ready.sem, recip_ready.at(b, h + 1))
                    for t, cols in enumerate((slice(0, P), slice(P, 3 * P))):
                        ins = g.tensor_tensor(prob[:, k, cols], prob[:, k, cols],
                                              recip[:, k, t:t + 1].broadcast_to((P, (t + 1) * P)), ALU.mult)
                    ins.then_inc(norm_ready.sem, 1)
                    if h == RSTD_AT and not first:
                        rsqrt(b - 1, 3)
                if not last:
                    rsqrt(b + 1, 1)
                if not first:
                    scatter(b - 1)
                rsqrt(b, 2)
                pool.wait_ge(xn_ready[1].sem, xn_ready[1].at(b, 1))
                for t in range(T):
                    ins = g.tensor_tensor(x1[:, t], x1[:, t], cbo_sb[:], ALU.add)
                ins.then_inc(x1b_done.sem, 1)
                pool.wait_ge(mask_loaded.sem, mask_loaded.at(b, 16))
                pool.sem_inc(passed.sem, 1)
                g.tensor_scalar(cmask[:], mask_in[:], XBIG, None, ALU.mult).then_inc(cmask_ready.sem, 1)
                if not first:
                    pool.wait_ge(scattered.sem, scattered.at(b - 1, 64))
                    pool.sem_inc(rows_free.sem, 1)

            batch(0, first=True)
            with pool.Fori(1, B - 1) as b:
                batch(b)
            batch(B - 1, last=True)
            rsqrt(B - 1, 3)
            scatter(B - 1)

            pool.wait_ge(x2_stored.sem, 16 * B)

            pool.sem_inc(ids_ready.sem, 1)

            def copy_tail(i, c):
                pool.wait_ge(xe_loaded[c % 2].sem, xe_loaded[c % 2].at(i, 16 * (c // 2 + 1)))
                g.tensor_copy(tails[:, bass.ds(i * 2 + c, 1), :].rearrange("p o n -> p (o n)").bitcast(I32),
                              xe[c % 2][:, D:ROW].bitcast(I32)).then_inc(tail_copied.sem, 1)

            def add_out(j, p, first=False):
                if not first:
                    pool.wait_ge(added.sem, added.at(j, 0))
                    pool.sem_inc(passed.sem, 1)
                pool.wait_ge(tail_copied.sem, tail_copied.at(j, 1))
                g.tensor_copy(ids[:], tails[:, bass.ds(j, 1), E:E + 1].rearrange("p o n -> p (o n)").bitcast(I32)).then_inc(ids_ready.sem, 1)
                pool.wait_ge(y2_ready.sem, y2_ready.at(j, 1))
                pool.sem_inc(passed.sem, 1)
                pool.wait_ge(ids_ready.sem, ids_ready.at(j, 1))
                pool.sem_inc(passed.sem, 1)
                g.indirect_dma_start(out[:, :], bass.IndirectOffsetOnAxis(ap=ids[:], axis=0),
                                     y2[p], None, compute_op=ALU.add).then_inc(added.sem, 16)

            copy_tail(0, 0)
            copy_tail(0, 1)
            copy_tail(0, 2)
            add_out(0, 0, first=True)
            with pool.Fori(0, PAIRED) as i:
                copy_tail(i, 3)
                add_out(i * 2 + 1, 1)
                copy_tail(i, 4)
                add_out(i * 2 + 2, 0)
            add_out(NTILE - 2, 1)
            add_out(NTILE - 1, 0)
            pool.wait_ge(added.sem, 16 * NTILE)

        @block.scalar
        def _(act):
            a = nc.scalar
            act.sem_inc(o_evac.sem, 2)
            act.sem_inc(pt_evac_act.sem, 4)

            def evac_xnT(b, n, src):
                act.wait_ge(turned[n - 1].sem, turned[n - 1].at(b, 1))
                dst = x_norm_T[:, 0] if n == 1 else xnT[:]
                a.copy(dst.rearrange("p k s -> p (k s)"), src[:]).then_inc(xnT_ready[n - 1].sem, 1)

            def evac_q(b, f):
                act.wait_ge(fill_done.sem, fill_done.at(b, 2 * f + 1))
                src = fill_bank(2 * f)[:].rearrange("p (c s) -> p c s", c=2)
                for par in range(2):
                    r = slice(64 * par, 64 * par + 64)
                    a.mul(q_pad[r, 2 * f:2 * f + 2, par, :], src[r], -float(DH) ** -0.5).then_inc(q_evac.sem, 1)

            def exps(b, u):
                k = u % H % P_RING
                act.wait_ge(masked_ready.sem, masked_ready.at(b, u + 1))
                w = P if u < H else S
                for t in range(T):
                    lo = t * w
                    hi = lo + w if u >= H else (t + 1) * (t + 2) // 2 * P
                    pr = prob[:, k, lo:hi]
                    if u < H:
                        ins = a.activation(pr, pr, ACT.Exp, bias=nmax[:, k, t:t + 1], scale=-1.0,
                                           accum_out=psum_[:, k, t:t + 1])
                    else:
                        ins = a.activation(pr, pr, ACT.Exp, bias=nmax[:, k, t:t + 1], scale=-1.0)
                ins.then_inc(exp_ready.sem, 1)

            def evac_pt(b, u):
                n = blocks(u) * P
                act.wait_ge(pt_ready.sem, pt_ready.at(b, u + 1))
                act.wait_ge(pv_done.sem, pv_done.at(b, before_ring(u, T_RING)))
                a.copy(prob_T[:, u % H % T_RING, 0:n], bank[4 + u % 2][:, 0:n]).then_inc(pt_evac_act.sem, 1)

            def heads(b, u0, router=False, last=False):
                for s in range(u0, u0 + H + LAG_V + 1):
                    if s < u0 + H:
                        exps(b, s)
                    if u0 == H and s == H + 2 and not last:
                        evac_q(b + 1, 3)
                    if router and s == EVAC_AT:
                        evac_xnT(b - 1, 3, bank[3])
                    if router and s == EXP_AT:
                        exp_difference(b - 1)
                    u = s - LAG_T
                    if u0 <= u < u0 + H and u % 4 == 3:
                        evac_pt(b, u)
                    u = s - LAG_V - 1
                    if u >= u0 and u0 < H and u % 2 == 1:
                        act.wait_ge(pv_done.sem, pv_done.at(b, u + 1))
                        j = u // 2
                        a.copy(z_T[:, j], bank[6 + j % 2][:, 0:S]).then_inc(o_evac.sem, 1)
                    if u >= u0 and u0 >= H and u % GROUP == GROUP - 1:
                        act.wait_ge(pv_done.sem, pv_done.at(b, u + 1))
                        j = PAIRS + (u - H) // GROUP
                        a.copy(o_T[:, j - PAIRS], bank[6 + j % 2][:, 0:S]).then_inc(o_evac.sem, 1)

            def exp_difference(b):
                act.wait_ge(d_ready.sem, d_ready.at(b, 1))
                a.activation(e2[:], v2[:], ACT.Exp).then_inc(e2_ready.sem, 1)

            def batch(b, first=False, last=False):
                heads(b, 0, router=not first)
                if not last:
                    evac_xnT(b + 1, 1, bank[6])
                for m in range(KT):
                    act.wait_ge(ckv_done.sem, ckv_done.at(b, 1))
                    a.activation(ck_T[:, m], bank[1][:, m * S:(m + 1) * S], ACT.Identity,
                                 bias=cbk_sb[:, m:m + 1]).then_inc(ck_evac.sem, 1)
                if not last:
                    evac_q(b + 1, 0)
                evac_xnT(b, 2, bank[7])
                if not last:
                    for f in range(1, 3):
                        evac_q(b + 1, f)
                heads(b, H, last=last)
                evac_xnT(b, 4, bank[7])

            def split_high(i):
                a.copy(w_split[:, 0, i], w_qkv[:, i].rearrange("p k n -> p (k n)")).then_inc(w_high.sem, 1)

            act.wait_ge(qk_in.sem, 32)
            split_high(0)
            split_high(1)
            evac_xnT(0, 1, bank[7])
            act.wait_ge(v_in.sem, 16)
            split_high(2)
            act.wait_ge(q_zeroed.sem, 1)
            for f in range(4):
                evac_q(0, f)
            act.wait_ge(w_in.sem, 16 * NW)
            act.wait_ge(consts.sem, 17)
            batch(0, first=True)
            with act.Fori(1, B - 1) as b:
                batch(b)
            batch(B - 1, last=True)
            evac_xnT(B - 1, 3, bank[3])
            exp_difference(B - 1)

            act.wait_ge(tables.sem, 1)
            with act.Fori(E // 2, E) as e:
                n = act.value_load(cnt_i[0:1, bass.ds(e, 1)], min_val=0, max_val=TOK)
                act.dma_start(dispatched[bass.ds(e * REGION + n, P), :], pad_rows[:]).then_inc(pads_done.sem, 16)
            act.wait_ge(tables.sem, 2)
            act.wait_ge(pads_done.sem, 16 * (E + 1))
            act.wait_ge(scattered.sem, 64 * B)

            act.sem_inc(xt_evac.sem, 1)
            act.sem_inc(ht_evac.sem, 2)
            act.sem_inc(y2_ready.sem, 1)

            def load_tile(i, c):
                j, p = i * 2 + c, c % 2
                r = act.value_load(tile_row[0:1, bass.ds(j, 1)], min_val=0, max_val=E * REGION)
                act.dma_start(xe[p], dispatched[bass.ds(r, P), :]).then_inc(xe_loaded[p].sem, 16)

            def front(j, p):
                act.wait_ge(xt_ready.sem, xt_ready.at(j, 1))
                act.wait_ge(l1_ready.sem, l1_ready.at(j, -4))
                a.copy(xe_T[p], bank[6][:, 0:KT * P]).then_inc(xt_evac.sem, 1)

            def silu(j, p, half):
                act.wait_ge(hb_ready.sem, hb_ready.at(j, 2 * half + 1))
                act.wait_ge(hid_ready.sem, hid_ready.at(j, -2 + half + 1))
                cols = slice(half * 512, (half + 1) * 512)
                a.activation(hsil[:, cols], hb[p][:, cols], ACT.Silu).then_inc(sil_ready.sem, 1)

            def back(j):
                act.wait_ge(tile_done.sem, tile_done.at(j, 0))
                for c in range(2):
                    act.wait_ge(ht_ready.sem, ht_ready.at(j, c + 1))
                    a.copy(hid_T[:, c * 512:(c + 1) * 512], bank[4 + c][:]).then_inc(ht_evac.sem, 1)

            def scale_y(j, p):
                e = act.value_load(tile_e[0:1, bass.ds(j, 1)], min_val=0, max_val=E - 1)
                act.wait_ge(y1_ready.sem, y1_ready.at(j, 1))
                act.wait_ge(tail_copied.sem, tail_copied.at(j, 1))
                act.wait_ge(ids_ready.sem, ids_ready.at(j, 0))
                w = xnT[:].rearrange("p a b -> p (a b)")[:, bass.ds(j * (E + 1) + e, 1)]
                a.mul(y2[p], y1, w).then_inc(y2_ready.sem, 1)

            def step(i, c, next_=True, load=True):
                j, p = i * 2 + c, c % 2
                back(j - 1)
                silu(j, p, 0)
                if next_:
                    front(j + 1, 1 - p)
                silu(j, p, 1)
                if load:
                    act.wait_ge(tail_copied.sem, tail_copied.at(j, 2))
                    load_tile(i, c + 3)
                scale_y(j - 1, 1 - p)

            load_tile(0, 0)
            load_tile(0, 1)
            front(0, 0)
            act.wait_ge(tail_copied.sem, tail_copied.at(0, 1))
            load_tile(0, 2)
            silu(0, 0, 0)
            front(1, 1)
            silu(0, 0, 1)
            act.wait_ge(tail_copied.sem, tail_copied.at(0, 2))
            load_tile(0, 3)
            with act.Fori(0, PAIRED) as i:
                step(i, 1)
                step(i, 2)
            step(PAIRED, 1, load=False)
            step(PAIRED, 2, next_=False, load=False)
            back(NTILE - 1)
            scale_y(NTILE - 1, 0)
            act.wait_ge(xe_loaded[1].sem, xe_loaded[1].at(NTILE // 2, 16))

        @block.vector
        def _(dve):
            v = nc.vector
            dve.sem_inc(masked_ready.sem, 3)
            dve.sem_inc(pt_evac_dve.sem, 4)
            dve.sem_inc(x2_ready.sem, 1)
            dve.sem_inc(rank_used.sem, 1)

            def stats(b, n, src):
                for t in range(T):
                    ins = v.bn_stats(st[:, t], src[:, t])
                ins.then_inc(ln_chain[n - 1].sem, 1)

            def aggregate(b, n):
                dve.wait_ge(ln_chain[n - 1].sem, ln_chain[n - 1].at(b, 1))
                dve.sem_inc(passed.sem, 1)
                for t in range(T):
                    ins = v.bn_aggr(mv[:, t], st[:, t])
                ins.then_inc(ln_chain[n - 1].sem, 1)

            def variance(b, n):
                dve.wait_ge(ln_chain[n - 1].sem, ln_chain[n - 1].at(b, 2))
                v.tensor_scalar(ve[:], mv[:, :, 1], EPS, None, ALU.add).then_inc(var_ready[n - 1].sem, 1)

            def normalise(b, n, src, dst):
                dve.wait_ge(rstd_ready[n - 1].sem, rstd_ready[n - 1].at(b, 1))
                for t in range(T):
                    ins = v.tensor_scalar(dst[:, t, 0:D], src[:, t], mv[:, t, 0:1], rstd[:, t:t + 1],
                                          ALU.subtract, ALU.mult)
                ins.then_inc(xn_ready[n - 1].sem, 1)

            def norm(b, n, src, dst):
                stats(b, n, src)
                aggregate(b, n)
                variance(b, n)
                normalise(b, n, src, dst)

            def low_x(b, src):
                dve.wait_ge(xnT_ready[0].sem, xnT_ready[0].at(b, 1))
                v.tensor_tensor(x_norm_T[:, 1].rearrange("p k s -> p (k s)"), src[:],
                                x_norm_T[:, 0].rearrange("p k s -> p (k s)").bitcast(F32), ALU.subtract).then_inc(x_norm_low.sem, 1)

            def split_low(i):
                dve.wait_ge(w_high.sem, i + 1)
                v.tensor_tensor(w_split[:, 1, i], w_qkv[:, i].rearrange("p k n -> p (k n)"),
                                w_split[:, 0, i].bitcast(F32), ALU.subtract).then_inc(w_low.sem, 1)

            def evac_k(b, f):
                dve.wait_ge(fill_done.sem, fill_done.at(b, 2 * f + 2))
                v.tensor_copy(k_T[:, 2 * f:2 * f + 2].rearrange("p c s -> p (c s)"),
                              fill_bank(2 * f + 1)[:]).then_inc(kv_evac.sem, 1)

            def evac_v(b, f):
                t, half = divmod(f, 2)
                dve.wait_ge(fill_done.sem, fill_done.at(b, QK_FILLS + f + 1))
                v.tensor_copy(v_sb[:, t, half * 512:(half + 1) * 512], fill_bank(QK_FILLS + f)[:]).then_inc(kv_evac.sem, 1)

            def mask_max(b, u):
                k = u % H % P_RING
                dve.wait_ge(pt_ready.sem, pt_ready.at(b, before_ring(u, P_RING)))
                dve.wait_ge(scores_ready.sem, scores_ready.at(b, u + 1))
                dve.sem_inc(passed.sem, 1)
                for t in range(T):
                    if u < H:
                        cols, m = (slice(0, P), slice(P, 3 * P))[t], causal
                        ma = m[:, cols]
                    else:
                        cols = slice(t * S, (t + 1) * S)
                        ma = cmask[:, t]
                    ins = v.tensor_tensor_reduce(prob[:, k, cols], bank[u % H % S_RING][:, cols], ma, 1.0, 3e38,
                                                 ALU.add, ALU.min, nmax[:, k, t:t + 1])
                ins.then_inc(masked_ready.sem, 1)

            def spread(c):
                return c[:].rearrange("p (t e) -> p t e", e=1).broadcast_to((P, T, E))

            def router(b, k):
                rc = router_chain
                ranks = bank[3][:, 2 * E * T:4 * E * T].rearrange("p (a t e) -> p a t e", a=2, t=T)
                if k > 3:
                    dve.wait_ge(rc.sem, rc.at(b, k))
                if k == 0:
                    stats(b, 3, x2)
                elif k == 1:
                    aggregate(b, 3)
                elif k == 2:
                    variance(b, 3)
                elif k == 3:
                    dve.wait_ge(rows_free.sem, rows_free.at(b, 0))
                    normalise(b, 3, x2, rows)
                    dve.sem_inc(rc.sem, 4)
                elif k == 4:
                    dve.wait_ge(logits.sem, logits.at(b, 1))
                    rbb = rb_sb[:].rearrange("p (t e) -> p t e", t=1).broadcast_to((P, T, E))
                    v.tensor_tensor(lg[:], bank[3][:, 0:T * E].rearrange("p (t e) -> p t e", t=T), rbb,
                                    ALU.add).then_inc(rc.sem, 1)
                elif k == 5:
                    v.tensor_reduce(v1[:], lg[:], AX_X, ALU.max).then_inc(rc.sem, 1)
                elif k == 6:
                    v.tensor_tensor(eq[:], lg[:], spread(v1), ALU.is_equal).then_inc(rc.sem, 1)
                elif k == 7:
                    v.tensor_tensor(eq[:], eq[:], rev[:], ALU.mult).then_inc(rc.sem, 1)
                elif k == 8:
                    v.tensor_reduce(mi[:], eq[:], AX_X, ALU.max).then_inc(rc.sem, 1)
                elif k == 9:
                    v.tensor_tensor(oh1[:], rev[:], spread(mi), ALU.is_equal).then_inc(rc.sem, 1)
                elif k == 10:
                    v.scalar_tensor_tensor(lg2[:], oh1[:], -3e38, lg[:], ALU.mult, ALU.add).then_inc(rc.sem, 1)
                elif k == 11:
                    v.tensor_reduce(v2[:], lg2[:], AX_X, ALU.max).then_inc(rc.sem, 1)
                elif k == 12:
                    v.tensor_tensor(eq[:], lg2[:], spread(v2), ALU.is_equal).then_inc(rc.sem, 1)
                elif k == 13:
                    v.tensor_tensor(eq[:], eq[:], rev[:], ALU.mult).then_inc(rc.sem, 1)
                elif k == 14:
                    v.tensor_reduce(mi[:], eq[:], AX_X, ALU.max).then_inc(rc.sem, 1)
                elif k == 15:
                    v.tensor_tensor(oh2[:], rev[:], spread(mi), ALU.is_equal).then_inc(rc.sem, 1)
                elif k == 16:
                    v.tensor_tensor(hot[:], oh1[:], oh2[:], ALU.add).then_inc(hot_ready.sem, 1)
                    v.tensor_tensor(v2[:], v2[:], v1[:], ALU.subtract).then_inc(d_ready.sem, 1)
                    dve.sem_inc(rc.sem, 1)
                elif k == 17:
                    dve.wait_ge(e2_ready.sem, e2_ready.at(b, 1))
                    v.tensor_scalar(pw1[:], e2[:], 1.0, None, ALU.add).then_inc(rc.sem, 1)
                elif k == 18:
                    v.reciprocal(pw1[:], pw1[:]).then_inc(rc.sem, 1)
                elif k == 19:
                    v.tensor_tensor(wa[:], oh1[:], spread(pw1), ALU.mult)
                    v.tensor_tensor(pw2[:], e2[:], pw1[:], ALU.mult).then_inc(rc.sem, 1)
                elif k == 20:
                    v.tensor_copy(rows[:, :, D + E:D + E + 1].bitcast(I32), token[:].rearrange("p (t o) -> p t o", o=1))
                    v.tensor_tensor(eq[:], oh2[:], spread(pw2), ALU.mult).then_inc(rc.sem, 1)
                elif k == 21:
                    v.tensor_tensor(rows[:, :, D:D + E], wa[:], eq[:], ALU.add).then_inc(rc.sem, 1)
                elif k == 22:
                    v.tensor_scalar(token[:], token[:], S, None, ALU.add).then_inc(rows_ready.sem, 1)
                    dve.wait_ge(rank_ready.sem, rank_ready.at(b, 1))
                    runb = run[:].rearrange("p (t e) -> p t e", t=1).broadcast_to((P, T, E))
                    v.tensor_tensor(rank[:], ranks[:, 0], runb, ALU.add).then_inc(rc.sem, 1)
                elif k == 23:
                    v.tensor_tensor(rank[:, 1], ranks[:, 1, 0], rank[:, 1], ALU.add)
                    v.tensor_tensor(run[:], ranks[:, 1, 0], run[:], ALU.add).then_inc(rc.sem, 1)
                elif k == 24:
                    v.tensor_tensor(run[:], ranks[:, 1, 1], run[:], ALU.add).then_inc(rank_used.sem, 1)
                    v.tensor_tensor(rank[:], rank[:], region0[:], ALU.add).then_inc(rc.sem, 1)
                elif k == 25:
                    v.tensor_tensor(wa[:], oh1[:], rank[:], ALU.mult)
                    v.tensor_tensor(eq[:], oh2[:], rank[:], ALU.mult).then_inc(rc.sem, 1)
                elif k == 26:
                    v.tensor_reduce(slotf[:, 0], wa[:], AX_X, ALU.add)
                    v.tensor_reduce(slotf[:, 1], eq[:], AX_X, ALU.add).then_inc(rc.sem, 1)
                elif k == 27:
                    v.tensor_copy(slot_i[:], slotf[:]).then_inc(slots_ready.sem, 1)
                    dve.sem_inc(rc.sem, 1)

            def heads(b, u0, with_router=False, last=False):
                for s in range(u0, u0 + H + LAG_T):
                    steps = ROUTER_AT.get(s, ()) if with_router else ()
                    if s < u0 + H:
                        mask_max(b, s)
                    if s == 2:
                        evac_v(b, 3)
                    if s == 2 * H + 1 and not last:
                        evac_k(b + 1, 3)
                    for k in steps[:1]:
                        router(b - 1, k)
                    h = s - 1
                    if u0 == 0 and 0 <= h < H:
                        k = h % H % P_RING
                        dve.wait_ge(exp_ready.sem, exp_ready.at(b, h + 1))
                        v.reciprocal(recip[:, k], psum_[:, k]).then_inc(recip_ready.sem, 1)
                    u = s - LAG_T
                    if u0 <= u < u0 + H and u % 4 != 3:
                        n = blocks(u) * P
                        dve.wait_ge(pt_ready.sem, pt_ready.at(b, u + 1))
                        dve.wait_ge(pv_done.sem, pv_done.at(b, before_ring(u, T_RING)))
                        v.tensor_copy(prob_T[:, u % H % T_RING, 0:n], bank[4 + u % 2][:, 0:n]).then_inc(pt_evac_dve.sem, 1)
                    for k in steps[1:]:
                        router(b - 1, k)

            def batch(b, first=False, last=False):
                heads(b, 0, with_router=not first)
                if not last:
                    dve.wait_ge(x_norm_loaded.sem, x_norm_loaded.at(b + 1, 16))
                    dve.sem_inc(passed.sem, 1)
                    norm(b + 1, 1, x_norm, x_norm)
                dve.wait_ge(x_loaded.sem, x_loaded.at(b, 16))
                dve.wait_ge(attn_out.sem, attn_out.at(b, 1))
                v.tensor_tensor(x1[:].rearrange("p t d -> p (t d)"), bank[0][:],
                                x_in[:].rearrange("p t d -> p (t d)"), ALU.add).then_inc(x1_done.sem, 1)
                dve.wait_ge(x1_done.sem, x1_done.at(b, 1))
                dve.sem_inc(passed.sem, 1)
                stats(b, 2, x1)
                aggregate(b, 2)
                variance(b, 2)
                if not last:
                    low_x(b + 1, bank[6])
                normalise(b, 2, x1, xn)
                dve.wait_ge(ckv_done.sem, ckv_done.at(b, 2))
                for t in range(T):
                    v.tensor_tensor(cv_sb[:, t, :, 0:CDH],
                                    bank[2][:, t * D:(t + 1) * D].rearrange("p (h c) -> p h c", c=CDH),
                                    cbv_sb[:].rearrange("p (h c) -> p h c", c=CDH), ALU.add).then_inc(cv_evac.sem, 1)
                if not last:
                    evac_k(b + 1, 0)
                dve.wait_ge(cq_done.sem, cq_done.at(b, 1))
                for m in range(KT):
                    v.tensor_scalar(cq_T[:, m], bank[0][:, m * S:(m + 1) * S], cbq_sb[:, m:m + 1],
                                    -float(CDH) ** -0.5, ALU.add, ALU.mult).then_inc(cq_evac.sem, 1)
                if not last:
                    for f in range(1, 3):
                        evac_k(b + 1, f)
                dve.wait_ge(cmask_ready.sem, cmask_ready.at(b, 1))
                heads(b, H, last=last)
                if not last:
                    evac_v(b + 1, 0)
                for t in range(T):
                    dve.wait_ge(ctx_tr.sem, ctx_tr.at(b, t + 1))
                    o = bank[4 + t][:].rearrange("p (h c) -> p h c", c=32)
                    v.reciprocal(crec[:, t], o[:, :, CDH]).then_inc(crec_ready.sem, 1)
                for t in range(T):
                    dve.wait_ge(crec_ready.sem, crec_ready.at(b, t + 1))
                    o = bank[4 + t][:].rearrange("p (h c) -> p h c", c=32)
                    rc = crec[:, t].rearrange("p (h c) -> p h c", c=1).broadcast_to((P, H, CDH))
                    ins = v.tensor_tensor(ctx_sb[:, t], o[:, :, 0:CDH], rc, ALU.mult)
                ins.then_inc(ctx_ready.sem, 1)
                if not last:
                    evac_v(b + 1, 1)
                    evac_v(b + 1, 2)
                dve.wait_ge(cx_out.sem, cx_out.at(b, 1))
                dve.wait_ge(x1b_done.sem, x1b_done.at(b, 1))
                dve.wait_ge(x2_free.sem, x2_free.at(b, 0))
                v.tensor_tensor(x2[:].rearrange("p t d -> p (t d)"), bank[6][:],
                                x1[:].rearrange("p t d -> p (t d)"), ALU.add).then_inc(x2_ready.sem, 1)
                dve.wait_ge(x2_ready.sem, x2_ready.at(b, 1))
                dve.sem_inc(passed.sem, 1)

            dve.wait_ge(x_norm_loaded.sem, x_norm_loaded.at(0, 16))
            norm(0, 1, x_norm, x_norm)
            split_low(0)
            split_low(1)
            low_x(0, bank[7])
            split_low(2)
            for f in range(4):
                evac_k(0, f)
            for f in range(3):
                evac_v(0, f)
            dve.wait_ge(w_in.sem, 16 * NW)
            dve.wait_ge(consts.sem, 17)
            batch(0, first=True)
            with dve.Fori(1, B - 1) as b:
                batch(b)
            batch(B - 1, last=True)
            for k in range(ROUTER_STEPS):
                router(B - 1, k)

            table_steps = iter(range(1, 32))

            def step(ins):
                ins.then_inc(table_chain, 1)
                dve.wait_ge(table_chain, next(table_steps))

            dve.wait_ge(rank_used.sem, rank_used.at(B - 1, 1))
            step(v.tensor_copy(cnt_i[:], run[0:1, :]))
            v.sem_inc(tables.sem, 1)
            step(v.tensor_scalar(til_f[:], run[0:1, :], float(P - 1), None, ALU.add))
            step(v.tensor_copy(til_i[:], til_f[:]))
            step(v.tensor_scalar(til_i[:], til_i[:], 7, None, ALU.arith_shift_right))
            step(v.tensor_copy(til_f[:], til_i[:]))
            step(v.tensor_tensor_scan(cum_f[:], one8[:], til_f[:], 0.0, ALU.mult, ALU.add))
            step(v.tensor_copy(cum_i[:], cum_f[:]))
            jb = jj[:].rearrange("p (j e) -> p j e", e=1).broadcast_to((1, NTAB, E))
            cb = cum_f[:].rearrange("p (j e) -> p j e", j=1).broadcast_to((1, NTAB, E))
            tb = til_f[:].rearrange("p (j e) -> p j e", j=1).broadcast_to((1, NTAB, E))
            step(v.tensor_tensor(ge, jb, cb, ALU.is_ge))
            step(v.tensor_tensor(get_, ge, tb, ALU.mult))
            step(v.tensor_reduce(ef[:], ge, AX_X, ALU.add))
            step(v.tensor_reduce(fin_t[:], get_, AX_X, ALU.add))
            step(v.tensor_tensor(loc[:], jj[:], fin_t[:], ALU.subtract))
            step(v.tensor_scalar(lt8[:], ef[:], float(E), float(P), ALU.is_lt, ALU.mult))
            step(v.tensor_tensor(loc[:], loc[:], lt8[:], ALU.mult))
            step(v.scalar_tensor_tensor(rowf[:], ef[:], float(REGION), loc[:], ALU.mult, ALU.add))
            step(v.tensor_copy(tile_row[:], rowf[:]))
            step(v.tensor_scalar(e7[:], ef[:], float(E - 1), None, ALU.min))
            step(v.tensor_copy(tile_e[:], e7[:]))
            step(v.tensor_scalar(tile_slot[:], tile_e[:], 1, None, ALU.bitwise_and))
            v.sem_inc(tables.sem, 1)
            dve.sem_inc(hb_ready.sem, 4)
            dve.sem_inc(hid_ready.sem, 4)
            dve.sem_inc(y1_ready.sem, 1)

            def hidden(j, p):
                e = dve.value_load(tile_e[0:1, bass.ds(j, 1)], min_val=0, max_val=E - 1)
                slot = dve.value_load(tile_slot[0:1, bass.ds(j, 1)], min_val=0, max_val=1)
                dve.wait_ge(b1_loaded.sem, b1_loaded.at(e, 16))
                dve.wait_ge(hid_ready.sem, hid_ready.at(j, -2))
                dve.wait_ge(ht_ready.sem, ht_ready.at(j, -2))
                for n, c in enumerate(L1_ORDER):
                    dve.wait_ge(l1_ready.sem, l1_ready.at(j, n + 1))
                    v.tensor_tensor(hb[p][:, c * 512:(c + 1) * 512], bank[c][:],
                                    b1_ring[:, bass.ds(slot, 1), c * 512:(c + 1) * 512].rearrange("p o n -> p (o n)"),
                                    ALU.add).then_inc(hb_ready.sem, 1)
                    if n % 2 == 1:
                        half = n // 2
                        dve.wait_ge(hb_ready.sem, hb_ready.at(j, n + 1))
                        dve.wait_ge(sil_ready.sem, sil_ready.at(j, half + 1))
                        cols = slice(half * 512, (half + 1) * 512)
                        v.tensor_tensor(hid[p][:, cols], hsil[:, cols], hb[p][:, HID + half * 512:HID + (half + 1) * 512],
                                        ALU.mult).then_inc(hid_ready.sem, 1)

            def bias_y(j):
                slot = dve.value_load(tile_slot[0:1, bass.ds(j, 1)], min_val=0, max_val=1)
                dve.wait_ge(tile_done.sem, tile_done.at(j, 1))
                dve.wait_ge(y2_ready.sem, y2_ready.at(j, 0))
                v.tensor_tensor(y1, bank[7][:, 0:D], b2_ring[:, bass.ds(slot, 1), :].rearrange("p o n -> p (o n)"),
                                ALU.add).then_inc(y1_ready.sem, 1)

            hidden(0, 0)
            with dve.Fori(0, PAIRED + 1) as i:
                hidden(i * 2 + 1, 1)
                bias_y(i * 2)
                hidden(i * 2 + 2, 0)
                bias_y(i * 2 + 1)
            bias_y(NTILE - 1)

        @block.tensor
        def _(pe):
            t_ = nc.tensor
            pe.sem_inc(pt_ready.sem, P_RING)
            pe.sem_inc(pv_done.sem, T_RING)
            pe.sem_inc(tile_done.sem, 1)

            def turn(b, n, src, dst):
                for k in range(KT):
                    for t in range(T):
                        ins = t_.transpose(dst[:, k * S + t * P:k * S + (t + 1) * P], src[:, t, k * P:(k + 1) * P], ident[:])
                ins.then_inc(turned[n - 1].sem, 1)

            def fill(b, n):
                if n >= 6:
                    o = max(m for m in range(n) if FILL_BANK[m] == FILL_BANK[n])
                    if o % 2 == 0:
                        pe.wait_ge(q_evac.sem, q_evac.at(b, o + 2))
                    else:
                        pe.wait_ge(kv_evac.sem, kv_evac.at(b, (o + 1) // 2))
                bk = fill_bank(n)
                if n < QK_FILLS:
                    f, which = n // 2, n % 2
                    for c in range(2):
                        for k in range(KT):
                            for w_part, x_part in PARTS:
                                at = k * H * DH + (2 * f + c) * P
                                ins = t_.matmul(bk[:, c * S:(c + 1) * S], w_split[:, w_part, which, at:at + P], x_norm_T[:, x_part, k, :],
                                                start=k == 0 and w_part == x_part, stop=k == KT - 1 and w_part == 1)
                else:
                    t, half = divmod(n - QK_FILLS, 2)
                    for k in range(KT):
                        for x_part, w_part in PARTS:
                            at = k * H * DH + half * 512
                            ins = t_.matmul(bk[:], x_norm_T[:, x_part, k, t * P:(t + 1) * P], w_split[:, w_part, 2, at:at + 512],
                                            start=k == 0 and w_part == x_part, stop=k == KT - 1 and x_part == 1)
                ins.then_inc(fill_done.sem, 1)

            def scores(b, u):
                bk = bank[u % H % S_RING]
                pe.wait_ge(masked_ready.sem, masked_ready.at(b, before_ring(u, S_RING)))
                if u < H:
                    m, par = divmod(u, 2)
                    t_.matmul(bk[:, 0:P], q_pad[:, m, par, 0:P], k_T[:, m, 0:P], start=True, stop=True)
                    t_.matmul(bk[:, P:3 * P], q_pad[:, m, par, P:S], k_T[:, m, :], start=True, stop=True).then_inc(scores_ready.sem, 1)
                else:
                    m, h8 = divmod(u - H, HPC)
                    if m == 0:
                        pe.wait_ge(cq_spread[h8].sem, cq_spread[h8].at(b, 16))
                    for t in range(T):
                        ins = t_.matmul(bk[:, t * S:(t + 1) * S], cq_pad[:, m, h8, t * P:(t + 1) * P], ck_T[:, m, :], start=True, stop=True)
                    ins.then_inc(scores_ready.sem, 1)

            def probs_T(b, u):
                wait_evac(pe, b, u - 2)
                if u < H:
                    pe.wait_ge(norm_ready.sem, norm_ready.at(b, u + 1))
                else:
                    pe.wait_ge(exp_ready.sem, exp_ready.at(b, u + 1))
                for c in range(blocks(u)):
                    to = c if u < H else (c % 2) * 2 + c // 2
                    ins = t_.transpose(bank[4 + u % 2][:, to * P:(to + 1) * P], prob[:, u % H % P_RING, c * P:(c + 1) * P], ident[:])
                ins.then_inc(pt_ready.sem, 1)

            def times_v(b, u):
                wait_evac(pe, b, u - 1)
                wait_evac(pe, b, u)
                pT = [prob_T[:, h % H % T_RING] for h in (u - 1, u)]
                if u < H:
                    j = u // 2
                    pe.wait_ge(o_evac.sem, o_evac.at(b, j - 1))
                    o = [bank[6 + j % 2][64 * i:64 * i + 64] for i in range(2)]
                    for i, h in enumerate((u - 1, u)):
                        t_.matmul(o[i][:, 0:S], v_sb[:, 0, h * DH:(h + 1) * DH], pT[i][:, 0:S], start=True, stop=False)
                    for i, h in enumerate((u - 1, u)):
                        ins = t_.matmul(o[i][:, P:S], v_sb[:, 1, h * DH:(h + 1) * DH], pT[i][:, S:S + P], start=False, stop=True)
                else:
                    h = u - 1 - H
                    j, c = PAIRS + h // GROUP, h % GROUP
                    if c == 0:
                        pe.wait_ge(o_evac.sem, o_evac.at(b, j - 1))
                    o = [bank[6 + j % 2][32 * (c + i):32 * (c + i) + 32] for i in range(2)]
                    for k in range(T):
                        for i in range(2):
                            ins = t_.matmul(o[i][:, 0:S], cv_sb[:, k, h + i, :], pT[i][:, k * S:(k + 1) * S], start=k == 0, stop=k == T - 1)
                ins.then_inc(pv_done.sem, 2)

            def router_turn(b):
                pe.wait_ge(xn_ready[2].sem, xn_ready[2].at(b, 1))
                turn(b, 3, rows[:, :, 0:D], bank[3])

            def router_logits(b):
                pe.wait_ge(xnT_ready[2].sem, xnT_ready[2].at(b, 1))
                for t in range(T):
                    for k in range(KT):
                        ins = t_.matmul(bank[3][:, t * E:(t + 1) * E], xnT[:, k, t * P:(t + 1) * P], rw_sb[:, k, :],
                                        start=k == 0, stop=k == KT - 1)
                ins.then_inc(logits.sem, 1)

            def router_rank(b):
                pe.wait_ge(hot_ready.sem, hot_ready.at(b, 1))
                hot2 = hot[:].rearrange("p t e -> p (t e)")
                t_.matmul(bank[3][:, 2 * T * E:3 * T * E], before[:], hot2, start=True, stop=True)
                t_.matmul(bank[3][:, 3 * T * E:4 * T * E], ones[:], hot2, start=True, stop=True).then_inc(rank_ready.sem, 1)

            def heads(b, u0, router=False, last=False):
                for s in range(u0, u0 + H + LAG_V):
                    if s == H and u0 == H and not last:
                        pe.wait_ge(kv_evac.sem, kv_evac.at(b + 1, 2))
                    if s == H + 1 and u0 == H and not last:
                        pe.wait_ge(q_evac.sem, q_evac.at(b + 1, 6))
                    if s == H + 2 and u0 == H and not last:
                        pe.wait_ge(kv_evac.sem, kv_evac.at(b + 1, 3))
                    if s == LAG_V:
                        pe.wait_ge(x2_ready.sem, x2_ready.at(b, 0))
                    if s < u0 + H:
                        scores(b, s)
                    if s == 1:
                        fill(b, 11)
                    if u0 == H and s == H + 1 and not last:
                        fill(b + 1, 6)
                    if u0 == 0 and s == H:
                        cross_keys(b)
                    if s == 2 * H and not last:
                        pe.wait_ge(masked_ready.sem, masked_ready.at(b, 2 * H - 2))
                        fill(b + 1, 7)
                    if s == LAG_T:
                        pe.wait_ge(kv_evac.sem, kv_evac.at(b, 8))
                    if router and s == TURN_AT:
                        router_turn(b - 1)
                    if router and s == LOGITS_AT:
                        router_logits(b - 1)
                    if router and s == RANK_AT:
                        router_rank(b - 1)
                    if u0 <= s - LAG_T < u0 + H:
                        probs_T(b, s - LAG_T)
                    if u0 <= s - LAG_V < u0 + H and (s - LAG_V) % 2 == 1:
                        times_v(b, s - LAG_V)

            def cross_keys(b):
                pe.wait_ge(masked_ready.sem, masked_ready.at(b, H - 2))
                pe.wait_ge(ctx_loaded.sem, ctx_loaded.at(b, 16))
                for m in range(KT):
                    for k in range(KT):
                        ins = t_.matmul(bank[1][:, m * S:(m + 1) * S], cw[:, 1, k, m * P:(m + 1) * P], ctxT_in[:, k, :],
                                        start=k == 0, stop=k == KT - 1)
                ins.then_inc(ckv_done.sem, 1)

            def batch(b, first=False, last=False):
                pe.wait_ge(q_evac.sem, q_evac.at(b, 8))
                pe.wait_ge(kv_evac.sem, kv_evac.at(b, 6))
                heads(b, 0, router=not first)
                for t in range(T):
                    for m in range(PAIRS):
                        if t == 0 and m % (PAIRS - 1) == 0:
                            pe.wait_ge(o_evac.sem, o_evac.at(b, PAIRS - 1 if m == 0 else PAIRS))
                        ins = t_.matmul(bank[0][:, t * D:(t + 1) * D], z_T[:, m, t * P:(t + 1) * P], wo_sb[:, m, :],
                                        start=m == 0, stop=m == PAIRS - 1)
                ins.then_inc(attn_out.sem, 1)
                if not last:
                    pe.wait_ge(xn_ready[0].sem, xn_ready[0].at(b + 1, 1))
                    turn(b + 1, 1, x_norm, bank[6])
                for t in range(T):
                    for k in range(KT):
                        ins = t_.matmul(bank[2][:, t * D:(t + 1) * D], ctxT_in[:, k, t * P:(t + 1) * P], cw[:, 2, k, :],
                                        start=k == 0, stop=k == KT - 1)
                ins.then_inc(ckv_done.sem, 1)
                if not last:
                    pe.wait_ge(x_norm_low.sem, x_norm_low.at(b + 1, 1))
                    pe.wait_ge(rank_used.sem, rank_used.at(b, 0))
                    fill(b + 1, 0)
                pe.wait_ge(xn_ready[1].sem, xn_ready[1].at(b, 1))
                turn(b, 2, xn, bank[7])
                if not last:
                    fill(b + 1, 1)
                pe.wait_ge(xnT_ready[1].sem, xnT_ready[1].at(b, 1))
                for m in range(KT):
                    for k in range(KT):
                        ins = t_.matmul(bank[0][:, m * S:(m + 1) * S], cw[:, 0, k, m * P:(m + 1) * P], xnT[:, k, :],
                                        start=k == 0, stop=k == KT - 1)
                ins.then_inc(cq_done.sem, 1)
                if not last:
                    fill(b + 1, 2)
                pe.wait_ge(cq_evac.sem, cq_evac.at(b, 2))
                pe.wait_ge(ck_evac.sem, ck_evac.at(b, 2))
                pe.wait_ge(cv_evac.sem, cv_evac.at(b, 2))
                if not last:
                    for n in range(3, 6):
                        fill(b + 1, n)
                heads(b, H, last=last)
                if not last:
                    pe.wait_ge(masked_ready.sem, masked_ready.at(b, U))
                    fill(b + 1, 8)
                pe.wait_ge(o_evac.sem, o_evac.at(b, PAIRS + H // GROUP))
                for t in range(T):
                    for g in range(H // GROUP):
                        ins = t_.transpose(bank[4 + t][:, g * P:(g + 1) * P], o_T[:, g, t * P:(t + 1) * P], ident[:])
                    ins.then_inc(ctx_tr.sem, 1)
                if not last:
                    fill(b + 1, 9)
                pe.wait_ge(ctx_ready.sem, ctx_ready.at(b, 1))
                turn(b, 4, ctx_sb[:].rearrange("p t h c -> p t (h c)"), bank[7])
                if not last:
                    fill(b + 1, 10)
                pe.wait_ge(xnT_ready[3].sem, xnT_ready[3].at(b, 1))
                for t in range(T):
                    for k in range(KT):
                        ins = t_.matmul(bank[6][:, t * D:(t + 1) * D], xnT[:, k, t * P:(t + 1) * P], cw[:, 3, k, :],
                                        start=k == 0, stop=k == KT - 1)
                ins.then_inc(cx_out.sem, 1)

            pe.wait_ge(ident_ready.sem, 3)
            pe.wait_ge(xn_ready[0].sem, xn_ready[0].at(0, 1))
            turn(0, 1, x_norm, bank[7])
            pe.wait_ge(x_norm_low.sem, x_norm_low.at(0, 1))
            pe.wait_ge(w_low.sem, 2)
            for n in range(QK_FILLS):
                fill(0, n)
            pe.wait_ge(w_low.sem, 3)
            for n in range(QK_FILLS, FILLS - 1):
                fill(0, n)
            pe.wait_ge(w_in.sem, 16 * NW)
            pe.wait_ge(consts.sem, 17)
            batch(0, first=True)
            with pe.Fori(1, B - 1) as b:
                batch(b)
            batch(B - 1, last=True)
            router_turn(B - 1)
            router_logits(B - 1)
            router_rank(B - 1)

            pe.sem_inc(l1_ready.sem, 8)
            pe.sem_inc(ht_ready.sem, 4)
            pe.wait_ge(tables.sem, 2)

            def turn_x(i, c):
                j, p = i * 2 + c, c % 2
                pe.wait_ge(xe_loaded[p].sem, xe_loaded[p].at(i, 16 * (c // 2 + 1)))
                pe.wait_ge(xt_evac.sem, xt_evac.at(j, 0))
                for k in range(KT):
                    ins = t_.transpose(bank[6][:, k * P:(k + 1) * P], xe[p][:, k * P:(k + 1) * P], ident[:])
                ins.then_inc(xt_ready.sem, 1)

            def layer1(j, p, slot, n):
                c = L1_ORDER[n]
                pe.wait_ge(hb_ready.sem, hb_ready.at(j, -4 + n + 1))
                for k in range(KT):
                    ins = t_.matmul(bank[c][:], xe_T[p][:, k * P:(k + 1) * P],
                                    w1_ring[:, bass.ds(slot, 1), k * 2 * HID + c * 512:k * 2 * HID + (c + 1) * 512].rearrange("p o n -> p (o n)"),
                                    start=k == 0, stop=k == KT - 1)
                ins.then_inc(l1_ready.sem, 1)

            def turn_h(j, p):
                for c in range(2):
                    pe.wait_ge(hid_ready.sem, hid_ready.at(j, c + 1))
                    pe.wait_ge(ht_evac.sem, ht_evac.at(j, -2 + c + 1))
                    for q in range(4):
                        k = 4 * c + q
                        ins = t_.transpose(bank[4 + c][:, q * P:(q + 1) * P], hid[p][:, k * P:(k + 1) * P], ident[:])
                    ins.then_inc(ht_ready.sem, 1)

            def layer2(j):
                slot = pe.value_load(tile_slot[0:1, bass.ds(j, 1)], min_val=0, max_val=1)
                pe.wait_ge(y1_ready.sem, y1_ready.at(j, 0))
                for k in range(8):
                    if k % 4 == 0:
                        pe.wait_ge(ht_evac.sem, ht_evac.at(j, k // 4 + 1))
                    ins = t_.matmul(bank[7][:, 0:D], hid_T[:, k * P:(k + 1) * P],
                                    w2_ring[:, bass.ds(slot, 1), k * D:(k + 1) * D].rearrange("p o n -> p (o n)"),
                                    start=k == 0, stop=k == 7)
                ins.then_inc(tile_done.sem, 1)

            def step(i, c, prev=True, next_=True):
                j, p = i * 2 + c, c % 2
                e = pe.value_load(tile_e[0:1, bass.ds(j, 1)], min_val=0, max_val=E - 1)
                slot = pe.value_load(tile_slot[0:1, bass.ds(j, 1)], min_val=0, max_val=1)
                pe.wait_ge(w_loaded.sem, w_loaded.at(e, 48))
                pe.wait_ge(xt_evac.sem, xt_evac.at(j, 1))
                layer1(j, p, slot, 0)
                if prev:
                    turn_h(j - 1, 1 - p)
                layer1(j, p, slot, 1)
                if next_:
                    turn_x(i, c + 1)
                layer1(j, p, slot, 2)
                layer1(j, p, slot, 3)
                if prev:
                    layer2(j - 1)

            turn_x(0, 0)
            step(0, 0, prev=False)
            with pe.Fori(0, PAIRED) as i:
                step(i, 1)
                step(i, 2)
            step(PAIRED, 1)
            step(PAIRED, 2, next_=False)
            turn_h(NTILE - 1, 0)
            layer2(NTILE - 1)


def kernel(**inputs):
    import numpy as _np
    import concourse.bacc as _bacc
    from concourse import mybir as _mybir
    from concourse.bass_utils import run_bass_kernel_spmd as _run

    a = {k.replace("L0_", ""): _np.asarray(v) for k, v in inputs.items()}

    def by_rows(w, lead=()):
        *_, r, n = w.shape
        w = w.reshape(*w.shape[:-2], r // 128, 128, n)
        return _np.ascontiguousarray(_np.swapaxes(w, -3, -2))

    arrays = {
        "x": by_rows(a["x"]),
        "ctx_t": by_rows(_np.swapaxes(a["ctx_1024"], 1, 2)),
        "mask": by_rows(a["mask_BxSxS2_bk1"]),
        "wq": by_rows(a["attn_W_Q"].reshape(1024, 256).T),
        "wk": by_rows(a["attn_W_K"].reshape(1024, 256).T),
        "wv": by_rows(a["attn_W_V"].reshape(1024, 256).T),
        "wo": by_rows(a["attn_W_O"].T),
        "cwq": by_rows(a["xattn_wq"].T),
        "cwk": by_rows(a["xattn_wk"].T),
        "cwv": by_rows(a["xattn_wv"].T),
        "cwo": by_rows(a["xattn_wo"].T),
        "cbq": _np.ascontiguousarray(a["xattn_bq"].reshape(2, 128).T),
        "cbk": _np.ascontiguousarray(a["xattn_bk"].reshape(2, 128).T),
        "cbv": a["xattn_bv"].reshape(1, 256),
        "cbo": a["xattn_bo"].reshape(1, 256),
        "rw": by_rows(a["ffn_router_w"].T),
        "rb": a["ffn_router_b"].reshape(1, 8),
        "w1": by_rows(_np.swapaxes(a["ffn_w1"], 1, 2)).reshape(8, 128, -1),
        "b1": a["ffn_b1"],
        "w2": by_rows(_np.swapaxes(a["ffn_w2"], 1, 2)).reshape(8, 128, -1),
        "b2": a["ffn_b2"],
    }
    nc = _bacc.Bacc("TRN2", target_bir_lowering=False, num_devices=1)
    args = [nc.dram_tensor(f"in_{n}_dram", v.shape, _mybir.dt.from_np(v.dtype), kind="ExternalInput").ap()
            for n, v in arrays.items()]
    out = nc.dram_tensor("out_0_dram", (TOK + P, D), F32, kind="ExternalOutput").ap()
    build(nc, *args, out)
    r = _run(nc, [{f"in_{n}_dram": v for n, v in arrays.items()}], core_ids=[0])
    return r.results[0]["out_0_dram"][:TOK].reshape(B, S, D)
```
